# Optimizing a Trainium2 kernel written in Bass

```python
import numpy as np
import jax
import jax.numpy as jnp

def _softmax(x, axis=-1):
    return jax.nn.softmax(x, axis=axis)

def _gelu(x):
    return jax.nn.gelu(x, approximate=True)

def _silu(x):
    return jax.nn.silu(x)

def _sigmoid(x):
    return jax.nn.sigmoid(x)

def _layernorm(x, axis=-1, eps=1e-05):
    m = jnp.mean(x, axis=axis, keepdims=True)
    v = jnp.var(x, axis=axis, keepdims=True)
    return (x - m) / jnp.sqrt(v + eps)

def _scatter_add(tgt, idx, src, axis=0):
    return tgt.at[idx].add(src)

def _segment_sum(src, seg, n):
    return jax.ops.segment_sum(src, seg, n)
kernel_name = 'mk_decoder_postln_d4_seqx_r8_91cd27'

def setup_inputs(seed: int=0):
    np.random.seed(seed)
    _w = jnp.asarray

    def _rec_inputs():
        import jax
        import jax.numpy as jnp
        _rk = jax.random.key(seed)
        x = -0.0002928 + 1 * jax.random.normal(jax.random.fold_in(_rk, 1), (8, 128, 128), jnp.float32)
        _lenS = 128 - jax.random.randint(jax.random.fold_in(_rk, 7), (8,), 0, max(1, 128 // 4) + 1, jnp.int32)
        _lenS2 = 128 - jax.random.randint(jax.random.fold_in(_rk, 8), (8,), 0, max(1, 128 // 4) + 1, jnp.int32)
        _ctx_1024P = jax.random.normal(jax.random.fold_in(_rk, 11), (8, 16, 128), jnp.float32)
        _ctx_1024c = jax.random.dirichlet(jax.random.fold_in(_rk, 511), 0.3 * jnp.ones((16,), jnp.float32), (8, 128))
        _ctx_1024t = jnp.einsum('bsk,bkd->bsd', _ctx_1024c, _ctx_1024P)
        _ctx_1024t = _ctx_1024t * jax.lax.rsqrt(jnp.mean(jnp.square(_ctx_1024t)) + 1e-12) * 0.953939
        ctx_1024 = 0.000227908 + 0.99994 * (_ctx_1024t + 0.3 * jax.random.normal(jax.random.fold_in(_rk, 611), (8, 128, 128), jnp.float32))
        return (x, ctx_1024)
    x, ctx_1024 = _rec_inputs()

    def _L0_attn_setup():
        import jax, jax.numpy as jnp
        import numpy as np
        D_MODEL = 128
        N_HEADS = 16
        HEAD_DIM = D_MODEL // N_HEADS
        BUCKET = 64
        key = jax.random.key(seed)
        k1, k2, k3 = jax.random.split(key, 3)
        B, T = (4, 512)
        x = jax.random.normal(k1, (B, T, D_MODEL), dtype=jnp.float32)
        W_qkv = jax.random.normal(k2, (3 * D_MODEL, D_MODEL), dtype=jnp.float32) * D_MODEL ** (-0.5)
        W_out = jax.random.normal(k3, (D_MODEL, D_MODEL), dtype=jnp.float32) * D_MODEL ** (-0.5)
        return {'x': x, 'W_qkv': W_qkv, 'W_out': W_out}
    _L0_attn_all = _L0_attn_setup()
    _L0_attn_in = {k: v for k, v in _L0_attn_all.items() if k in ('W_qkv', 'W_out')}
    del _L0_attn_all

    def _L0_xattn_setup():
        import jax, jax.numpy as jnp
        import numpy as np
        HEADS = 16
        key = jax.random.key(seed)
        ks = jax.random.split(key, 6)
        b, n, m, dim = (2, 256, 64, 128)
        s = dim ** (-0.5)
        return {'x': jax.random.normal(ks[0], (b, n, dim), jnp.float32), 'mem': jax.random.normal(ks[1], (b, m, dim), jnp.float32), 'Wq': jax.random.normal(ks[2], (dim, dim), jnp.float32) * s, 'Wkv': jax.random.normal(ks[3], (dim, 2 * dim), jnp.float32) * s, 'Wout': jax.random.normal(ks[4], (dim, dim), jnp.float32) * s, 'bout': jnp.zeros((dim,), jnp.float32)}
    _L0_xattn_all = _L0_xattn_setup()
    _L0_xattn_in = {k: v for k, v in _L0_xattn_all.items() if k in ('Wq', 'Wkv', 'Wout', 'bout')}
    del _L0_xattn_all

    def _L0_ffn_setup():
        import jax, jax.numpy as jnp
        import numpy as np
        DIM = 128
        INTER = 256
        E = 8
        TOPK = 2
        ROUTE_SCALE = 1.0

        def _mlp(x, w1, w2, w3):
            h = jax.nn.silu(x @ w1.T) * (x @ w3.T)
            return h @ w2.T
        key = jax.random.key(seed)
        ks = jax.random.split(key, 10)
        s_in = 0.02
        return {'x': jax.random.normal(ks[0], (4, 256, DIM), dtype=jnp.float32), 'gate_w': jax.random.normal(ks[1], (E, DIM), dtype=jnp.float32) * s_in, 'gate_bias': jax.random.normal(ks[2], (E,), dtype=jnp.float32) * 0.01, 'w1': jax.random.normal(ks[3], (E, INTER, DIM), dtype=jnp.float32) * s_in, 'w2': jax.random.normal(ks[4], (E, DIM, INTER), dtype=jnp.float32) * s_in, 'w3': jax.random.normal(ks[5], (E, INTER, DIM), dtype=jnp.float32) * s_in, 'sw1': jax.random.normal(ks[6], (INTER, DIM), dtype=jnp.float32) * s_in, 'sw2': jax.random.normal(ks[7], (DIM, INTER), dtype=jnp.float32) * s_in, 'sw3': jax.random.normal(ks[8], (INTER, DIM), dtype=jnp.float32) * s_in}
    _L0_ffn_all = _L0_ffn_setup()
    _L0_ffn_in = {k: v for k, v in _L0_ffn_all.items() if k in ('gate_w', 'gate_bias', 'w1', 'w2', 'w3', 'sw1', 'sw2', 'sw3')}
    del _L0_ffn_all

    def _L1_attn_setup():
        import jax, jax.numpy as jnp
        import numpy as np
        HID, H, B, T = (128, 16, 4, 256)
        D = HID // H
        BETA_MIN, BETA_MAX, EPS = (0.8, 0.999, 1e-06)

        def _rope_cache(T, D):
            inv_freq = 1.0 / 10000.0 ** (jnp.arange(0, D, 2, dtype=jnp.float32) / D)
            t = jnp.arange(T, dtype=jnp.float32)
            freqs = t[:, None] * inv_freq[None, :]
            emb = jnp.concatenate([freqs, freqs], axis=-1)
            return (jnp.cos(emb)[None, :, None, :], jnp.sin(emb)[None, :, None, :])

        def _apply_rope(u, cos, sin):
            u1, u2 = jnp.split(u, 2, axis=-1)
            rot = jnp.concatenate([-u2, u1], axis=-1)
            return u * cos + rot * sin

        def _phi(u):
            return jax.nn.elu(u) + 1.0
        key = jax.random.key(seed)
        ks = jax.random.split(key, 8)
        s = 1.0 / np.sqrt(HID)
        x = jax.random.normal(ks[0], (B, T, HID), dtype=jnp.float32)
        Wq = jax.random.normal(ks[1], (HID, HID), dtype=jnp.float32) * s
        Wk = jax.random.normal(ks[2], (HID, HID), dtype=jnp.float32) * s
        Wv = jax.random.normal(ks[3], (HID, HID), dtype=jnp.float32) * s
        Wb = jax.random.normal(ks[4], (H, HID), dtype=jnp.float32) * s
        bb = jnp.full((H,), float(np.log(0.95 / 0.05)), dtype=jnp.float32)
        Wo = jax.random.normal(ks[5], (HID, HID), dtype=jnp.float32) * s
        bo = jnp.zeros((HID,), dtype=jnp.float32)
        scale = jnp.ones((HID,), dtype=jnp.float32)
        return {'x': x, 'Wq': Wq, 'Wk': Wk, 'Wv': Wv, 'Wb': Wb, 'bb': bb, 'Wo': Wo, 'bo': bo, 'scale': scale}
    _L1_attn_all = _L1_attn_setup()
    _L1_attn_in = {k: v for k, v in _L1_attn_all.items() if k in ('Wq', 'Wk', 'Wv', 'Wb', 'bb', 'Wo', 'bo', 'scale')}
    del _L1_attn_all

    def _L1_xattn_setup():
        import jax, jax.numpy as jnp
        import numpy as np
        HEADS = 16
        DIM_HEAD = 64
        DIM = 128
        CTX_DIM = 128
        INNER = HEADS * DIM_HEAD
        key = jax.random.key(seed)
        ks = jax.random.split(key, 6)
        b, n, m = (4, 256, 256)
        x = jax.random.normal(ks[0], (b, n, DIM), dtype=jnp.float32)
        context = jax.random.normal(ks[1], (b, m, CTX_DIM), dtype=jnp.float32)
        s = 0.02
        w_q = jax.random.normal(ks[2], (DIM, INNER), dtype=jnp.float32) * s
        w_kv = jax.random.normal(ks[3], (CTX_DIM, 2 * INNER), dtype=jnp.float32) * s
        w_out = jax.random.normal(ks[4], (INNER, DIM), dtype=jnp.float32) * s
        b_out = jnp.zeros((DIM,), dtype=jnp.float32)
        return {'x': x, 'context': context, 'w_q': w_q, 'w_kv': w_kv, 'w_out': w_out, 'b_out': b_out}
    _L1_xattn_all = _L1_xattn_setup()
    _L1_xattn_in = {k: v for k, v in _L1_xattn_all.items() if k in ('w_q', 'w_kv', 'w_out', 'b_out')}
    del _L1_xattn_all

    def _L1_ffn_setup():
        import jax, jax.numpy as jnp
        import numpy as np
        TOP_K = 2
        key = jax.random.key(seed)
        k1, k2, k3, k4 = jax.random.split(key, 4)
        B, N, D, E, F = (4, 256, 128, 8, 512)
        x = jax.random.normal(k1, (B, N, D), dtype=jnp.float32)
        gate_w = jax.random.normal(k2, (D, E), dtype=jnp.float32) * D ** (-0.5)
        w1 = jax.random.normal(k3, (E, D, F), dtype=jnp.float32) * D ** (-0.5)
        w2 = jax.random.normal(k4, (E, F, D), dtype=jnp.float32) * F ** (-0.5)
        return {'x': x, 'gate_w': gate_w, 'w1': w1, 'w2': w2}
    _L1_ffn_all = _L1_ffn_setup()
    _L1_ffn_in = {k: v for k, v in _L1_ffn_all.items() if k in ('gate_w', 'w1', 'w2')}
    del _L1_ffn_all

    def _L2_attn_setup():
        import jax, jax.numpy as jnp
        import numpy as np
        B, N, D = (4, 512, 128)
        H, F = (16, 32)
        HD = D // H
        EPS_ATTN = 1e-08
        EPS_LN = 1e-05

        def _layernorm(x, gamma, beta):
            mu = jnp.mean(x, axis=-1, keepdims=True)
            var = jnp.var(x, axis=-1, keepdims=True)
            return (x - mu) * jax.lax.rsqrt(var + EPS_LN) * gamma + beta
        key = jax.random.key(seed)
        ks = jax.random.split(key, 10)

        def kaiming(k, shape):
            fan_in = shape[1]
            return jax.random.normal(k, shape, jnp.float32) * jnp.sqrt(2.0 / fan_in)
        pm = jax.random.normal(ks[0], (H, HD, F), jnp.float32)
        return {'x': jax.random.normal(ks[1], (B, N, D), jnp.float32), 'proj': pm, 'w_qkv': kaiming(ks[2], (3 * D, D)), 'w_out': kaiming(ks[3], (D, D)), 'b_out': jnp.zeros((D,), jnp.float32), 'gamma': jnp.ones((D,), jnp.float32), 'beta': jnp.zeros((D,), jnp.float32), 'w1': kaiming(ks[4], (4 * D, D)), 'b1': jnp.zeros((4 * D,), jnp.float32), 'w2': kaiming(ks[5], (D, 4 * D)), 'b2': jnp.zeros((D,), jnp.float32)}
    _L2_attn_all = _L2_attn_setup()
    _L2_attn_in = {k: v for k, v in _L2_attn_all.items() if k in ('proj', 'w_qkv', 'w_out', 'b_out', 'gamma', 'beta', 'w1', 'b1', 'w2', 'b2')}
    del _L2_attn_all

    def _L2_xattn_setup():
        import jax, jax.numpy as jnp
        import numpy as np
        N_HEADS = 16
        HIDDEN = 128
        HEAD = HIDDEN // N_HEADS
        key = jax.random.key(seed)
        ks = jax.random.split(key, 11)
        B, S, H = (2, 256, HIDDEN)
        s = 1.0 / np.sqrt(H)
        return {'query': jax.random.normal(ks[0], (B, S, H), jnp.float32), 'key': jax.random.normal(ks[1], (B, S, H), jnp.float32), 'value': jax.random.normal(ks[2], (B, S, H), jnp.float32), 'Wq': jax.random.normal(ks[3], (H, H), jnp.float32) * s, 'bq': jnp.zeros((H,), jnp.float32), 'Wk': jax.random.normal(ks[4], (H, H), jnp.float32) * s, 'bk': jnp.zeros((H,), jnp.float32), 'Wv': jax.random.normal(ks[5], (H, H), jnp.float32) * s, 'bv': jnp.zeros((H,), jnp.float32), 'Wo': jax.random.normal(ks[6], (H, H), jnp.float32) * s, 'bo': jnp.zeros((H,), jnp.float32)}
    _L2_xattn_all = _L2_xattn_setup()
    _L2_xattn_in = {k: v for k, v in _L2_xattn_all.items() if k in ('Wq', 'bq', 'Wk', 'bk', 'Wv', 'bv', 'Wo', 'bo')}
    del _L2_xattn_all

    def _L2_ffn_setup():
        import jax, jax.numpy as jnp
        import numpy as np
        E = 8
        H = 128
        M = 256
        K = 2
        SE = 1
        BSZ, SEQ = (2, 128)
        W_SCALE = 0.02
        key = jax.random.key(seed)
        ks = jax.random.split(key, 9)
        return {'x': jax.random.normal(ks[0], (BSZ, SEQ, H), jnp.float32), 'gate_w': jax.random.normal(ks[1], (E, H), jnp.float32) * W_SCALE, 'beta': jnp.zeros((E,), jnp.float32), 'gate_proj_w': jax.random.normal(ks[2], (E, H, M), jnp.float32) * W_SCALE, 'up_proj_w': jax.random.normal(ks[3], (E, H, M), jnp.float32) * W_SCALE, 'down_proj_w': jax.random.normal(ks[4], (E, M, H), jnp.float32) * W_SCALE, 'shared_gate_w': jax.random.normal(ks[5], (SE, H, M), jnp.float32) * W_SCALE, 'shared_up_w': jax.random.normal(ks[6], (SE, H, M), jnp.float32) * W_SCALE, 'shared_down_w': jax.random.normal(ks[7], (SE, M, H), jnp.float32) * W_SCALE}
    _L2_ffn_all = _L2_ffn_setup()
    _L2_ffn_in = {k: v for k, v in _L2_ffn_all.items() if k in ('gate_w', 'beta', 'gate_proj_w', 'up_proj_w', 'down_proj_w', 'shared_gate_w', 'shared_up_w', 'shared_down_w')}
    del _L2_ffn_all

    def _L3_attn_setup():
        import jax, jax.numpy as jnp
        import numpy as np
        import math
        N_HEAD = 16
        LATENT_RANK = 64
        key = jax.random.key(seed)
        ks = jax.random.split(key, 8)
        B, T, C, H, R = (4, 256, 128, N_HEAD, LATENT_RANK)
        std = 0.02
        return {'hidden_states': jax.random.normal(ks[0], (B, T, C), jnp.float32), 'basis_w': jax.random.normal(ks[1], (R, C), jnp.float32) * std, 'core': jax.random.normal(ks[2], (R, R), jnp.float32) * std, 'head_residual': jax.random.normal(ks[3], (H, R, R), jnp.float32) * (std / 10.0), 'v_w': jax.random.normal(ks[4], (C, C), jnp.float32) * std, 'v_b': jnp.zeros((C,), jnp.float32), 'o_w': jax.random.normal(ks[5], (C, C), jnp.float32) * std, 'o_b': jnp.zeros((C,), jnp.float32)}
    _L3_attn_all = _L3_attn_setup()
    _L3_attn_in = {k: v for k, v in _L3_attn_all.items() if k in ('basis_w', 'core', 'head_residual', 'v_w', 'v_b', 'o_w', 'o_b')}
    del _L3_attn_all

    def _L3_xattn_setup():
        import jax, jax.numpy as jnp
        import numpy as np
        EPS = 1e-06
        LN_EPS = 1e-06

        def _mlstm_parallel_stabilized(q, k, v, igate_preact, fgate_preact):
            B, NH, S, DH = q.shape
            log_fg = jax.nn.log_sigmoid(fgate_preact[..., 0])
            cs = jnp.cumsum(log_fg, axis=-1)
            fg_mat = cs[..., :, None] - cs[..., None, :]
            mask = jnp.tril(jnp.ones((S, S), dtype=bool))
            log_D = jnp.where(mask, fg_mat + igate_preact[..., 0][..., None, :], -jnp.inf)
            max_log_D = jnp.max(log_D, axis=-1, keepdims=True)
            D = jnp.exp(log_D - max_log_D)
            k_scaled = k / jnp.sqrt(jnp.float32(DH)).astype(k.dtype)
            qk = jnp.einsum('bhsd,bhtd->bhst', q, k_scaled)
            C = qk * D
            normalizer = jnp.maximum(jnp.abs(jnp.sum(C, axis=-1, keepdims=True)), jnp.exp(-max_log_D))
            C_norm = C / (normalizer + EPS)
            return jnp.einsum('bhst,bhtd->bhsd', C_norm, v)

        def _multihead_layernorm(x, weight):
            mu = jnp.mean(x, axis=-1, keepdims=True)
            var = jnp.mean(jnp.square(x - mu), axis=-1, keepdims=True)
            xn = (x - mu) * jax.lax.rsqrt(var + LN_EPS)
            return xn * weight[None, :, None, :]
        key = jax.random.key(seed)
        ks = jax.random.split(key, 6)
        B, S, E, NH = (2, 256, 128, 8)
        q = jax.random.normal(ks[0], (B, S, E), dtype=jnp.float32)
        k = jax.random.normal(ks[1], (B, S, E), dtype=jnp.float32)
        v = jax.random.normal(ks[2], (B, S, E), dtype=jnp.float32)
        igate_kernel = jnp.zeros((3 * E, NH), dtype=jnp.float32)
        igate_bias = 0.1 * jax.random.normal(ks[3], (NH,), dtype=jnp.float32)
        fgate_kernel = jnp.zeros((3 * E, NH), dtype=jnp.float32)
        fgate_bias = jnp.linspace(3.0, 6.0, NH, dtype=jnp.float32)
        outnorm_weight = jnp.ones((NH, E // NH), dtype=jnp.float32)
        return {'q': q, 'k': k, 'v': v, 'igate_kernel': igate_kernel, 'igate_bias': igate_bias, 'fgate_kernel': fgate_kernel, 'fgate_bias': fgate_bias, 'outnorm_weight': outnorm_weight}
    _L3_xattn_all = _L3_xattn_setup()
    _L3_xattn_in = {k: v for k, v in _L3_xattn_all.items() if k in ('igate_kernel', 'igate_bias', 'fgate_kernel', 'fgate_bias', 'outnorm_weight')}
    del _L3_xattn_all

    def _L3_ffn_setup():
        import jax, jax.numpy as jnp
        import numpy as np
        IN_FEATURES = 128
        OUT_FEATURES = 128
        B, S = (8, 512)
        key = jax.random.key(seed)
        kx, kw = jax.random.split(key)
        x = jax.random.normal(kx, (B, S, IN_FEATURES), dtype=jnp.float32)
        weight = jax.random.normal(kw, (OUT_FEATURES, IN_FEATURES), dtype=jnp.float32) * 0.1
        bias = jnp.zeros((OUT_FEATURES,), dtype=jnp.float32)
        return {'x': x, 'weight': weight, 'bias': bias}
    _L3_ffn_all = _L3_ffn_setup()
    _L3_ffn_in = {k: v for k, v in _L3_ffn_all.items() if k in ('weight', 'bias')}
    del _L3_ffn_all
    return {'x': x, 'ctx_1024': ctx_1024, 'L0_attn_W_qkv': _L0_attn_in['W_qkv'], 'L0_attn_W_out': _L0_attn_in['W_out'], 'L0_xattn_Wq': _L0_xattn_in['Wq'], 'L0_xattn_Wkv': _L0_xattn_in['Wkv'], 'L0_xattn_Wout': _L0_xattn_in['Wout'], 'L0_xattn_bout': _L0_xattn_in['bout'], 'L0_ffn_gate_w': _L0_ffn_in['gate_w'], 'L0_ffn_gate_bias': _L0_ffn_in['gate_bias'], 'L0_ffn_w1': _L0_ffn_in['w1'], 'L0_ffn_w2': _L0_ffn_in['w2'], 'L0_ffn_w3': _L0_ffn_in['w3'], 'L0_ffn_sw1': _L0_ffn_in['sw1'], 'L0_ffn_sw2': _L0_ffn_in['sw2'], 'L0_ffn_sw3': _L0_ffn_in['sw3'], 'L1_attn_Wq': _L1_attn_in['Wq'], 'L1_attn_Wk': _L1_attn_in['Wk'], 'L1_attn_Wv': _L1_attn_in['Wv'], 'L1_attn_Wb': _L1_attn_in['Wb'], 'L1_attn_bb': _L1_attn_in['bb'], 'L1_attn_Wo': _L1_attn_in['Wo'], 'L1_attn_bo': _L1_attn_in['bo'], 'L1_attn_scale': _L1_attn_in['scale'], 'L1_xattn_w_q': _L1_xattn_in['w_q'], 'L1_xattn_w_kv': _L1_xattn_in['w_kv'], 'L1_xattn_w_out': _L1_xattn_in['w_out'], 'L1_xattn_b_out': _L1_xattn_in['b_out'], 'L1_ffn_gate_w': _L1_ffn_in['gate_w'], 'L1_ffn_w1': _L1_ffn_in['w1'], 'L1_ffn_w2': _L1_ffn_in['w2'], 'L2_attn_proj': _L2_attn_in['proj'], 'L2_attn_w_qkv': _L2_attn_in['w_qkv'], 'L2_attn_w_out': _L2_attn_in['w_out'], 'L2_attn_b_out': _L2_attn_in['b_out'], 'L2_attn_gamma': _L2_attn_in['gamma'], 'L2_attn_beta': _L2_attn_in['beta'], 'L2_attn_w1': _L2_attn_in['w1'], 'L2_attn_b1': _L2_attn_in['b1'], 'L2_attn_w2': _L2_attn_in['w2'], 'L2_attn_b2': _L2_attn_in['b2'], 'L2_xattn_Wq': _L2_xattn_in['Wq'], 'L2_xattn_bq': _L2_xattn_in['bq'], 'L2_xattn_Wk': _L2_xattn_in['Wk'], 'L2_xattn_bk': _L2_xattn_in['bk'], 'L2_xattn_Wv': _L2_xattn_in['Wv'], 'L2_xattn_bv': _L2_xattn_in['bv'], 'L2_xattn_Wo': _L2_xattn_in['Wo'], 'L2_xattn_bo': _L2_xattn_in['bo'], 'L2_ffn_gate_w': _L2_ffn_in['gate_w'], 'L2_ffn_beta': _L2_ffn_in['beta'], 'L2_ffn_gate_proj_w': _L2_ffn_in['gate_proj_w'], 'L2_ffn_up_proj_w': _L2_ffn_in['up_proj_w'], 'L2_ffn_down_proj_w': _L2_ffn_in['down_proj_w'], 'L2_ffn_shared_gate_w': _L2_ffn_in['shared_gate_w'], 'L2_ffn_shared_up_w': _L2_ffn_in['shared_up_w'], 'L2_ffn_shared_down_w': _L2_ffn_in['shared_down_w'], 'L3_attn_basis_w': _L3_attn_in['basis_w'], 'L3_attn_core': _L3_attn_in['core'], 'L3_attn_head_residual': _L3_attn_in['head_residual'], 'L3_attn_v_w': _L3_attn_in['v_w'], 'L3_attn_v_b': _L3_attn_in['v_b'], 'L3_attn_o_w': _L3_attn_in['o_w'], 'L3_attn_o_b': _L3_attn_in['o_b'], 'L3_xattn_igate_kernel': _L3_xattn_in['igate_kernel'], 'L3_xattn_igate_bias': _L3_xattn_in['igate_bias'], 'L3_xattn_fgate_kernel': _L3_xattn_in['fgate_kernel'], 'L3_xattn_fgate_bias': _L3_xattn_in['fgate_bias'], 'L3_xattn_outnorm_weight': _L3_xattn_in['outnorm_weight'], 'L3_ffn_weight': _L3_ffn_in['weight'], 'L3_ffn_bias': _L3_ffn_in['bias']}

def reference(x, ctx_1024, L0_attn_W_qkv, L0_attn_W_out, L0_xattn_Wq, L0_xattn_Wkv, L0_xattn_Wout, L0_xattn_bout, L0_ffn_gate_w, L0_ffn_gate_bias, L0_ffn_w1, L0_ffn_w2, L0_ffn_w3, L0_ffn_sw1, L0_ffn_sw2, L0_ffn_sw3, L1_attn_Wq, L1_attn_Wk, L1_attn_Wv, L1_attn_Wb, L1_attn_bb, L1_attn_Wo, L1_attn_bo, L1_attn_scale, L1_xattn_w_q, L1_xattn_w_kv, L1_xattn_w_out, L1_xattn_b_out, L1_ffn_gate_w, L1_ffn_w1, L1_ffn_w2, L2_attn_proj, L2_attn_w_qkv, L2_attn_w_out, L2_attn_b_out, L2_attn_gamma, L2_attn_beta, L2_attn_w1, L2_attn_b1, L2_attn_w2, L2_attn_b2, L2_xattn_Wq, L2_xattn_bq, L2_xattn_Wk, L2_xattn_bk, L2_xattn_Wv, L2_xattn_bv, L2_xattn_Wo, L2_xattn_bo, L2_ffn_gate_w, L2_ffn_beta, L2_ffn_gate_proj_w, L2_ffn_up_proj_w, L2_ffn_down_proj_w, L2_ffn_shared_gate_w, L2_ffn_shared_up_w, L2_ffn_shared_down_w, L3_attn_basis_w, L3_attn_core, L3_attn_head_residual, L3_attn_v_w, L3_attn_v_b, L3_attn_o_w, L3_attn_o_b, L3_xattn_igate_kernel, L3_xattn_igate_bias, L3_xattn_fgate_kernel, L3_xattn_fgate_bias, L3_xattn_outnorm_weight, L3_ffn_weight, L3_ffn_bias):
    import jax
    import jax.numpy as jnp

    def _L0_attn_ref(x, W_qkv, W_out):
        import jax, jax.numpy as jnp
        import numpy as np
        D_MODEL = 128
        N_HEADS = 16
        HEAD_DIM = D_MODEL // N_HEADS
        BUCKET = 64
        B, T, _ = x.shape
        qkv = x @ W_qkv.T
        qkv = qkv.reshape(B, T, 3 * N_HEADS, HEAD_DIM).transpose(0, 2, 1, 3)
        q, k, v = jnp.split(qkv, 3, axis=1)
        q = jax.nn.softmax(q, axis=-1) * HEAD_DIM ** (-0.5)
        k = jnp.exp(k)
        n = T // BUCKET
        bucket = lambda t: t.reshape(B, N_HEADS, n, BUCKET, HEAD_DIM)
        b_q, b_k, b_v = (bucket(q), bucket(k), bucket(v))
        b_k_sum = jnp.sum(b_k, axis=-2)
        b_k_cumsum = jnp.cumsum(b_k_sum, axis=-2)
        b_k_cumsum = jnp.pad(b_k_cumsum, ((0, 0), (0, 0), (1, 0), (0, 0)))[:, :, :-1]
        context = jnp.einsum('bhnsd,bhnse->bhnde', b_k, b_v)
        context = jnp.cumsum(context, axis=-3)
        context = jnp.pad(context, ((0, 0), (0, 0), (1, 0), (0, 0), (0, 0)))[:, :, :-1]
        den = jnp.einsum('bhnsd,bhnd->bhns', b_q, b_k_cumsum)
        D_inv = 1.0 / jnp.maximum(den, 1e-06)
        attn = jnp.einsum('bhnsd,bhnde,bhns->bhnse', b_q, context, D_inv)
        xo = attn.reshape(B, N_HEADS, T, HEAD_DIM)
        xo = xo.transpose(0, 2, 1, 3).reshape(B, T, D_MODEL)
        return xo @ W_out.T

    def _L0_xattn_ref(x, mem, Wq, Wkv, Wout, bout):
        import jax, jax.numpy as jnp
        import numpy as np
        HEADS = 16
        b, n, dim = x.shape
        h = HEADS
        d = dim // h
        scale = d ** (-0.5)
        mem_len = mem.shape[1]
        q = x @ Wq
        xc = jnp.concatenate((mem, x), axis=1)
        kv = xc @ Wkv
        k, v = jnp.split(kv, 2, axis=-1)

        def to_heads(t):
            bb, nn, _ = t.shape
            return t.reshape(bb, nn, h, d).transpose(0, 2, 1, 3)
        q, k, v = (to_heads(q), to_heads(k), to_heads(v))
        dots = jnp.einsum('bhid,bhjd->bhij', q, k) * scale
        j = dots.shape[-1]
        i_idx = jnp.arange(n)[:, None]
        j_idx = jnp.arange(j)[None, :]
        mask = j_idx > i_idx + mem_len
        dots = jnp.where(mask[None, None], -jnp.inf, dots)
        attn = jax.nn.softmax(dots, axis=-1)
        out = jnp.einsum('bhij,bhjd->bhid', attn, v)
        out = out.transpose(0, 2, 1, 3).reshape(b, n, dim)
        return out @ Wout + bout

    def _L0_ffn_ref(x, gate_w, gate_bias, w1, w2, w3, sw1, sw2, sw3):
        import jax, jax.numpy as jnp
        import numpy as np
        DIM = 128
        INTER = 256
        E = 8
        TOPK = 2
        ROUTE_SCALE = 1.0

        def _mlp(x, w1, w2, w3):
            h = jax.nn.silu(x @ w1.T) * (x @ w3.T)
            return h @ w2.T
        shape = x.shape
        xt = x.reshape(-1, DIM)
        T = xt.shape[0]
        logits = xt @ gate_w.T
        scores = jax.nn.softmax(logits.astype(jnp.float32), axis=-1)
        original_scores = scores
        biased = scores + gate_bias
        _, indices = jax.lax.top_k(biased, TOPK)
        weights = jnp.take_along_axis(original_scores, indices, axis=1)
        weights = (weights * ROUTE_SCALE).astype(x.dtype)
        combine = (jax.nn.one_hot(indices, E, dtype=weights.dtype) * weights[..., None]).sum(axis=1)
        y = jnp.zeros_like(xt)
        for e in range(E):
            y = y + _mlp(xt, w1[e], w2[e], w3[e]) * combine[:, e:e + 1]
        z = _mlp(xt, sw1, sw2, sw3)
        return (y + z).reshape(shape)

    def _L1_attn_ref(x, Wq, Wk, Wv, Wb, bb, Wo, bo, scale):
        import jax, jax.numpy as jnp
        import numpy as np
        HID, H, B, T = (128, 16, 4, 256)
        D = HID // H
        BETA_MIN, BETA_MAX, EPS = (0.8, 0.999, 1e-06)

        def _rope_cache(T, D):
            inv_freq = 1.0 / 10000.0 ** (jnp.arange(0, D, 2, dtype=jnp.float32) / D)
            t = jnp.arange(T, dtype=jnp.float32)
            freqs = t[:, None] * inv_freq[None, :]
            emb = jnp.concatenate([freqs, freqs], axis=-1)
            return (jnp.cos(emb)[None, :, None, :], jnp.sin(emb)[None, :, None, :])

        def _apply_rope(u, cos, sin):
            u1, u2 = jnp.split(u, 2, axis=-1)
            rot = jnp.concatenate([-u2, u1], axis=-1)
            return u * cos + rot * sin

        def _phi(u):
            return jax.nn.elu(u) + 1.0
        Bx, Tx, hid = x.shape
        q = (x @ Wq.T).reshape(Bx, Tx, H, D)
        k = (x @ Wk.T).reshape(Bx, Tx, H, D)
        v = (x @ Wv.T).reshape(Bx, Tx, H, D)
        beta = jax.nn.sigmoid(x @ Wb.T + bb)
        beta = jnp.clip(beta, BETA_MIN, BETA_MAX).astype(jnp.float32)
        cos, sin = _rope_cache(Tx, D)
        phi_q = _phi(_apply_rope(q, cos, sin)).astype(jnp.float32)
        phi_k = _phi(_apply_rope(k, cos, sin)).astype(jnp.float32)
        v32 = v.astype(jnp.float32)
        pq = jnp.swapaxes(phi_q, 0, 1)
        pk = jnp.swapaxes(phi_k, 0, 1)
        vv = jnp.swapaxes(v32, 0, 1)
        bt = jnp.swapaxes(beta, 0, 1)

        def step(carry, inp):
            S, z = carry
            pqt, pkt, vt, b = inp
            S = b[..., None, None] * S + pkt[..., :, None] * vt[..., None, :]
            z = b[..., None] * z + pkt
            num = jnp.einsum('bhd,bhde->bhe', pqt, S)
            den = jnp.einsum('bhd,bhd->bh', pqt, z) + EPS
            return ((S, z), num / den[..., None])
        S0 = jnp.zeros((Bx, H, D, D), jnp.float32)
        z0 = jnp.zeros((Bx, H, D), jnp.float32)
        _, outs = jax.lax.scan(step, (S0, z0), (pq, pk, vv, bt))
        attn = jnp.swapaxes(outs, 0, 1).reshape(Bx, Tx, hid).astype(x.dtype)
        y = attn @ Wo.T + bo
        h = x + y
        rms = jnp.sqrt(jnp.mean(h * h, axis=-1, keepdims=True) + EPS)
        return h / rms * scale

    def _L1_xattn_ref(x, context, w_q, w_kv, w_out, b_out):
        import jax, jax.numpy as jnp
        import numpy as np
        HEADS = 16
        DIM_HEAD = 64
        DIM = 128
        CTX_DIM = 128
        INNER = HEADS * DIM_HEAD
        b, n, _ = x.shape
        m = context.shape[1]
        scale = DIM_HEAD ** (-0.5)
        q = (x @ w_q).reshape(b, n, HEADS, DIM_HEAD)
        kv = (context @ w_kv).reshape(b, m, 2, HEADS, DIM_HEAD)
        k, v = (kv[:, :, 0], kv[:, :, 1])
        attn = jnp.einsum('bnhd,bmhd->bhnm', q, k) * scale
        attn = jax.nn.softmax(attn, axis=-1)
        out = jnp.einsum('bhnm,bmhd->bnhd', attn, v).reshape(b, n, INNER)
        return out @ w_out + b_out

    def _L1_ffn_ref(x, gate_w, w1, w2):
        import jax, jax.numpy as jnp
        import numpy as np
        TOP_K = 2
        E = gate_w.shape[-1]
        gate_logits = jnp.einsum('bnd,de->bne', x, gate_w)
        gate_probs = jax.nn.softmax(gate_logits, axis=-1)
        top_k_probs, top_k_idx = jax.lax.top_k(gate_probs, TOP_K)
        top_k_weights = top_k_probs / jnp.sum(top_k_probs, axis=-1, keepdims=True)
        comb = jnp.sum(jax.nn.one_hot(top_k_idx, E, dtype=x.dtype) * top_k_weights[..., None], axis=2)
        h = jax.nn.gelu(jnp.einsum('bnd,edf->benf', x, w1))
        expert_out = jnp.einsum('benf,efd->bend', h, w2)
        output = jnp.einsum('bne,bend->bnd', comb, expert_out)
        return output

    def _L2_attn_ref(x, proj, w_qkv, w_out, b_out, gamma, beta, w1, b1, w2, b2):
        import jax, jax.numpy as jnp
        import numpy as np
        B, N, D = (4, 512, 128)
        H, F = (16, 32)
        HD = D // H
        EPS_ATTN = 1e-08
        EPS_LN = 1e-05

        def _layernorm(x, gamma, beta):
            mu = jnp.mean(x, axis=-1, keepdims=True)
            var = jnp.var(x, axis=-1, keepdims=True)
            return (x - mu) * jax.lax.rsqrt(var + EPS_LN) * gamma + beta
        residual = x
        b, n, d = x.shape
        qkv = x @ w_qkv.T
        q, k, v = jnp.split(qkv, 3, axis=-1)

        def to_heads(t):
            return t.reshape(b, n, H, HD).transpose(0, 2, 1, 3)
        q, k, v = (to_heads(q), to_heads(k), to_heads(v))
        q_f = jax.nn.elu(jnp.einsum('bhnd,hdf->bhnf', q, proj)) + 1.0
        k_f = jax.nn.elu(jnp.einsum('bhnd,hdf->bhnf', k, proj)) + 1.0
        kv = jnp.einsum('bhnf,bhnd->bhfd', k_f, v)
        attn = jnp.einsum('bhnf,bhfd->bhnd', q_f, kv)
        k_sum = jnp.sum(k_f, axis=2)
        z = 1.0 / (jnp.einsum('bhnf,bhf->bhn', q_f, k_sum) + EPS_ATTN)
        attn = attn * z[..., None]
        attn = attn.transpose(0, 2, 1, 3).reshape(b, n, d)
        x = residual + attn @ w_out.T + b_out
        x = _layernorm(x, gamma, beta)
        h = jax.nn.gelu(x @ w1.T + b1, approximate=False)
        x = x + h @ w2.T + b2
        x = _layernorm(x, gamma, beta)
        return x

    def _L2_xattn_ref(query, key, value, Wq, bq, Wk, bk, Wv, bv, Wo, bo):
        import jax, jax.numpy as jnp
        import numpy as np
        N_HEADS = 16
        HIDDEN = 128
        HEAD = HIDDEN // N_HEADS
        B, Sq, H = query.shape
        Sk = key.shape[1]
        q = (query @ Wq + bq).reshape(B, Sq, N_HEADS, HEAD).transpose(0, 2, 1, 3)
        k = (key @ Wk + bk).reshape(B, Sk, N_HEADS, HEAD).transpose(0, 2, 1, 3)
        v = (value @ Wv + bv).reshape(B, Sk, N_HEADS, HEAD).transpose(0, 2, 1, 3)
        scores = jnp.einsum('bhqd,bhkd->bhqk', q, k) / np.sqrt(HEAD).astype(np.float32)
        attn = jax.nn.softmax(scores, axis=-1)
        out = jnp.einsum('bhqk,bhkd->bhqd', attn, v)
        out = out.transpose(0, 2, 1, 3).reshape(B, Sq, H)
        return out @ Wo + bo

    def _L2_ffn_ref(x, gate_w, beta, gate_proj_w, up_proj_w, down_proj_w, shared_gate_w, shared_up_w, shared_down_w):
        import jax, jax.numpy as jnp
        import numpy as np
        E = 8
        H = 128
        M = 256
        K = 2
        SE = 1
        BSZ, SEQ = (2, 128)
        W_SCALE = 0.02
        B0, S0, H0 = x.shape
        xt = x.reshape(-1, H0)
        B = xt.shape[0]
        logits = xt @ gate_w.T
        _, idx = jax.lax.top_k(logits + beta, K)
        probs = jax.nn.sigmoid(jnp.take_along_axis(logits, idx, axis=-1))
        c = jnp.zeros((B, E), xt.dtype).at[jnp.arange(B)[:, None], idx].add(probs)
        g = jnp.einsum('bh,ehm->bem', xt, gate_proj_w)
        u = jnp.einsum('bh,ehm->bem', xt, up_proj_w)
        h = jax.nn.silu(g) * u
        eo = jnp.einsum('bem,emh->beh', h, down_proj_w)
        combined = jnp.einsum('beh,be->bh', eo, c)
        sg = jnp.einsum('bh,ehm->bem', xt, shared_gate_w)
        su = jnp.einsum('bh,ehm->bem', xt, shared_up_w)
        sh = jax.nn.silu(sg) * su
        shared_out = jnp.einsum('bem,emh->beh', sh, shared_down_w).sum(axis=1)
        return (combined + shared_out).reshape(B0, S0, H0)

    def _L3_attn_ref(hidden_states, basis_w, core, head_residual, v_w, v_b, o_w, o_b):
        import jax, jax.numpy as jnp
        import numpy as np
        import math
        N_HEAD = 16
        LATENT_RANK = 64
        B, T, C = hidden_states.shape
        H = N_HEAD
        R = LATENT_RANK
        head_dim = C // H
        latent = jnp.einsum('btc,rc->btr', hidden_states, basis_w)
        core_sym = 0.5 * (core + core.T)
        centered = head_residual - head_residual.mean(axis=0, keepdims=True)
        head_mats = core_sym[None] / float(H) + centered
        lt = jnp.einsum('btr,hrs->bhts', latent, head_mats)
        att = jnp.einsum('bhts,bus->bhtu', lt, latent) * (1.0 / math.sqrt(R))
        causal = jnp.tril(jnp.ones((T, T), jnp.bool_))
        att = jnp.where(causal[None, None], att, jnp.float32(-jnp.inf))
        att = jax.nn.softmax(att, axis=-1)
        v = (hidden_states @ v_w.T + v_b).reshape(B, T, H, head_dim).transpose(0, 2, 1, 3)
        y = att @ v
        y = y.transpose(0, 2, 1, 3).reshape(B, T, C)
        y = y @ o_w.T + o_b
        return y

    def _L3_xattn_ref(q, k, v, igate_kernel, igate_bias, fgate_kernel, fgate_bias, outnorm_weight):
        import jax, jax.numpy as jnp
        import numpy as np
        EPS = 1e-06
        LN_EPS = 1e-06

        def _mlstm_parallel_stabilized(q, k, v, igate_preact, fgate_preact):
            B, NH, S, DH = q.shape
            log_fg = jax.nn.log_sigmoid(fgate_preact[..., 0])
            cs = jnp.cumsum(log_fg, axis=-1)
            fg_mat = cs[..., :, None] - cs[..., None, :]
            mask = jnp.tril(jnp.ones((S, S), dtype=bool))
            log_D = jnp.where(mask, fg_mat + igate_preact[..., 0][..., None, :], -jnp.inf)
            max_log_D = jnp.max(log_D, axis=-1, keepdims=True)
            D = jnp.exp(log_D - max_log_D)
            k_scaled = k / jnp.sqrt(jnp.float32(DH)).astype(k.dtype)
            qk = jnp.einsum('bhsd,bhtd->bhst', q, k_scaled)
            C = qk * D
            normalizer = jnp.maximum(jnp.abs(jnp.sum(C, axis=-1, keepdims=True)), jnp.exp(-max_log_D))
            C_norm = C / (normalizer + EPS)
            return jnp.einsum('bhst,bhtd->bhsd', C_norm, v)

        def _multihead_layernorm(x, weight):
            mu = jnp.mean(x, axis=-1, keepdims=True)
            var = jnp.mean(jnp.square(x - mu), axis=-1, keepdims=True)
            xn = (x - mu) * jax.lax.rsqrt(var + LN_EPS)
            return xn * weight[None, :, None, :]
        B, S, E = q.shape
        NH = igate_bias.shape[0]
        qkv = jnp.concatenate([q, k, v], axis=-1)
        igate_preact = qkv @ igate_kernel + igate_bias
        fgate_preact = qkv @ fgate_kernel + fgate_bias
        qh = q.reshape(B, S, NH, -1).transpose(0, 2, 1, 3)
        kh = k.reshape(B, S, NH, -1).transpose(0, 2, 1, 3)
        vh = v.reshape(B, S, NH, -1).transpose(0, 2, 1, 3)
        ig = igate_preact.transpose(0, 2, 1)[..., None]
        fg = fgate_preact.transpose(0, 2, 1)[..., None]
        h = _mlstm_parallel_stabilized(qh, kh, vh, ig, fg)
        h_norm = _multihead_layernorm(h, outnorm_weight)
        return h_norm.transpose(0, 2, 1, 3).reshape(B, S, -1)

    def _L3_ffn_ref(x, weight, bias):
        import jax, jax.numpy as jnp
        import numpy as np
        IN_FEATURES = 128
        OUT_FEATURES = 128
        B, S = (8, 512)
        w_scale = jnp.mean(jnp.abs(weight))
        q_weight = jnp.sign(weight) * (jnp.abs(weight) > 0.5 * w_scale).astype(weight.dtype)
        i_scale = jnp.max(jnp.abs(x)) / 127.0
        q_input = jnp.clip(jnp.round(x / i_scale), -128.0, 127.0)
        out = jnp.einsum('bsk,ok->bso', q_input, q_weight) * w_scale * i_scale
        out = out + bias
        return out
    x = _layernorm(x + _L0_attn_ref(x, L0_attn_W_qkv, L0_attn_W_out), axis=-1)
    x = _layernorm(x + _L0_xattn_ref(x, ctx_1024, L0_xattn_Wq, L0_xattn_Wkv, L0_xattn_Wout, L0_xattn_bout), axis=-1)
    x = _layernorm(x + _L0_ffn_ref(x, L0_ffn_gate_w, L0_ffn_gate_bias, L0_ffn_w1, L0_ffn_w2, L0_ffn_w3, L0_ffn_sw1, L0_ffn_sw2, L0_ffn_sw3), axis=-1)
    x = _layernorm(x + _L1_attn_ref(x, L1_attn_Wq, L1_attn_Wk, L1_attn_Wv, L1_attn_Wb, L1_attn_bb, L1_attn_Wo, L1_attn_bo, L1_attn_scale), axis=-1)
    x = _layernorm(x + _L1_xattn_ref(x, ctx_1024, L1_xattn_w_q, L1_xattn_w_kv, L1_xattn_w_out, L1_xattn_b_out), axis=-1)
    x = _layernorm(x + _L1_ffn_ref(x, L1_ffn_gate_w, L1_ffn_w1, L1_ffn_w2), axis=-1)
    x = _layernorm(x + _L2_attn_ref(x, L2_attn_proj, L2_attn_w_qkv, L2_attn_w_out, L2_attn_b_out, L2_attn_gamma, L2_attn_beta, L2_attn_w1, L2_attn_b1, L2_attn_w2, L2_attn_b2), axis=-1)
    x = _layernorm(x + _L2_xattn_ref(x, ctx_1024, ctx_1024, L2_xattn_Wq, L2_xattn_bq, L2_xattn_Wk, L2_xattn_bk, L2_xattn_Wv, L2_xattn_bv, L2_xattn_Wo, L2_xattn_bo), axis=-1)
    x = _layernorm(x + _L2_ffn_ref(x, L2_ffn_gate_w, L2_ffn_beta, L2_ffn_gate_proj_w, L2_ffn_up_proj_w, L2_ffn_down_proj_w, L2_ffn_shared_gate_w, L2_ffn_shared_up_w, L2_ffn_shared_down_w), axis=-1)
    x = _layernorm(x + _L3_attn_ref(x, L3_attn_basis_w, L3_attn_core, L3_attn_head_residual, L3_attn_v_w, L3_attn_v_b, L3_attn_o_w, L3_attn_o_b), axis=-1)
    x = _layernorm(x + _L3_xattn_ref(x, ctx_1024, ctx_1024, L3_xattn_igate_kernel, L3_xattn_igate_bias, L3_xattn_fgate_kernel, L3_xattn_fgate_bias, L3_xattn_outnorm_weight), axis=-1)
    x = _layernorm(x + _L3_ffn_ref(x, L3_ffn_weight, L3_ffn_bias), axis=-1)
    return x

_drawn_inputs = setup_inputs


def setup_inputs(seed=0):
    import zlib

    import numpy as np

    out = dict(_drawn_inputs(seed))
    spreads = {'L0_xattn_bout': (0.0, 0.1),
     'L1_attn_bb': (2.944438934326172, 0.2),
     'L1_attn_bo': (0.0, 0.1),
     'L1_attn_scale': (1.0, 0.2),
     'L1_xattn_b_out': (0.0, 0.1),
     'L2_attn_b_out': (0.0, 0.1),
     'L2_attn_gamma': (1.0, 0.2),
     'L2_attn_beta': (0.0, 0.1),
     'L2_attn_b1': (0.0, 0.1),
     'L2_attn_b2': (0.0, 0.1),
     'L2_xattn_bq': (0.0, 0.1),
     'L2_xattn_bk': (0.0, 2.0),
     'L2_xattn_bv': (0.0, 0.1),
     'L2_xattn_bo': (0.0, 0.1),
     'L2_ffn_beta': (0.0, 0.8),
     'L3_attn_v_b': (0.0, 0.296),
     'L3_attn_o_b': (0.0, 0.1),
     'L3_xattn_igate_kernel': (0.0, 0.1),
     'L3_xattn_fgate_kernel': (0.0, 0.1),
     'L3_xattn_outnorm_weight': (1.0, 0.2),
     'L3_ffn_bias': (0.0, 0.1)}
    factors = {'L0_ffn_gate_w': 4.324,
     'L0_ffn_gate_bias': 5.481,
     'L0_ffn_w1': 4.705,
     'L0_ffn_w2': 4.908,
     'L0_ffn_w3': 5.901,
     'L1_xattn_w_q': 8.0,
     'L2_ffn_gate_w': 6.55,
     'L2_ffn_gate_proj_w': 5.338,
     'L2_ffn_up_proj_w': 5.613,
     'L2_ffn_down_proj_w': 5.746,
     'L2_ffn_shared_gate_w': 4.68,
     'L2_ffn_shared_up_w': 4.786,
     'L2_ffn_shared_down_w': 4.15,
     'L3_attn_basis_w': 59.737,
     'L3_attn_core': 64.0,
     'L3_attn_head_residual': 54.438,
     'L3_xattn_igate_bias': 64.0}
    for name, (base, spread) in spreads.items():
        noise = np.random.default_rng([zlib.crc32(name.encode()), seed]).standard_normal(out[name].shape)
        drawn = base * np.exp(spread * noise) if base else spread * noise
        out[name] = jnp.asarray(drawn.astype(out[name].dtype))
    for name, factor in factors.items():
        out[name] = (out[name] * factor).astype(out[name].dtype)
    return out
```

```python
from contextlib import ExitStack

import numpy as np

import concourse.bass as bass
from concourse import mybir

F32 = mybir.dt.float32
BF16 = mybir.dt.bfloat16
ACT = mybir.ActivationFunctionType
ALU = mybir.AluOpType
X = mybir.AxisListType.X

P = 128
T = 128
D = 128
B = 8
NS = 2
NT = NS * T
H = 16
DH = D // H
HC = 8
DC = D // HC
R = 64
E = 8
BANK = 512
EXP_LN = "natural_log_exp_and_others"
NEG = -float(2 ** 100)
LN_EPS = 1e-5
STAGES = 12
WARM_X, WARM_A, WARM_Y = (8, 1), (4, 1), (3, 0)
WARM_UNIT = {"L0x": 0, "L1x": 2, "L2x": 0, "L3a": 1}
WARM_LONG = 12

CONST = {}
_at = 0
for _n, _w in [("ident", 128), ("neg_causal", 128), ("neg_causal_t", 128), ("causal_t", 128),
               ("head8", 16), ("head8in32", 4), ("head16in64", 4), ("feat32", 4), ("late", 1),
               ("cos", 8), ("sin", 8), ("delta8", 8), ("ones", 128), ("eps", 4)]:
    CONST[_n] = (_at, _w)
    _at += _w
NCONST = _at


def shape_constants():
    c = np.zeros((P, NCONST), np.float32)
    p = np.arange(P)

    def put(name, v):
        a, w = CONST[name]
        c[:v.shape[0], a:a + w] = v.reshape(v.shape[0], w)

    put("ident", np.eye(P, dtype=np.float32))
    put("neg_causal", np.where(p[None, :] > p[:, None], NEG, 0).astype(np.float32))
    put("neg_causal_t", np.where(p[:, None] > p[None, :], NEG, 0).astype(np.float32))
    put("causal_t", (p[:, None] <= p[None, :]).astype(np.float32))
    put("head8", (p[:, None] // 8 == np.arange(16)).astype(np.float32))
    put("head8in32", (p[:, None] % 32 // 8 == np.arange(4)).astype(np.float32))
    put("head16in64", (p[:, None] % 64 // 16 == np.arange(4)).astype(np.float32))
    put("feat32", (p[:, None] // 32 == np.arange(4)).astype(np.float32))
    put("late", (p[:, None] >= 64).astype(np.float32))
    inv = np.float32(1.0) / np.float32(10000.0) ** (np.arange(0, 8, 2, dtype=np.float32) / np.float32(8))
    ang = np.concatenate([p.astype(np.float32)[:, None] * inv[None, :]] * 2, axis=1)
    sin = np.sin(ang)
    sin[:, :4] *= -1
    put("cos", np.cos(ang))
    put("sin", sin)
    put("delta8", np.eye(8, dtype=np.float32))
    put("ones", np.ones((P, 128), np.float32))
    put("eps", np.tile(np.array([1e-5, 1e-6, 1.0, 0.0], np.float32), (P, 1)))
    return c


WEIGHTS = [
    ("consts", P, NCONST), ("L3m_core", R, 64), ("L3m_coreT", R, 64), ("L3m_mats", R, 1024),
    ("L0a_qkv", P, 384), ("L0a_o", P, 128),
    ("L0x_q", P, 128), ("L0x_kv", P, 256), ("L0x_o", P, 128), ("L0x_bo", 1, 128),
    ("L0f_gate", P, 8), ("L0f_gb", P, 8), ("L0f_w1", P, 9 * 256), ("L0f_w3", P, 9 * 256), ("L0f_w2", P, 9 * 256),
    ("L1a_qkv", P, 384), ("L1a_b", P, 16), ("L1a_bb", 16, 1), ("L1a_o", P, 128), ("L1a_bo", 1, 128),
    ("L1a_scale", P, 128),
    ("L1x_q", P, 1024), ("L1x_kv", P, 2048), ("L1x_o", P, 1024), ("L1x_bo", 1, 128),
    ("L1f_gate", P, 8), ("L1f_w1", P, 8 * 512), ("L1f_w2", P, 8 * 512),
    ("L2a_qkv", P, 384), ("L2a_proj", P, 512), ("L2a_o", P, 128), ("L2a_bo", 1, 128),
    ("L2a_gamma", P, 128), ("L2a_beta", P, 128), ("L2a_w1", P, 512), ("L2a_b1", P, 4), ("L2a_w2", P, 512),
    ("L2a_b2", 1, 128),
    ("L2x_q", P, 128), ("L2x_k", P, 128), ("L2x_v", P, 128), ("L2x_o", P, 128),
    ("L2x_bq", P, 1), ("L2x_bk", P, 1), ("L2x_bv", 1, 128), ("L2x_bo", 1, 128),
    ("L2f_gate", P, 8), ("L2f_gb", P, 8), ("L2f_w1", P, 9 * 256), ("L2f_w3", P, 9 * 256), ("L2f_w2", P, 9 * 256),
    ("L3a_basis", P, 128), 
    ("L3a_v", P, 128), ("L3a_vb", 1, 128), ("L3a_o", P, 128), ("L3a_bo", 1, 128),
    ("L3x_gates", P, 3 * 16), ("L3x_ib", 8, 1), ("L3x_fb", 8, 1), ("L3x_w", P, 128),
    ("L3f_w", P, 128), ("L3f_b", P, 128),
]


def build(nc, dram, out):
    with ExitStack() as ctx:
        _build(nc, ctx, dram, out)


def _build(nc, ctx, dram, out):
    def sb(name, shape, dt=F32):
        return ctx.enter_context(nc.sbuf_tensor(name, shape, dt))

    pe, dve, act, sp = nc.tensor, nc.vector, nc.scalar, nc.sync

    W = {n: sb(n, [p, w]) for n, p, w in WEIGHTS if not n.startswith("L2f_w")}
    for n in ("w1", "w3", "w2"):
        W["L2f_" + n] = W["L0f_" + n]
    head_mats = W["L3m_mats"]
    w_in, w_count = {}, {}
    for n, _, _ in WEIGHTS:
        if n.startswith("L2f_w"):
            continue
        if n[:3] not in w_in:
            w_in[n[:3]] = ctx.enter_context(nc.semaphore(f"weights_{n[:3]}"))
        w_count[n[:3]] = w_count.get(n[:3], 0) + 16

    def weights(prefix):
        return w_in[prefix], w_count[prefix]

    def const(name, rows=P):
        a, w = CONST[name]
        return W["consts"][0:rows, a:a + w]

    IDENT = const("ident")
    ident_bf = sb("ident_bf", [P, P], BF16)
    neg_wide_bf = sb("neg_wide_bf", [P, 2 * P], BF16)
    neg_causal_bf = neg_wide_bf[:, P:2 * P]
    neg_causal_t_bf = sb("neg_causal_t_bf", [P, P], BF16)
    ones_row = const("ones", 1)[:, 0:128]
    core_sym = sb("core_sym", [R, R])
    res_mean = sb("res_mean", [R, R])
    neg_bb = sb("neg_bb", [H, 1])
    a_tok = sb("a_tok", [P, NS, HC])

    x_tok = sb("x_tok", [P, NS, D])
    xT = sb("xT", [P, NT])
    ctx_tok = sb("ctx_tok", [P, NS, D])
    ctxT = sb("ctxT", [P, NT])
    x_all = sb("x_all", [P, B, D])
    xT_all = sb("xT_all", [P, B * T])

    res = sb("res", [P, NS, D])
    stats = sb("stats", [P, NS, 6])
    mv = sb("mv", [P, NS, 2])
    lnv = sb("lnv", [P, NS, 1])
    rstd = sb("rstd", [P, NS, 1])
    qs = sb("qs", [P, NS, D])
    ks = sb("ks", [P, NS, D])
    qk2 = sb("qk2", [P, 2, D])
    qk3 = sb("qk3", [P, 2, D])
    qT = sb("qT", [P, 2, NT])
    kT = sb("kT", [P, NT])
    share_a = sb("share_a", [P, NS * H * (R + 1)])
    bd = share_a[:, 0:NS * 4 * 2 * T].rearrange("p (u j t) -> p u j t", u=NS, j=4)
    vaug_r = share_a[:].rearrange("p (u h d) -> p u h d", u=NS, h=H)
    small = sb("small", [P, NS, 64])
    small2 = sb("small2", [P, NS, 64])
    vaug = sb("vaug", [P, NS, 2, H, DH + 1])
    vaug_c = sb("vaug_c", [P, NS, HC, DC + 1])
    ctxbd = sb("ctxbd", [P, NS, H, DH + 1])
    attn = sb("attn", [P, NS, D])
    attnT = sb("attnT", [P, NS, D])
    NPB = 3
    probs = sb("probs", [P, NPB, BANK])
    probsT = sb("probsT", [P, NPB, BANK])
    q64 = sb("q64", [P, 8, NT])
    k64 = sb("k64", [P, 8, NT])
    NHB = 4
    gact = sb("gact", [P, NHB, BANK])
    hT = sb("hT", [P, NHB, BANK])
    attn64 = gact[:].rearrange("p b (c r d) -> p (b c) r d", c=4, r=2).rearrange("p (u c) r d -> p u c r d", u=NS)
    attn64T = hT[:].rearrange("p b (c t) -> p (b c) t", c=4).rearrange("p (u c) t -> p u c t", u=NS)
    feats_q = q64
    pad4 = q64[:, 0:4, :]
    lat_pad = k64[:, 0:2, :]
    bq4 = sb("bq4", [P, 4])
    gateT = sb("gateT", [H, 6, NT])
    mdiag = k64[0:8].rearrange("p (u h) (a t) -> p u (h a) t", u=NS, a=2)

    psum = [ctx.enter_context(nc.psum_tensor(f"bank{i}", [P, BANK], F32)) for i in range(8)]

    setup_dve = ctx.enter_context(nc.semaphore("setup_dve"))
    stored = ctx.enter_context(nc.semaphore("stored"))

    sems = {}

    def S(name):
        if name not in sems:
            sems[name] = ctx.enter_context(nc.semaphore(name))
        return sems[name]

    counted = {}

    def nth(eng, name, n=1):
        counted[eng, name] = counted.get((eng, name), 0) + n
        return S(name), counted[eng, name]

    class Ring:

        def __init__(self):
            self.fills = [0] * 8
            self.frees = [{"dve": 0, "act": 0} for _ in range(8)]
            self.last = [None] * 8
            self.at = {}
            self.n = 0

        def open(self, key, by, bank=None):
            if bank is None:
                bank, self.n = self.n % 6, self.n + 1
            if self.last[bank]:
                pe.wait_ge(S(f"bank{bank}_freed_{self.last[bank]}"), self.frees[bank][self.last[bank]])
            self.fills[bank] += 1
            self.frees[bank][by] += 1
            self.last[bank] = by
            assert key not in self.at, key
            self.at[key] = (bank, self.fills[bank], by, self.frees[bank][by])
            return psum[bank]

        def filled(self, key):
            return S(f"bank{self.at[key][0]}_full")

        def full(self, key):
            b, n, _, _ = self.at[key]
            return S(f"bank{b}_full"), n

        def freed(self, key):
            b, _, by, n = self.at[key]
            return S(f"bank{b}_freed_{by}"), n

        def free(self, key):
            b, _, by, _ = self.at[key]
            return S(f"bank{b}_freed_{by}")

        def bank(self, key):
            return psum[self.at[key][0]]

    ring = Ring()

    class Order:

        def __init__(self, eng, name):
            self.eng, self.name, self.n = eng, name, {}

        def link(self, ins, sem=None):
            sem = sem or S(f"{self.name}_step")
            key = id(sem)
            self.n[key] = self.n.get(key, 0) + 1
            ins.then_inc(sem, 1)
            self.eng.wait_ge(sem, self.n[key])

    def heads(ap, n):
        return ap.rearrange("p (h d) -> p h d", h=n)

    def over(ap, n):
        return ap.unsqueeze(2).to_broadcast([ap.shape[0], ap.shape[1], n])

    def among(ap, n):
        return ap.unsqueeze(1).to_broadcast([ap.shape[0], n, ap.shape[1]])

    def hidden(e, k, per):
        if per == 2:
            return hT[:, (2 * e + k) % NHB, 0:NT]
        return hT[:, (2 * e + k // 2) % NHB, (k % 2) * NT:(k % 2 + 1) * NT]

    def tk(u):
        return slice(u * T, u * T + T)

    with nc.Block(name="setup") as block:
        @block.sync
        def _(eng):
            for n, _, _ in WEIGHTS:
                if not n.startswith("L2f_w"):
                    sp.dma_start(W[n][:], dram[n]).then_inc(w_in[n[:3]], 16)

        @block.vector
        def _(eng):
            o = Order(dve, "setup")
            dve.wait_ge(*weights("con"))
            o.link(dve.tensor_copy(ident_bf[:], IDENT), setup_dve)
            o.link(dve.memset(neg_wide_bf[:, 0:P], 0.0), setup_dve)
            o.link(dve.tensor_copy(neg_causal_bf, const("neg_causal")), setup_dve)
            o.link(dve.tensor_copy(neg_causal_t_bf[:], const("neg_causal_t")), setup_dve)
            o.link(dve.memset(vaug[:], 1.0), setup_dve)
            o.link(dve.memset(vaug_c[:], 1.0), setup_dve)
            dve.wait_ge(*weights("L3m"))
            hr = head_mats[:].rearrange("p (h s) -> p h s", h=H)
            o.link(dve.tensor_tensor(core_sym[:], W["L3m_core"][:], W["L3m_coreT"][:], ALU.add), setup_dve)
            o.link(dve.tensor_reduce(res_mean[:], hr.rearrange("p h s -> p s h"), X, ALU.add), setup_dve)
            o.link(dve.tensor_scalar(res_mean[:], res_mean[:], -1.0 / H, None, ALU.mult), setup_dve)
            o.link(dve.scalar_tensor_tensor(core_sym[:], core_sym[:], 0.5 / H, res_mean[:], ALU.mult, ALU.add), setup_dve)
            o.link(dve.tensor_tensor(hr, hr, among(core_sym[:], H), ALU.add), setup_dve)

    STAGES_RUN = STAGES
    with nc.Fori(0, B // NS) as pair:
        with nc.Block(name="pair") as block:
            @block.tensor
            def _(eng):
                mm, tr = pe.matmul, pe.transpose

                def warm(bank, n):
                    for _ in range(n):
                        mm(heads(bank[:], 2), ident_bf[:], among(neg_wide_bf[:], 2), start=True, stop=True)

                def transpose_x():
                    for u in range(NS):
                        b = ring.open(("xT", stage[0], u), "act")
                        warm(b, WARM_X[u])
                        pe.wait_ge(*nth("pe", "x_new"))
                        tr(b[:, 0:T], x_tok[:, u, :], IDENT).then_inc(ring.filled(("xT", stage[0], u)), 1)

                def wait_xT():
                    for u in range(NS):
                        pe.wait_ge(*ring.freed(("xT", stage[0] - 1, u)))

                def row_bias(out_ap, row):
                    mm(out_ap, ones_row, row, start=False, stop=True)

                def attn_out(st, w, bias):
                    for u in range(NS):
                        b = ring.open((st, "aT", u), "act")
                        warm(b, WARM_A[u])
                        pe.wait_ge(*ring.freed((st, "o", u)))
                        tr(b[:, 0:T], attn[:, u, :], IDENT).then_inc(ring.filled((st, "aT", u)), 1)
                    for u in range(NS):
                        b = ring.open((st, "y", u), "dve")
                        warm(b, WARM_Y[u])
                        pe.wait_ge(*ring.freed((st, "aT", u)))
                        m = mm(b[:, 0:D], attnT[:, u, :], w, start=True, stop=bias is None)
                        if bias is not None:
                            m = mm(b[:, 0:D], ones_row, bias, start=False, stop=True)
                        m.then_inc(ring.filled((st, "y", u)), 1)

                def softmax_units(st, n_units, score, value, acc):
                    total = NS * n_units
                    for step in range(total + 3):
                        if step < total:
                            b = ring.open((st, "s", step), "dve")
                            score(step // n_units, step % n_units, b).then_inc(ring.filled((st, "s", step)), 1)
                        i = step - 2
                        if 0 <= i < total:
                            b = ring.open((st, "pT", i), "act")
                            warm(b, WARM_UNIT[st])
                            pe.wait_ge(*nth("pe", "probs_ready"))
                            for k in range(4):
                                t_ = tr(b[:, k * T:k * T + T], probs[:, i % NPB, k * T:k * T + T], IDENT)
                            t_.then_inc(ring.filled((st, "pT", i)), 1)
                        i = step - 3
                        if 0 <= i < total:
                            pe.wait_ge(*ring.freed((st, "pT", i)))
                            u, n = i // n_units, i % n_units
                            if acc == "slot":
                                b = psum[6 + u] if n else ring.open((st, "o", u), "dve", 6 + u)
                            else:
                                b = ring.open((st, "o", i), "dve")
                            last = value(u, n, i % NPB, b)
                            if acc == "unit":
                                last.then_inc(ring.filled((st, "o", i)), 1)
                            elif n == n_units - 1:
                                last.then_inc(ring.filled((st, "o", u)), 1)

                stage = [0]
                pe.wait_ge(S("x_in"), 4 * 16)
                pe.wait_ge(*weights("con"))
                pe.wait_ge(setup_dve, 4)

                if STAGES_RUN > 0:
                    pe.wait_ge(*weights("L0a"))
                    for u in range(NS):
                        b = ring.open(("L0a", "qv", u), "dve")
                        mm(b[:, 0:D], xT[:, tk(u)], W["L0a_qkv"][:, 0:D], start=True, stop=True)
                        mm(b[:, D:2 * D], xT[:, tk(u)], W["L0a_qkv"][:, 2 * D:3 * D], start=True, stop=True)\
                            .then_inc(ring.filled(("L0a", "qv", u)), 1)
                        b = ring.open(("L0a", "k", u), "act")
                        mm(b[:, 0:D], xT[:, tk(u)], W["L0a_qkv"][:, D:2 * D], start=True, stop=True)\
                            .then_inc(ring.filled(("L0a", "k", u)), 1)
                    for u in range(NS):
                        pe.wait_ge(*nth("pe", "L0a_v"))
                        pe.wait_ge(*ring.freed(("L0a", "k", u)))
                        b = ring.open(("L0a", "ctx", u), "dve")
                        mm(b[:, 0:H * 9], ks[0:64, u, :], vaug[0:64, u, 0].rearrange("p h d -> p (h d)"),
                           start=True, stop=True).then_inc(ring.filled(("L0a", "ctx", u)), 1)
                        pe.wait_ge(*nth("pe", "L0a_qs"))
                        b = ring.open(("L0a", "qsT", u), "act")
                        tr(b[:, 0:T], qs[:, u, :], IDENT).then_inc(ring.filled(("L0a", "qsT", u)), 1)
                    for u in range(NS):
                        pe.wait_ge(*ring.freed(("L0a", "ctx", u)))
                        pe.wait_ge(*ring.freed(("L0a", "qsT", u)))
                        b = ring.open(("L0a", "o", u), "dve", 6 + u)
                        mm(b[:, 0:H * 9], qT[:, 0, tk(u)], ctxbd[:, u].rearrange("p h d -> p (h d)"),
                           start=True, stop=True).then_inc(ring.filled(("L0a", "o", u)), 1)
                    attn_out("L0a", W["L0a_o"][:], None)
                    transpose_x()

                def qkT_products(st, pairs_, key, by):
                    b = ring.open((st, key), by)
                    for i, (w, src) in enumerate(pairs_):
                        m = mm(b[:, i * NT:(i + 1) * NT], w, src, start=True, stop=True)
                    m.then_inc(ring.filled((st, key)), 1)

                if STAGES_RUN > 1:
                    stage[0] = 1
                    pe.wait_ge(*weights("L0x"))
                    wait_xT()
                    qkT_products("L0x", [(W["L0x_q"][:], xT[:])], "q", "act")
                    qkT_products("L0x", [(W["L0x_kv"][:, 0:D], ctxT[:]), (W["L0x_kv"][:, 0:D], xT[:])], "k", "dve")
                    b = ring.open(("L0x", "v"), "dve")
                    for u in range(NS):
                        for s_, src in enumerate((ctxT, xT)):
                            c = (2 * u + s_) * D
                            m = mm(b[:, c:c + D], src[:, tk(u)], W["L0x_kv"][:, D:2 * D], start=True, stop=True)
                    m.then_inc(ring.filled(("L0x", "v")), 1)
                    pe.wait_ge(*ring.freed(("L0x", "q")))
                    pe.wait_ge(*ring.freed(("L0x", "k")))

                    def score(u, n, b):
                        c, j = n // 2, 2 * (n % 2)
                        mm(heads(b[:], 2), ident_bf[:], among(neg_wide_bf[:], 2), start=True, stop=False)
                        return mm(heads(b[:], 2), pad4[:, c, tk(u)], bd[:, u, j:j + 2, :], start=False, stop=True)

                    def value(u, n, buf, b):
                        for k in range(2):
                            h = 2 * n + k
                            for s_ in range(2):
                                c = (2 * k + s_) * T
                                m = mm(b[:, 9 * h:9 * h + 9], probsT[:, buf, c:c + T], vaug[:, u, s_, h, :],
                                       start=s_ == 0, stop=s_ == 1)
                        return m

                    pe.wait_ge(*ring.freed(("L0x", "v")))
                    softmax_units("L0x", 8, score, value, "slot")
                    attn_out("L0x", W["L0x_o"][:], W["L0x_bo"][:])
                    transpose_x()

                def gate_logits(st, w):
                    b = ring.open((st, "logits"), "dve")
                    for u in range(NS):
                        m = mm(b[:, 8 * u:8 * u + 8], xT[:, tk(u)], w, start=True, stop=True)
                    m.then_inc(ring.filled((st, "logits")), 1)

                def expert_up(st, i, parts):
                    b = ring.open((st, "up", i), "dve" if st != "L1f" else "act")
                    for k, w in enumerate(parts):
                        m = mm(b[:, k * NT:(k + 1) * NT], w, xT[:], start=True, stop=True)
                    m.then_inc(ring.filled((st, "up", i)), 1)

                def expert_down(st, e, per):
                    b = ring.open((st, "y", e), "dve")
                    for u in range(NS):
                        for k in range(per):
                            m = mm(b[:, u * D:(u + 1) * D], hidden(e, k, per)[:, tk(u)],
                                   W[st + "_w2"][:, (per * e + k) * P:(per * e + k + 1) * P],
                                   start=k == 0, stop=k == per - 1)
                    m.then_inc(ring.filled((st, "y", e)), 1)

                def swiglu(st):
                    pe.wait_ge(*weights(st))
                    wait_xT()
                    gate_logits(st, W[st + "_gate"][:])
                    if st == "L2f":
                        pe.wait_ge(S("L2f_in"), 3 * 16)
                    for i in range(20):
                        if i < 18:
                            f = i * 128
                            expert_up(st, i, (W[st + "_w1"][:, f:f + 128], W[st + "_w3"][:, f:f + 128]))
                        if i % 2 == 1 and i >= 3:
                            pe.wait_ge(*ring.freed((st, "up", i - 3)))
                            pe.wait_ge(*ring.freed((st, "up", i - 2)))
                            expert_down(st, (i - 3) // 2, 2)
                    transpose_x()

                if STAGES_RUN > 2:
                    stage[0] = 2
                    swiglu("L0f")

                if STAGES_RUN > 3:
                    stage[0] = 3
                    pe.wait_ge(*weights("L1a"))
                    wait_xT()
                    b = ring.open(("L1a", "beta"), "act")
                    mm(b[0:H, 0:NT], W["L1a_b"][:], xT[:], start=True, stop=True)\
                        .then_inc(ring.filled(("L1a", "beta")), 1)
                    for u in range(NS):
                        b = ring.open(("L1a", "qkv", u), "dve")
                        mm(b[:, 0:3 * D], xT[:, tk(u)], W["L1a_qkv"][:], start=True, stop=True)\
                            .then_inc(ring.filled(("L1a", "qkv", u)), 1)
                    b = ring.open(("L1a", "decay"), "dve")
                    warm(b, WARM_LONG)
                    pe.wait_ge(*nth("pe", "L1a_decay"))
                    for u in range(NS):
                        m = tr(b[:, u * H:u * H + H], gateT[0:H, 3, tk(u)], IDENT[0:H, 0:H])
                    m.then_inc(ring.filled(("L1a", "decay")), 1)
                    for u in range(NS):
                        b = ring.open(("L1a", "qT", u), "dve")
                        warm(b, WARM_LONG)
                        pe.wait_ge(*nth("pe", "L1a_qk"))
                        tr(b[:, 0:T], qs[:, u, :], IDENT).then_inc(ring.filled(("L1a", "qT", u)), 1)
                        b = ring.open(("L1a", "kT", u), "act")
                        tr(b[:, 0:T], ks[:, u, :], IDENT).then_inc(ring.filled(("L1a", "kT", u)), 1)
                    for u in range(NS):
                        pe.wait_ge(*ring.freed(("L1a", "qT", u)))
                        pe.wait_ge(*ring.freed(("L1a", "kT", u)))
                    for i in range(2 * 4 + 1):
                        if i < 8:
                            u, c = i // 4, i % 4
                            b = ring.open(("L1a", "s", i), "dve")
                            mm(heads(b[:], 4), pad4[:, c, tk(u)], bd[:, u, :, 0:T],
                               start=True, stop=True).then_inc(ring.filled(("L1a", "s", i)), 1)
                        if i >= 1:
                            u, c = (i - 1) // 4, (i - 1) % 4
                            pe.wait_ge(*ring.freed(("L1a", "s", i - 1)))
                            b = psum[6 + u] if c else ring.open(("L1a", "o", u), "dve", 6 + u)
                            for j in range(4):
                                h = 4 * c + j
                                m = mm(b[:, 9 * h:9 * h + 9], probs[:, (i - 1) % NPB, j * T:j * T + T],
                                       vaug[:, u, 0, h, :], start=True, stop=True)
                            m.then_inc(ring.filled(("L1a", "o", u)) if c == 3 else S("L1a_used"), 1)
                    attn_out("L1a", W["L1a_o"][:], W["L1a_bo"][:])
                    transpose_x()

                def score64(rhs_of):
                    def score(u, n, b, first=True):
                        r, c0 = n % 2, 4 * (n // 2)
                        for j in range(4):
                            rows, rhs = rhs_of(r, c0 + j, u)
                            m = mm(b[:, j * T:j * T + T], q64[rows, c0 + j, tk(u)], rhs,
                                   start=first, stop=first or j == 3)
                        return m
                    return score

                if STAGES_RUN > 4:
                    stage[0] = 4
                    pe.wait_ge(*weights("L1x"))
                    for c in range(0, 8, 2):
                        qkT_products("L1x", [(W["L1x_kv"][:, (c + k) * P:(c + k + 1) * P], ctxT[:]) for k in range(2)],
                                     f"k{c}", "dve")
                    for u in range(NS):
                        for c in range(2):
                            b = ring.open(("L1x", "v", u, c), "dve")
                            mm(b[:], ctxT[:, tk(u)], W["L1x_kv"][:, 1024 + c * BANK:1024 + (c + 1) * BANK],
                               start=True, stop=True).then_inc(ring.filled(("L1x", "v", u, c)), 1)
                    wait_xT()
                    for c in range(0, 8, 2):
                        qkT_products("L1x", [(W["L1x_q"][:, (c + k) * P:(c + k + 1) * P], xT[:]) for k in range(2)],
                                     f"q{c}", "act")
                    for c in range(0, 8, 2):
                        pe.wait_ge(*ring.freed(("L1x", f"k{c}")))
                        pe.wait_ge(*ring.freed(("L1x", f"q{c}")))
                    for u in range(NS):
                        for c in range(2):
                            pe.wait_ge(*ring.freed(("L1x", "v", u, c)))

                    def value64(u, n, buf, b):
                        r, c0 = n % 2, 4 * (n // 2)
                        for j in range(4):
                            h = 2 * (c0 + j) + r
                            m = mm(b[:, j * (R + 1):(j + 1) * (R + 1)], probsT[:, buf, j * T:j * T + T],
                                   vaug_r[:, u, h, :], start=True, stop=True)
                        return m

                    softmax_units("L1x", 4, score64(lambda r, c, u: (slice(64 * r, 64 * r + 64), k64[64 * r:64 * r + 64, c, tk(u)])),
                                  value64, "unit")
                    for u in range(NS):
                        for n in range(4):
                            pe.wait_ge(*ring.freed(("L1x", "o", 4 * u + n)))
                        for c in range(0, 8, 4):
                            b = ring.open(("L1x", "aT", u, c), "act")
                            for k in range(4):
                                m = tr(b[:, k * T:k * T + T], attn64[:, u, c + k].rearrange("p r d -> p (r d)"), IDENT)
                            m.then_inc(ring.filled(("L1x", "aT", u, c)), 1)
                    for u in range(NS):
                        for c in range(0, 8, 4):
                            pe.wait_ge(*ring.freed(("L1x", "aT", u, c)))
                        b = ring.open(("L1x", "y", u), "dve")
                        for c in range(8):
                            mm(b[:, 0:D], attn64T[:, u, c, :], W["L1x_o"][:, c * P:(c + 1) * P], start=c == 0, stop=False)
                        mm(b[:, 0:D], ones_row, W["L1x_bo"][:], start=False, stop=True)\
                            .then_inc(ring.filled(("L1x", "y", u)), 1)
                    transpose_x()

                if STAGES_RUN > 5:
                    stage[0] = 5
                    pe.wait_ge(*weights("L1f"))
                    wait_xT()
                    gate_logits("L1f", W["L1f_gate"][:])
                    for i in range(16 + 3):
                        if i < 16:
                            f = i * 256
                            expert_up("L1f", i, (W["L1f_w1"][:, f:f + 128], W["L1f_w1"][:, f + 128:f + 256]))
                        if i % 2 == 1 and i >= 3:
                            pe.wait_ge(*ring.freed(("L1f", "up", i - 3)))
                            pe.wait_ge(*ring.freed(("L1f", "up", i - 2)))
                            expert_down("L1f", (i - 3) // 2, 4)
                    transpose_x()

                if STAGES_RUN > 6:
                    stage[0] = 6
                    pe.wait_ge(*weights("L2a"))
                    wait_xT()
                    qkT_products("L2a", [(W["L2a_qkv"][:, 0:D], xT[:]), (W["L2a_qkv"][:, D:2 * D], xT[:])], "qk", "act")
                    b = ring.open(("L2a", "v"), "dve")
                    for u in range(NS):
                        m = mm(b[:, u * D:(u + 1) * D], xT[:, tk(u)], W["L2a_qkv"][:, 2 * D:3 * D], start=True, stop=True)
                    m.then_inc(ring.filled(("L2a", "v")), 1)
                    pe.wait_ge(*ring.freed(("L2a", "qk")))
                    for u in range(NS):
                        b = ring.open(("L2a", "kf", u), "dve")
                        mm(b[:], qT[:, 1, tk(u)], W["L2a_proj"][:], start=True, stop=True)\
                            .then_inc(ring.filled(("L2a", "kf", u)), 1)
                    for c in range(0, 4, 2):
                        b = ring.open(("L2a", "qf", c), "dve")
                        for k in range(2):
                            m = mm(b[:, k * NT:(k + 1) * NT], W["L2a_proj"][:, (c + k) * P:(c + k + 1) * P], qT[:, 0, :],
                                   start=True, stop=True)
                        m.then_inc(ring.filled(("L2a", "qf", c)), 1)
                    pe.wait_ge(*ring.freed(("L2a", "v")))
                    for u in range(NS):
                        b = ring.open(("L2a", "kv", u), "dve")
                        warm(b, 2)
                        pe.wait_ge(*ring.freed(("L2a", "kf", u)))
                        for c in range(4):
                            m = mm(b[:, 36 * c:36 * c + 36], probs[:, u, c * P:(c + 1) * P],
                                   vaug[:, u, 0, 4 * c:4 * c + 4, :], start=True, stop=True)
                        m.then_inc(ring.filled(("L2a", "kv", u)), 1)
                    for c in range(0, 4, 2):
                        pe.wait_ge(*ring.freed(("L2a", "qf", c)))
                    for u in range(NS):
                        pe.wait_ge(*ring.freed(("L2a", "kv", u)))
                        b = ring.open(("L2a", "o", u), "dve", 6 + u)
                        for c in range(4):
                            m = mm(b[:, 36 * c:36 * c + 36], feats_q[:, c, tk(u)], ctxbd[:, u, 4 * c:4 * c + 4, :],
                                   start=True, stop=True)
                        m.then_inc(ring.filled(("L2a", "o", u)), 1)
                    attn_out("L2a", W["L2a_o"][:], W["L2a_bo"][:])
                    for u in range(NS):
                        b = ring.open(("L2a", "x1T", u), "act")
                        warm(b, WARM_X[u])
                        pe.wait_ge(*nth("pe", "L2a_x1"))
                        tr(b[:, 0:T], qs[:, u, :], IDENT).then_inc(ring.filled(("L2a", "x1T", u)), 1)
                    for u in range(NS):
                        pe.wait_ge(*ring.freed(("L2a", "x1T", u)))
                    for c in range(0, 4, 2):
                        qkT_products("L2a", [(W["L2a_w1"][:, (c + k) * P:(c + k + 1) * P], kT[:]) for k in range(2)],
                                     f"h{c}", "act")
                    for c in range(0, 4, 2):
                        pe.wait_ge(*ring.freed(("L2a", f"h{c}")))
                    for u in range(NS):
                        b = ring.open(("L2a", "y2", u), "dve")
                        for c in range(4):
                            mm(b[:, 0:D], gact[:, c // 2, (c % 2) * NT + u * T:(c % 2) * NT + u * T + T],
                               W["L2a_w2"][:, c * P:(c + 1) * P], start=c == 0, stop=False)
                        mm(b[:, 0:D], ones_row, W["L2a_b2"][:], start=False, stop=True)\
                            .then_inc(ring.filled(("L2a", "y2", u)), 1)
                    transpose_x()

                def score8(u, n, b):
                    return mm(heads(b[:], 4), pad4[:, n, tk(u)], bd[:, u, :, 0:T], start=True, stop=True)

                def value8(u, n, buf, b):
                    for j in range(4):
                        h = 4 * n + j
                        m = mm(b[:, 9 * h:9 * h + 9], probsT[:, buf, j * T:j * T + T], vaug[:, u, 0, h, :],
                               start=True, stop=True)
                    return m

                if STAGES_RUN > 7:
                    stage[0] = 7
                    pe.wait_ge(*weights("L2x"))
                    qkT_products("L2x", [(W["L2x_k"][:], ctxT[:])], "k", "dve")
                    b = ring.open(("L2x", "v"), "dve")
                    for u in range(NS):
                        mm(b[:, u * D:(u + 1) * D], ctxT[:, tk(u)], W["L2x_v"][:], start=True, stop=False)
                        m = mm(b[:, u * D:(u + 1) * D], ones_row, W["L2x_bv"][:], start=False, stop=True)
                    m.then_inc(ring.filled(("L2x", "v")), 1)
                    wait_xT()
                    qkT_products("L2x", [(W["L2x_q"][:], xT[:])], "q", "act")
                    pe.wait_ge(*ring.freed(("L2x", "k")))
                    pe.wait_ge(*ring.freed(("L2x", "v")))
                    pe.wait_ge(*ring.freed(("L2x", "q")))
                    softmax_units("L2x", 4, score8, value8, "slot")
                    attn_out("L2x", W["L2x_o"][:], W["L2x_bo"][:])
                    transpose_x()

                if STAGES_RUN > 8:
                    stage[0] = 8
                    swiglu("L2f")

                if STAGES_RUN > 9:
                    stage[0] = 9
                    pe.wait_ge(*weights("L3a"))
                    wait_xT()
                    qkT_products("L3a", [(W["L3a_basis"][:], xT[:])], "lat", "act")
                    b = ring.open(("L3a", "v"), "dve")
                    for u in range(NS):
                        mm(b[:, u * D:(u + 1) * D], xT[:, tk(u)], W["L3a_v"][:], start=True, stop=False)
                        m = mm(b[:, u * D:(u + 1) * D], ones_row, W["L3a_vb"][:], start=False, stop=True)
                    m.then_inc(ring.filled(("L3a", "v")), 1)
                    pe.wait_ge(*ring.freed(("L3a", "lat")))
                    for c in range(0, 8, 2):
                        qkT_products("L3a", [(head_mats[:, (c + k) * P:(c + k + 1) * P], lat_pad[0:R, 0, :]) for k in range(2)],
                                     f"q{c}", "act")
                    for c in range(0, 8, 2):
                        pe.wait_ge(*ring.freed(("L3a", f"q{c}")))
                    pe.wait_ge(*ring.freed(("L3a", "v")))
                    latent = score64(lambda r, c, u: (slice(0, P), lat_pad[:, r, tk(u)]))

                    def score_causal(u, n, b):
                        mm(heads(b[:], 4), ident_bf[:], among(neg_causal_bf, 4), start=True, stop=False)
                        return latent(u, n, b, first=False)

                    def value_latent(u, n, buf, b):
                        r, c0 = n % 2, 4 * (n // 2)
                        for j in range(4):
                            h = 2 * (c0 + j) + r
                            m = mm(b[:, 9 * h:9 * h + 9], probsT[:, buf, j * T:j * T + T], vaug[:, u, 0, h, :],
                                   start=True, stop=True)
                        return m

                    softmax_units("L3a", 4, score_causal, value_latent, "slot")
                    attn_out("L3a", W["L3a_o"][:], W["L3a_bo"][:])
                    transpose_x()

                if STAGES_RUN > 10:
                    stage[0] = 10
                    pe.wait_ge(*weights("L3x"))
                    wait_xT()
                    b = ring.open(("L3x", "gates"), "dve")
                    for g in range(2):
                        for k, src in enumerate((xT, ctxT, ctxT)):
                            m = mm(b[0:8, g * NT:(g + 1) * NT], W["L3x_gates"][:, 16 * k + 8 * g:16 * k + 8 * g + 8],
                                   src[:], start=k == 0, stop=k == 2)
                    m.then_inc(ring.filled(("L3x", "gates")), 1)
                    pe.wait_ge(*nth("pe", "L3x_gates"))
                    b = ring.open(("L3x", "mx"), "act")
                    for k, row in enumerate((4, 2)):
                        for u in range(NS):
                            m = tr(b[:, 16 * k + u * 8:16 * k + u * 8 + 8], gateT[0:8, row, tk(u)], IDENT[0:8, 0:8])
                    m.then_inc(ring.filled(("L3x", "mx")), 1)
                    for i in range(2 * 2 + 1):
                        if i < 4:
                            u, g = i // 2, i % 2
                            pe.wait_ge(*nth("pe", "L3x_bd")) if g == 0 else None
                            b = ring.open(("L3x", "D", i), "act")
                            warm(b, 1)
                            mm(heads(b[:], 4), ident_bf[:], among(neg_causal_t_bf[:], 4), start=True, stop=False)
                            mm(heads(b[:], 4), const("ones", 8)[:, 0:T], mdiag[:, u, 4 * g:4 * g + 4, :],
                               start=False, stop=True).then_inc(ring.filled(("L3x", "D", i)), 1)
                            b = ring.open(("L3x", "s", i), "dve")
                            mm(heads(b[:], 4), ctxT[64 * g:64 * g + 64, tk(u)], bd[64 * g:64 * g + 64, u, :, 0:T],
                               start=True, stop=True).then_inc(ring.filled(("L3x", "s", i)), 1)
                        if i >= 1:
                            u, g = (i - 1) // 2, (i - 1) % 2
                            pe.wait_ge(*ring.freed(("L3x", "s", i - 1)))
                            b = psum[6 + u] if g else ring.open(("L3x", "o", u), "dve", 6 + u)
                            for j in range(4):
                                h = 4 * g + j
                                m = mm(b[:, 17 * h:17 * h + 17], probsT[:, (i - 1) % NPB, j * T:j * T + T],
                                       vaug_c[:, u, h, :], start=True, stop=True)
                            m.then_inc(ring.filled(("L3x", "o", u)) if g else S("L3x_used"), 1)
                    transpose_x()

            @block.vector
            def _(eng):
                o = Order(dve, "dve")
                link = o.link

                def layer_norm(u, dst, affine=None, told=None):
                    link(dve.bn_stats(stats[:, u, :], res[:, u, :]))
                    link(dve.bn_aggr(mv[:, u, :], stats[:, u, :]), S("var_ready"))
                    dve.wait_ge(*nth("dve", "rstd_ready"))
                    if affine is None:
                        link(dve.tensor_scalar(dst, res[:, u, :], mv[:, u, 0:1], rstd[:, u, :], ALU.subtract, ALU.mult),
                             told)
                    else:
                        link(dve.tensor_scalar(dst, res[:, u, :], mv[:, u, 0:1], rstd[:, u, :], ALU.subtract, ALU.mult))
                        link(dve.tensor_tensor(dst, dst, affine[0], ALU.mult))
                        link(dve.tensor_tensor(dst, dst, affine[1], ALU.add), told)

                def post_norm(st):
                    for u in range(NS):
                        dve.wait_ge(*ring.full((st, "y", u)))
                        link(dve.tensor_tensor(res[:, u, :], ring.bank((st, "y", u))[:, 0:D], x_tok[:, u, :], ALU.add),
                             ring.free((st, "y", u)))
                    for u in range(NS):
                        layer_norm(u, x_tok[:, u, :], told=S("x_new"))

                def divide_heads(st, u, floor=None, add=None, rows=None):
                    b = heads(ring.bank((st, "o", u))[:, 0:H * 9], H)
                    dve.wait_ge(*ring.full((st, "o", u)))
                    den = small[:, u, 0:H]
                    if floor is not None:
                        link(dve.tensor_scalar(den, b[:, :, 8], floor, None, ALU.max))
                    elif add is not None:
                        link(dve.tensor_scalar(den, b[:, :, 8], add, None, ALU.add))
                    else:
                        link(dve.tensor_copy(den, b[:, :, 8]))
                    link(dve.reciprocal(small2[:, u, 0:H], den))
                    if rows is not None:
                        link(dve.tensor_scalar(small2[:, u, 0:H], small2[:, u, 0:H], rows, None, ALU.mult))
                    link(dve.tensor_tensor(heads(attn[:, u, :], H), b[:, :, 0:8], over(small2[:, u, 0:H], 8), ALU.mult),
                         ring.free((st, "o", u)))

                def softmax_units(st, n_units, keys, after=None):
                    nh = BANK // keys
                    total = NS * n_units
                    for i in range(total):
                        s_ = heads(ring.bank((st, "s", i))[:], nh)
                        dve.wait_ge(*ring.full((st, "s", i)))
                        mx = small[:, i % 2, 32:32 + nh]
                        link(dve.tensor_reduce(mx, s_, X, ALU.max))
                        if i >= NPB:
                            dve.wait_ge(*ring.full((st, "pT", i - NPB)))
                        link(dve.tensor_tensor(heads(probs[:, i % NPB, :], nh), s_, over(mx, keys), ALU.subtract),
                             ring.free((st, "s", i)))
                        if after:
                            after(i)

                dve.wait_ge(S("x_in"), 4 * 16)

                if STAGES_RUN > 0:
                    dve.wait_ge(*weights("L0a"))
                    for u in range(NS):
                        b = ring.bank(("L0a", "qv", u))
                        dve.wait_ge(*ring.full(("L0a", "qv", u)))
                        q3 = heads(b[:, 0:D], H)
                        link(dve.tensor_copy(vaug[:, u, 0, :, 0:8], heads(b[:, D:2 * D], H)), S("L0a_v"))
                        link(dve.tensor_reduce(small[:, u, 0:H], q3, X, ALU.max))
                        link(dve.tensor_tensor(heads(qs[:, u, :], H), q3, over(small[:, u, 0:H], 8), ALU.subtract),
                             ring.free(("L0a", "qv", u)))
                    for u in range(NS):
                        dve.wait_ge(*nth("dve", "L0a_expq"))
                        link(dve.tensor_reduce(small[:, u, 0:H], heads(qs[:, u, :], H), X, ALU.add))
                        link(dve.reciprocal(small2[:, u, 0:H], small[:, u, 0:H]))
                        link(dve.tensor_scalar(small2[:, u, 0:H], small2[:, u, 0:H], DH ** -0.5, None, ALU.mult))
                        link(dve.tensor_tensor(heads(qs[:, u, :], H), heads(qs[:, u, :], H), over(small2[:, u, 0:H], 8),
                                               ALU.mult), S("L0a_qs"))
                        dve.wait_ge(*ring.full(("L0a", "ctx", u)))
                        link(dve.tensor_tensor(ctxbd[:, u], heads(ring.bank(("L0a", "ctx", u))[:, 0:H * 9], H),
                                               over(const("head8"), 9), ALU.mult), ring.free(("L0a", "ctx", u)))
                    for u in range(NS):
                        divide_heads("L0a", u, floor=1e-6, rows=const("late"))
                    post_norm("L0a")

                if STAGES_RUN > 1:
                    b = ring.bank(("L0x", "k"))
                    dve.wait_ge(*ring.full(("L0x", "k")))
                    for u in range(NS):
                        for s_ in range(2):
                            ins = dve.tensor_tensor(bd[:, u, :, s_ * T:(s_ + 1) * T],
                                                    among(b[:, s_ * NT + u * T:s_ * NT + u * T + T], 4),
                                                    over(const("head8in32"), T), ALU.mult)
                            link(ins, ring.free(("L0x", "k")) if u == 1 and s_ == 1 else None)
                    b = ring.bank(("L0x", "v"))
                    dve.wait_ge(*ring.full(("L0x", "v")))
                    for u in range(NS):
                        for s_ in range(2):
                            c = (2 * u + s_) * D
                            last = u == 1 and s_ == 1
                            link(dve.tensor_copy(vaug[:, u, s_, :, 0:8], heads(b[:, c:c + D], H)),
                                 ring.free(("L0x", "v")) if last else None)
                    softmax_units("L0x", 8, 2 * T)
                    for u in range(NS):
                        divide_heads("L0x", u)
                    post_norm("L0x")

                lg, mx, pr, pick = small2[:, :, 0:8], small2[:, :, 8], small2[:, :, 16:24], small2[:, :, 24:32]
                comb = small[:, :, 0:8]

                def gates_in(st, kind):
                    b = ring.bank((st, "logits"))
                    dve.wait_ge(*ring.full((st, "logits")))
                    link(dve.tensor_copy(lg, b[:, 0:16].rearrange("p (u e) -> p u e", u=2)), ring.free((st, "logits")))
                    if kind == "sigmoid":
                        link(dve.tensor_copy(pr, lg), S("gates_in"))
                    else:
                        link(dve.tensor_reduce(mx, lg, X, ALU.max))
                        link(dve.tensor_tensor(pr, lg, over(mx, 8), ALU.subtract), S("gates_in"))

                def gates(st, kind):
                    dve.wait_ge(*nth("dve", "gates_exp"))
                    if kind == "sigmoid":
                        link(dve.tensor_scalar(pr, pr, 1.0, None, ALU.add))
                        link(dve.reciprocal(pr, pr))
                    else:
                        link(dve.tensor_reduce(mx, pr, X, ALU.add))
                        link(dve.reciprocal(mx, mx))
                        link(dve.tensor_tensor(pr, pr, over(mx, 8), ALU.mult))
                    if kind == "softmax":
                        link(dve.tensor_tensor(pick, pr, among(W[st + "_gb"][:], 2), ALU.add))
                    elif kind == "sigmoid":
                        link(dve.tensor_tensor(pick, lg, among(W[st + "_gb"][:], 2), ALU.add))
                    else:
                        link(dve.tensor_copy(pick, pr))
                    for u in range(NS):
                        link(dve.max(small2[:, u, 32:40], small2[:, u, 24:32]))
                        link(dve.tensor_scalar(small2[:, u, 34:40], small2[:, u, 34:40], 0.0, -3e38, ALU.mult, ALU.add))
                        link(dve.match_replace(small2[:, u, 40:48], small2[:, u, 32:40], small2[:, u, 24:32], -2e38))
                    link(dve.tensor_scalar(small2[:, :, 48:56], small2[:, :, 40:48], -2e38, None, ALU.is_equal))
                    link(dve.tensor_tensor(comb, small2[:, :, 48:56], pr, ALU.mult))
                    if kind == "softmax_top":
                        link(dve.tensor_reduce(mx, comb, X, ALU.add))
                        link(dve.reciprocal(mx, mx))
                        link(dve.tensor_tensor(comb, comb, over(mx, 8), ALU.mult))

                def add_expert(st, i, e):
                    b = ring.bank((st, "y", i))
                    dve.wait_ge(*ring.full((st, "y", i)))
                    for u in range(NS):
                        y, r = b[:, u * D:(u + 1) * D], res[:, u, :]
                        ins = (dve.tensor_tensor(r, y, x_tok[:, u, :], ALU.add) if e < 0 else
                               dve.scalar_tensor_tensor(r, y, comb[:, u, e:e + 1], x_tok[:, u, :] if i == 0 else r,
                                                        ALU.mult, ALU.add))
                        link(ins, ring.free((st, "y", i)) if u else None)

                def swiglu(st, kind):
                    dve.wait_ge(*weights(st))
                    gates_in(st, kind)
                    for i in range(18 + 2):
                        if i < 18:
                            if i >= NHB:
                                dve.wait_ge(*ring.full((st, "y", (i - NHB) // 2)))
                            dve.wait_ge(*nth("dve", "gact_ready"))
                            link(dve.tensor_tensor(hT[:, i % NHB, 0:NT], gact[:, i % NHB, 0:NT],
                                                   ring.bank((st, "up", i))[:, NT:2 * NT], ALU.mult),
                                 ring.free((st, "up", i)))
                        if i == 1:
                            gates(st, kind)
                        if i % 2 == 1 and i >= 3:
                            add_expert(st, (i - 3) // 2, (i - 3) // 2 - 1)
                    for u in range(NS):
                        layer_norm(u, x_tok[:, u, :], told=S("x_new"))

                if STAGES_RUN > 2:
                    swiglu("L0f", "softmax")

                if STAGES_RUN > 3:
                    dve.wait_ge(*weights("L1a"))
                    link(dve.tensor_scalar(neg_bb[:], W["L1a_bb"][:], -1.0, None, ALU.mult), S("L1a_negbb"))
                    dve.wait_ge(*ring.freed(("L1a", "beta")))
                    g = gateT
                    link(dve.tensor_scalar(g[:, 1, :], g[:, 0, :], 1.0, None, ALU.add))
                    link(dve.reciprocal(g[:, 1, :], g[:, 1, :]))
                    link(dve.tensor_scalar(g[:, 1, :], g[:, 1, :], 0.8, 0.999, ALU.max, ALU.min))
                    link(dve.memset(g[:, 0, :], 0.0))
                    for u in range(NS):
                        link(dve.tensor_tensor_scan(g[:, 2, tk(u)], g[:, 1, tk(u)], g[:, 0, tk(u)], 1.0,
                                                    ALU.mult, ALU.add))
                    link(dve.reciprocal(g[:, 3, :], g[:, 2, :]), S("L1a_decay"))
                    dve.wait_ge(*ring.full(("L1a", "decay")))
                    iv = [small2[:, u, 16:32] for u in range(NS)]
                    for u in range(NS):
                        link(dve.tensor_copy(iv[u], ring.bank(("L1a", "decay"))[:, u * H:u * H + H]),
                             ring.free(("L1a", "decay")) if u == 1 else None)
                    for u in range(NS):
                        b = ring.bank(("L1a", "qkv", u))
                        dve.wait_ge(*ring.full(("L1a", "qkv", u)))
                        qk = heads(b[:, 0:2 * D], 2 * H)
                        t1 = heads(qk2[:].rearrange("p a d -> p (a d)"), 2 * H)
                        t2 = heads(qk3[:].rearrange("p a d -> p (a d)"), 2 * H)
                        link(dve.tensor_copy(vaug[:, u, 0, :, 0:8], heads(b[:, 2 * D:3 * D], H)))
                        link(dve.tensor_tensor(t1, qk, among(const("cos"), 2 * H), ALU.mult))
                        link(dve.tensor_tensor(t2[:, :, 0:4], qk[:, :, 4:8], among(const("sin")[:, 0:4], 2 * H), ALU.mult))
                        link(dve.tensor_tensor(t2[:, :, 4:8], qk[:, :, 0:4], among(const("sin")[:, 4:8], 2 * H), ALU.mult),
                             ring.free(("L1a", "qkv", u)))
                        link(dve.tensor_tensor(t1, t1, t2, ALU.add))
                        link(dve.tensor_scalar(t2, t1, 0.0, None, ALU.min), S("L1a_min"))
                        dve.wait_ge(*nth("dve", "L1a_exp"))
                        link(dve.scalar_tensor_tensor(t1, t1, 0.0, t2, ALU.max, ALU.add))
                        link(dve.tensor_copy(qs[:, u, :], qk2[:, 0, :]))
                        link(dve.tensor_tensor(heads(ks[:, u, :], H), t1[:, H:2 * H, :], over(iv[u], 8), ALU.mult),
                             S("L1a_qk"))
                    for u in range(NS):
                        dve.wait_ge(*ring.full(("L1a", "qT", u)))
                        link(dve.tensor_tensor(bd[:, u, :, 0:T], among(ring.bank(("L1a", "qT", u))[:, 0:T], 4),
                                               over(const("head8in32"), T), ALU.mult), ring.free(("L1a", "qT", u)))
                    for i in range(8):
                        dve.wait_ge(*ring.full(("L1a", "s", i)))
                        if i >= NPB:
                            k = i - NPB
                            if k == 3:
                                dve.wait_ge(*ring.full(("L1a", "o", 0)))
                            else:
                                dve.wait_ge(*nth("dve", "L1a_used"))
                        link(dve.tensor_tensor(heads(probs[:, i % NPB, :], 4), heads(ring.bank(("L1a", "s", i))[:], 4),
                                               among(const("causal_t"), 4), ALU.mult), ring.free(("L1a", "s", i)))
                    for u in range(NS):
                        b = heads(ring.bank(("L1a", "o", u))[:, 0:H * 9], H)
                        dve.wait_ge(*ring.full(("L1a", "o", u)))
                        den = small[:, u, 0:H]
                        link(dve.scalar_tensor_tensor(den, iv[u], 1e-6, b[:, :, 8], ALU.mult, ALU.add))
                        link(dve.reciprocal(small[:, u, 16:32], den))
                        link(dve.tensor_tensor(heads(attn[:, u, :], H), b[:, :, 0:8], over(small[:, u, 16:32], 8), ALU.mult),
                             ring.free(("L1a", "o", u)))
                    for u in range(NS):
                        dve.wait_ge(*ring.full(("L1a", "y", u)))
                        link(dve.tensor_tensor(res[:, u, :], ring.bank(("L1a", "y", u))[:, 0:D], x_tok[:, u, :], ALU.add),
                             ring.free(("L1a", "y", u)))
                        link(dve.tensor_tensor(attn[:, u, :], res[:, u, :], res[:, u, :], ALU.mult))
                        link(dve.tensor_reduce(mv[:, u, 1:2], attn[:, u, :], X, ALU.add), S("ms_ready"))
                        dve.wait_ge(*nth("dve", "rstd_ready"))
                        link(dve.scalar_tensor_tensor(res[:, u, :], res[:, u, :], rstd[:, u, :], W["L1a_scale"][:],
                                                      ALU.mult, ALU.mult))
                        link(dve.tensor_tensor(res[:, u, :], res[:, u, :], x_tok[:, u, :], ALU.add))
                    for u in range(NS):
                        layer_norm(u, x_tok[:, u, :], told=S("x_new"))

                if STAGES_RUN > 4:
                    for c in range(0, 8, 2):
                        dve.wait_ge(*ring.full(("L1x", f"k{c}")))
                        link(dve.tensor_copy(k64[:, c:c + 2, :], ring.bank(("L1x", f"k{c}"))[:].rearrange("p (c t) -> p c t", c=2)),
                             ring.free(("L1x", f"k{c}")))
                    link(dve.memset(vaug_r[:, :, :, R:R + 1], 1.0))
                    for u in range(NS):
                        for c in range(2):
                            dve.wait_ge(*ring.full(("L1x", "v", u, c)))
                            link(dve.tensor_copy(vaug_r[:, u, 8 * c:8 * c + 8, 0:R], heads(ring.bank(("L1x", "v", u, c))[:], 8)),
                                 ring.free(("L1x", "v", u, c)))

                    def finish_unit(k):
                        u, n = k // 4, k % 4
                        r, c0 = n % 2, 4 * (n // 2)
                        b = heads(ring.bank(("L1x", "o", k))[:, 0:4 * (R + 1)], 4)
                        dve.wait_ge(*ring.full(("L1x", "o", k)))
                        link(dve.reciprocal(small2[:, u, 0:4], b[:, :, R]))
                        link(dve.tensor_tensor(attn64[:, u, c0:c0 + 4, r, :], b[:, :, 0:R], over(small2[:, u, 0:4], R),
                                               ALU.mult), ring.free(("L1x", "o", k)))

                    softmax_units("L1x", 4, T, lambda i: finish_unit(i - 4) if i >= 4 else None)
                    for k in range(4, 8):
                        finish_unit(k)
                    post_norm("L1x")

                if STAGES_RUN > 5:
                    gates_in("L1f", "softmax_top")
                    gates("L1f", "softmax_top")
                    for e in range(E):
                        add_expert("L1f", e, e)
                    for u in range(NS):
                        layer_norm(u, x_tok[:, u, :], told=S("x_new"))

                if STAGES_RUN > 6:
                    dve.wait_ge(*weights("L2a"))
                    b = ring.bank(("L2a", "v"))
                    dve.wait_ge(*ring.full(("L2a", "v")))
                    for u in range(NS):
                        link(dve.tensor_copy(vaug[:, u, 0, :, 0:8], heads(b[:, u * D:(u + 1) * D], H)),
                             ring.free(("L2a", "v")) if u else None)
                    for i, key in enumerate([("L2a", "kf", 0), ("L2a", "kf", 1), ("L2a", "qf", 0), ("L2a", "qf", 2)]):
                        b = ring.bank(key)
                        dve.wait_ge(*ring.full(key))
                        link(dve.tensor_scalar(gact[:, i, :], b[:], 0.0, None, ALU.min), S("L2a_min"))
                        dst = probs[:, i, :] if i < 2 else feats_q[:, 2 * (i - 2):2 * (i - 2) + 2, :].rearrange("p c t -> p (c t)")
                        dve.wait_ge(*nth("dve", "L2a_exp"))
                        link(dve.scalar_tensor_tensor(dst, b[:], 0.0, gact[:, i, :], ALU.max, ALU.add), ring.free(key))
                    for u in range(NS):
                        dve.wait_ge(*ring.full(("L2a", "kv", u)))
                        m = const("feat32").unsqueeze(1).unsqueeze(3).to_broadcast([P, 4, 4, 9])
                        link(dve.tensor_tensor(ctxbd[:, u].rearrange("p (c j) d -> p c j d", c=4),
                                               ring.bank(("L2a", "kv", u))[:, 0:144].rearrange("p (c j d) -> p c j d", c=4, j=4),
                                               m, ALU.mult), ring.free(("L2a", "kv", u)))
                    for u in range(NS):
                        divide_heads("L2a", u, add=1e-8)
                    aff = (W["L2a_gamma"][:], W["L2a_beta"][:])
                    for u in range(NS):
                        dve.wait_ge(*ring.full(("L2a", "y", u)))
                        link(dve.tensor_tensor(res[:, u, :], ring.bank(("L2a", "y", u))[:, 0:D], x_tok[:, u, :], ALU.add),
                             ring.free(("L2a", "y", u)))
                    for u in range(NS):
                        layer_norm(u, qs[:, u, :], aff, S("L2a_x1"))
                    for u in range(NS):
                        dve.wait_ge(*ring.full(("L2a", "y2", u)))
                        link(dve.tensor_tensor(res[:, u, :], ring.bank(("L2a", "y2", u))[:, 0:D], qs[:, u, :], ALU.add),
                             ring.free(("L2a", "y2", u)))
                    for u in range(NS):
                        layer_norm(u, qs[:, u, :], aff)
                        link(dve.tensor_tensor(res[:, u, :], qs[:, u, :], x_tok[:, u, :], ALU.add))
                    for u in range(NS):
                        layer_norm(u, x_tok[:, u, :], told=S("x_new"))

                if STAGES_RUN > 7:
                    dve.wait_ge(*weights("L2x"))
                    link(dve.tensor_tensor(bq4[:], const("feat32"), W["L2x_bq"][:].to_broadcast([P, 4]), ALU.mult),
                         S("L2x_bias"))
                    b = ring.bank(("L2x", "k"))
                    dve.wait_ge(*ring.full(("L2x", "k")))
                    for u in range(NS):
                        ins = dve.scalar_tensor_tensor(bd[:, u, :, 0:T], among(b[:, tk(u)], 4), W["L2x_bk"][:],
                                                       over(const("head8in32"), T), ALU.add, ALU.mult)
                        link(ins, ring.free(("L2x", "k")) if u else None)
                    b = ring.bank(("L2x", "v"))
                    dve.wait_ge(*ring.full(("L2x", "v")))
                    for u in range(NS):
                        link(dve.tensor_copy(vaug[:, u, 0, :, 0:8], heads(b[:, u * D:(u + 1) * D], H)),
                             ring.free(("L2x", "v")) if u else None)
                    softmax_units("L2x", 4, T)
                    for u in range(NS):
                        divide_heads("L2x", u)
                    post_norm("L2x")

                if STAGES_RUN > 8:
                    swiglu("L2f", "sigmoid")

                if STAGES_RUN > 9:
                    dve.wait_ge(*weights("L3a"))
                    for r in range(2):
                        link(dve.memset(lat_pad[64 - 64 * r:128 - 64 * r, r, :], 0.0), S("L3a_zeros") if r else None)
                    b = ring.bank(("L3a", "v"))
                    dve.wait_ge(*ring.full(("L3a", "v")))
                    for u in range(NS):
                        link(dve.tensor_copy(vaug[:, u, 0, :, 0:8], heads(b[:, u * D:(u + 1) * D], H)),
                             ring.free(("L3a", "v")) if u else None)
                    softmax_units("L3a", 4, T)
                    for u in range(NS):
                        divide_heads("L3a", u)
                    post_norm("L3a")

                if STAGES_RUN > 10:
                    dve.wait_ge(*weights("L3x"))
                    g = gateT
                    b = ring.bank(("L3x", "gates"))
                    dve.wait_ge(*ring.full(("L3x", "gates")))
                    link(dve.tensor_scalar(g[0:8, 0, :], b[0:8, 0:NT], W["L3x_ib"][:], None, ALU.add))
                    link(dve.tensor_scalar(g[0:8, 1, :], b[0:8, NT:2 * NT], W["L3x_fb"][:], None, ALU.add),
                         ring.free(("L3x", "gates")))
                    link(dve.scalar_tensor_tensor(g[0:8, 5, :], g[0:8, 1, :], -1.0, g[0:8, 1, :], ALU.mult, ALU.min),
                         S("L3x_absf"))
                    dve.wait_ge(*nth("dve", "L3x_softplus"))
                    link(dve.scalar_tensor_tensor(g[0:8, 1, :], g[0:8, 1, :], 0.0, g[0:8, 5, :], ALU.min, ALU.subtract))
                    ones8 = const("ones", 8)[:, 0:T]
                    for u in range(NS):
                        link(dve.tensor_tensor_scan(g[0:8, 3, tk(u)], ones8, g[0:8, 1, tk(u)], 0.0, ALU.mult, ALU.add))
                    link(dve.tensor_tensor(g[0:8, 2, :], g[0:8, 0, :], g[0:8, 3, :], ALU.subtract))
                    for u in range(NS):
                        link(dve.tensor_tensor_scan(g[0:8, 5, tk(u)], ones8, g[0:8, 2, tk(u)], -3.0e38, ALU.mult, ALU.max))
                    link(dve.tensor_tensor(g[0:8, 4, :], g[0:8, 3, :], g[0:8, 5, :], ALU.add), S("L3x_gates"))
                    for u in range(NS):
                        link(dve.scalar_tensor_tensor(mdiag[:, u], among(g[0:8, 5, tk(u)], 8), -1.0,
                                                      over(const("delta8", 8), T), ALU.mult, ALU.mult))
                        link(dve.tensor_tensor(bd[:, u, :, 0:T], among(xT[:, tk(u)], 4),
                                               over(const("head16in64"), T), ALU.mult), S("L3x_bd"))
                        link(dve.tensor_copy(vaug_c[:, u, :, 0:DC], heads(ctx_tok[:, u, :], HC)))
                    for i in range(4):
                        dve.wait_ge(*ring.full(("L3x", "s", i)))
                        dve.wait_ge(*ring.freed(("L3x", "D", i)))
                        if i >= NPB:
                            dve.wait_ge(*nth("dve", "L3x_used"))
                        link(dve.scalar_tensor_tensor(probsT[:, i % NPB, :], ring.bank(("L3x", "s", i))[:], DC ** -0.5,
                                                      probs[:, i % NPB, :], ALU.mult, ALU.mult), ring.free(("L3x", "s", i)))
                    dve.wait_ge(*ring.freed(("L3x", "mx")))
                    for u in range(NS):
                        b = heads(ring.bank(("L3x", "o", u))[:, 0:HC * 17], HC)
                        dve.wait_ge(*ring.full(("L3x", "o", u)))
                        n = small[:, u, 0:8]
                        link(dve.tensor_copy(n, b[:, :, DC]))
                        link(dve.scalar_tensor_tensor(n, n, -1.0, n, ALU.mult, ALU.max))
                        link(dve.tensor_tensor(n, n, small2[:, u, 32:40], ALU.max))
                        link(dve.tensor_scalar(n, n, 1e-6, None, ALU.add))
                        link(dve.reciprocal(n, n))
                        h3 = heads(attn[:, u, :], HC)
                        link(dve.tensor_tensor(h3, b[:, :, 0:DC], over(n, DC), ALU.mult), ring.free(("L3x", "o", u)))
                        m = small[:, u, 8:16]
                        link(dve.tensor_reduce(m, h3, X, ALU.add))
                        link(dve.tensor_scalar(m, m, 1.0 / DC, None, ALU.mult))
                        link(dve.tensor_tensor(h3, h3, over(m, DC), ALU.subtract))
                        link(dve.tensor_tensor(qs[:, u, :], attn[:, u, :], attn[:, u, :], ALU.mult))
                        link(dve.tensor_reduce(small[:, u, 16:24], heads(qs[:, u, :], HC), X, ALU.add), S("L3x_var"))
                        dve.wait_ge(*nth("dve", "L3x_rstd"))
                        link(dve.tensor_tensor(h3, h3, over(small[:, u, 24:32], DC), ALU.mult))
                        link(dve.tensor_tensor(attn[:, u, :], attn[:, u, :], W["L3x_w"][:], ALU.mult))
                        link(dve.tensor_tensor(res[:, u, :], attn[:, u, :], x_tok[:, u, :], ALU.add))
                    for u in range(NS):
                        layer_norm(u, x_tok[:, u, :], told=S("x_new"))

                link(dve.tensor_copy(x_all[:, bass.ds(pair * NS, NS), :], x_tok[:]))

            @block.scalar
            def _(eng):
                link = Order(act, "act").link
                eps5, eps6, one, _z = (const("eps")[:, i:i + 1] for i in range(4))

                def inv_sqrt(dst, src, tmp, eps, scale=1.0, told=None):
                    link(act.activation(tmp, src, ACT.Ln, bias=eps[0:src.shape[0]], scale=scale))
                    link(act.activation(dst, tmp, ACT.Exp, scale=-0.5), told)

                def norm_rstd(n=NS):
                    for u in range(n):
                        act.wait_ge(*nth("act", "var_ready"))
                        inv_sqrt(rstd[:, u, :], mv[:, u, 1:2], lnv[:, u, :], eps5, told=S("rstd_ready"))

                def keep_xT(st):
                    for u in range(NS):
                        act.wait_ge(*ring.full(("xT", st, u)))
                        link(act.copy(xT[:, tk(u)], ring.bank(("xT", st, u))[:, 0:T]), ring.free(("xT", st, u)))

                def attnT_copy(st):
                    for u in range(NS):
                        act.wait_ge(*ring.full((st, "aT", u)))
                        link(act.copy(attnT[:, u, :], ring.bank((st, "aT", u))[:, 0:T]), ring.free((st, "aT", u)))

                def softmax_units(st, n_units, scale):
                    total = NS * n_units
                    for step in range(total + 2):
                        if step < total:
                            i = step
                            act.wait_ge(*ring.freed((st, "s", i)))
                            link(act.activation(probs[:, i % NPB, :], probs[:, i % NPB, :], ACT.Exp, scale=scale),
                                 S("probs_ready"))
                        i = step - 2
                        if 0 <= i < total:
                            act.wait_ge(*ring.full((st, "pT", i)))
                            link(act.copy(probsT[:, i % NPB, :], ring.bank((st, "pT", i))[:]), ring.free((st, "pT", i)))

                def to_sbuf(key, dst, bias=None, shape=None):
                    src = ring.bank(key)[:]
                    act.wait_ge(*ring.full(key))
                    src = src[:, 0:NT] if shape is None else shape(src)
                    if bias is None:
                        link(act.copy(dst, src), ring.free(key))
                    else:
                        link(act.activation(dst, src, ACT.Identity, bias=bias), ring.free(key))

                def to_pad4(key, tokens, n, bias=None):
                    act.wait_ge(*ring.full(key))
                    for c in range(4):
                        ins = act.activation(pad4[:, c, tokens], ring.bank(key)[:, 0:n], ACT.Identity,
                                             scale=const("feat32")[:, c:c + 1],
                                             **({} if bias is None else {"bias": bias[:, c:c + 1]}))
                        link(ins, ring.free(key) if c == 3 else None)

                act.preload_act_table_set(EXP_LN)
                act.wait_ge(*weights("L0a"))
                for name, dst in (("x_tok", x_tok), ("xT", xT), ("ctx_tok", ctx_tok), ("ctxT", ctxT)):
                    act.dma_start(dst[:], dram[name][pair]).then_inc(S("x_in"), 16)

                if STAGES_RUN > 0:
                    for u in range(NS):
                        act.wait_ge(*ring.full(("L0a", "k", u)))
                        link(act.activation(ks[:, u, :], ring.bank(("L0a", "k", u))[:, 0:D], ACT.Exp),
                             ring.free(("L0a", "k", u)))
                        act.wait_ge(*ring.freed(("L0a", "qv", u)))
                        link(act.activation(qs[:, u, :], qs[:, u, :], ACT.Exp), S("L0a_expq"))
                    for u in range(NS):
                        to_sbuf(("L0a", "qsT", u), qT[:, 0, tk(u)], shape=lambda s: s[:, 0:T])
                    attnT_copy("L0a")
                    norm_rstd()
                    keep_xT(0)
                if STAGES_RUN > 1:
                    to_pad4(("L0x", "q"), slice(0, NT), NT)
                    softmax_units("L0x", 8, DH ** -0.5)
                    attnT_copy("L0x")
                    norm_rstd()
                    keep_xT(1)

                def gates_exp(scale):
                    act.wait_ge(*nth("act", "gates_in"))
                    pr = small2[:, :, 16:24]
                    link(act.activation(pr, pr, ACT.Exp, scale=scale), S("gates_exp"))

                def swiglu(st, scale):
                    gates_exp(scale)
                    for i in range(18):
                        act.wait_ge(*ring.full((st, "up", i)))
                        if i >= NHB:
                            act.wait_ge(*ring.freed((st, "up", i - NHB)))
                        link(act.activation(gact[:, i % NHB, 0:NT], ring.bank((st, "up", i))[:, 0:NT], ACT.Silu),
                             S("gact_ready"))
                    act.preload_act_table_set(EXP_LN)
                    norm_rstd()

                if STAGES_RUN > 2:
                    swiglu("L0f", 1.0)
                    keep_xT(2)

                if STAGES_RUN > 3:
                    act.wait_ge(*nth("act", "L1a_negbb"))
                    act.wait_ge(*ring.full(("L1a", "beta")))
                    link(act.activation(gateT[0:H, 0, :], ring.bank(("L1a", "beta"))[0:H, 0:NT], ACT.Exp,
                                        bias=neg_bb[:], scale=-1.0), ring.free(("L1a", "beta")))
                    for u in range(NS):
                        act.wait_ge(*nth("act", "L1a_min"))
                        link(act.activation(qk3[:], qk3[:], ACT.Exp), S("L1a_exp"))
                    for u in range(NS):
                        to_pad4(("L1a", "kT", u), tk(u), T)
                    attnT_copy("L1a")
                    for u in range(NS):
                        act.wait_ge(*nth("act", "ms_ready"))
                        inv_sqrt(rstd[:, u, :], mv[:, u, 1:2], lnv[:, u, :], eps6, scale=1.0 / D, told=S("rstd_ready"))
                    norm_rstd()
                    keep_xT(3)

                if STAGES_RUN > 4:
                    for c in range(0, 8, 2):
                        to_sbuf(("L1x", f"q{c}"), q64[:, c:c + 2, :], shape=lambda s: heads(s, 2))
                    softmax_units("L1x", 4, R ** -0.5)
                    for u in range(NS):
                        for c in range(0, 8, 4):
                            to_sbuf(("L1x", "aT", u, c), attn64T[:, u, c:c + 4, :], shape=lambda s: heads(s, 4))
                    norm_rstd()
                    keep_xT(4)

                if STAGES_RUN > 5:
                    gates_exp(1.0)
                    for i in range(16):
                        act.wait_ge(*ring.full(("L1f", "up", i)))
                        if i >= NHB:
                            act.wait_ge(*ring.full(("L1f", "y", (i - NHB) // 2)))
                        link(act.activation(hT[:, i % NHB, :], ring.bank(("L1f", "up", i))[:], ACT.Gelu_apprx_tanh),
                             ring.free(("L1f", "up", i)))
                    act.preload_act_table_set(EXP_LN)
                    norm_rstd()
                    keep_xT(5)

                if STAGES_RUN > 6:
                    to_sbuf(("L2a", "qk"), qT[:], shape=lambda s: heads(s, 2))
                    for i in range(4):
                        act.wait_ge(*nth("act", "L2a_min"))
                        link(act.activation(gact[:, i, :], gact[:, i, :], ACT.Exp), S("L2a_exp"))
                    attnT_copy("L2a")
                    norm_rstd()
                    for u in range(NS):
                        to_sbuf(("L2a", "x1T", u), kT[:, tk(u)], shape=lambda s: s[:, 0:T])
                    for c in range(4):
                        key = ("L2a", f"h{c // 2 * 2}")
                        act.wait_ge(*ring.full(key))
                        half = slice((c % 2) * NT, (c % 2 + 1) * NT)
                        ins = act.activation(gact[:, c // 2, half], ring.bank(key)[:, half], ACT.Gelu,
                                             bias=W["L2a_b1"][:, c:c + 1])
                        link(ins, ring.free(key) if c % 2 else None)
                    act.preload_act_table_set(EXP_LN)
                    norm_rstd()
                    norm_rstd()
                    keep_xT(6)

                if STAGES_RUN > 7:
                    act.wait_ge(*nth("act", "L2x_bias"))
                    to_pad4(("L2x", "q"), slice(0, NT), NT, bias=bq4)
                    softmax_units("L2x", 4, DH ** -0.5)
                    attnT_copy("L2x")
                    norm_rstd()
                    keep_xT(7)

                if STAGES_RUN > 8:
                    swiglu("L2f", -1.0)
                    keep_xT(8)

                if STAGES_RUN > 9:
                    act.wait_ge(*nth("act", "L3a_zeros"))
                    act.wait_ge(*ring.full(("L3a", "lat")))
                    for r in range(2):
                        rows = slice(64 * r, 64 * r + 64)
                        link(act.copy(lat_pad[rows, r, :], ring.bank(("L3a", "lat"))[rows, 0:NT]),
                             ring.free(("L3a", "lat")) if r else None)
                    for c in range(0, 8, 2):
                        to_sbuf(("L3a", f"q{c}"), q64[:, c:c + 2, :], shape=lambda s: heads(s, 2))
                    softmax_units("L3a", 4, R ** -0.5)
                    attnT_copy("L3a")
                    norm_rstd()
                    keep_xT(9)

                if STAGES_RUN > 10:
                    act.wait_ge(*nth("act", "L3x_absf"))
                    link(act.activation(gateT[0:8, 5, :], gateT[0:8, 5, :], ACT.Exp))
                    link(act.activation(gateT[0:8, 5, :], gateT[0:8, 5, :], ACT.Ln, bias=one[0:8]), S("L3x_softplus"))
                    act.wait_ge(*ring.full(("L3x", "mx")))
                    link(act.activation(small2[:, :, 32:40], ring.bank(("L3x", "mx"))[:, 0:16].rearrange("p (u h) -> p u h", u=2),
                                        ACT.Exp, scale=-1.0))
                    link(act.copy(a_tok[:], ring.bank(("L3x", "mx"))[:, 16:32].rearrange("p (u h) -> p u h", u=2)),
                         ring.free(("L3x", "mx")))
                    for i in range(4):
                        act.wait_ge(*ring.full(("L3x", "D", i)))
                        if i >= NPB:
                            act.wait_ge(*ring.freed(("L3x", "s", i - NPB)))
                        for j in range(4):
                            cols = slice(j * T, j * T + T)
                            ins = act.activation(probs[:, i % NPB, cols], ring.bank(("L3x", "D", i))[:, cols], ACT.Exp,
                                                 bias=a_tok[:, i // 2, 4 * (i % 2) + j:4 * (i % 2) + j + 1])
                            link(ins, ring.free(("L3x", "D", i)) if j == 3 else None)
                    for u in range(NS):
                        act.wait_ge(*nth("act", "L3x_var"))
                        inv_sqrt(small[:, u, 24:32], small[:, u, 16:24], small[:, u, 32:40], eps6, scale=1.0 / DC,
                                 told=S("L3x_rstd"))
                    norm_rstd()
                    keep_xT(10)
                link(act.copy(xT_all[:, bass.ds(pair * NT, NT)], xT[:]))

            @block.sync
            def _(eng):
                if STAGES_RUN > 8:
                    for done, st in (("L0f", "L2f"), ("L2f", "L0f")):
                        sp.wait_ge(*ring.full((done, "y", 8)))
                        for n in ("_w1", "_w3", "_w2"):
                            sp.dma_start(W[st + n][:], dram[st + n]).then_inc(S(st + "_in"), 16)
                    sp.wait_ge(S("L0f_in"), 3 * 16)

        with nc.Block(name="reset") as block:
            @block.sync
            def _(eng):
                nums = sorted(s.num for s in sems.values())
                assert nums == list(range(nums[0], nums[-1] + 1))
                sp.sem_clear(range(nums[0], nums[-1] + 1))

    amax = sb("amax", [P, 4])
    q_in = k64[:, 0:4, :].rearrange("p c t -> p (c t)")
    q_bf = sb("q_bf", [P, B * T], BF16)
    w_bf = sb("w_bf", [P, D], BF16)
    y_all = q64[:, 0:4, :].rearrange("p c t -> p (c t)").rearrange("p (b d) -> p b d", b=B)
    stats8 = sb("stats8", [P, B, 6])
    mv8 = sb("mv8", [P, B, 2])
    rstd8 = sb("rstd8", [P, B])
    fin = {n: ctx.enter_context(nc.semaphore(f"ffn_{n}")) for n in
           ("partial", "turned", "whole", "spread", "operands", "products", "var", "rstd", "normed")}
    fin_step = ctx.enter_context(nc.semaphore("ffn_dve_step"))
    fin_act = ctx.enter_context(nc.semaphore("ffn_act_step"))
    ROUND = float(1.5 * 2 ** 23)

    with nc.Block(name="last_ffn") as block:
        @block.tensor
        def _(eng):
            pe.wait_ge(fin["partial"], 2)
            pe.matmul(psum[1][:, 0:1], const("ones")[:, 0:P], amax[:, 1:2], start=True, stop=True)
            pe.transpose(psum[0][0:1, 0:P], amax[:, 0:1], IDENT).then_inc(fin["turned"], 1)
            pe.wait_ge(fin["whole"], 1)
            pe.matmul(psum[2][:, 0:1], ones_row, amax[0:1, 2:3], start=True, stop=True).then_inc(fin["spread"], 1)
            pe.wait_ge(fin["operands"], 1)
            for b in range(B):
                m = pe.matmul(psum[3 + b // 4][:, b % 4 * D:b % 4 * D + D], q_bf[:, b * T:(b + 1) * T], w_bf[:],
                              start=True, stop=True)
                if b % 4 == 3:
                    m.then_inc(fin["products"], 1)

        @block.vector
        def _(eng):
            link = Order(dve, "ffn").link
            st = fin_step
            dve.wait_ge(*weights("L3f"))
            link(dve.tensor_reduce(amax[:, 0:1], xT_all[:], X, ALU.max, apply_absolute_value=True), fin["partial"])
            link(dve.tensor_reduce(amax[:, 1:2], W["L3f_w"][:], X, ALU.add, apply_absolute_value=True), fin["partial"])
            link(dve.tensor_tensor(x_all[:], x_all[:], among(W["L3f_b"][:], B), ALU.add), st)
            dve.wait_ge(fin["turned"], 1)
            link(dve.tensor_reduce(amax[0:1, 2:3], psum[0][0:1, 0:P], X, ALU.max), fin["whole"])
            dve.wait_ge(fin["spread"], 1)
            s = small[:, 0, :]
            link(dve.tensor_scalar(s[:, 0:1], psum[2][:, 0:1], 1.0 / 127.0, None, ALU.mult), st)
            link(dve.reciprocal(s[:, 1:2], s[:, 0:1]), st)
            link(dve.tensor_scalar(s[:, 2:3], psum[1][:, 0:1], 1.0 / (D * D), None, ALU.mult), st)
            link(dve.tensor_scalar(s[:, 3:4], s[:, 2:3], 0.5, None, ALU.mult), st)
            link(dve.tensor_scalar(s[:, 4:5], s[:, 2:3], -0.5, None, ALU.mult), st)
            link(dve.tensor_tensor(s[:, 5:6], s[:, 2:3], s[:, 0:1], ALU.mult), st)
            link(dve.tensor_scalar(qs[:, 0, :], W["L3f_w"][:], s[:, 3:4], None, ALU.is_gt), st)
            link(dve.tensor_scalar(qs[:, 1, :], W["L3f_w"][:], s[:, 4:5], None, ALU.is_lt), st)
            link(dve.tensor_tensor(w_bf[:], qs[:, 0, :], qs[:, 1, :], ALU.subtract), st)
            link(dve.tensor_scalar(q_in, xT_all[:], s[:, 1:2], ROUND, ALU.mult, ALU.add), st)
            link(dve.tensor_scalar(q_in, q_in, ROUND, 127.0, ALU.subtract, ALU.min), st)
            link(dve.tensor_scalar(q_bf[:], q_in, -128.0, None, ALU.max), fin["operands"])
            for g in range(2):
                dve.wait_ge(fin["products"], g + 1)
                xs = x_all[:, 4 * g:4 * g + 4, :].rearrange("p b d -> p (b d)")
                link(dve.scalar_tensor_tensor(xs, psum[3 + g][:], s[:, 5:6], xs, ALU.mult, ALU.add), st)
            for b in range(B):
                link(dve.bn_stats(stats8[:, b, :], x_all[:, b, :]), st)
                link(dve.bn_aggr(mv8[:, b, :], stats8[:, b, :]), fin["var"])
            dve.wait_ge(fin["rstd"], 1)
            for b in range(B):
                link(dve.tensor_scalar(y_all[:, b, :], x_all[:, b, :], mv8[:, b, 0:1], rstd8[:, b:b + 1],
                                       ALU.subtract, ALU.mult), fin["normed"])

        @block.scalar
        def _(eng):
            act.preload_act_table_set(EXP_LN)
            act.wait_ge(fin["var"], B)
            act.activation(rstd8[:], mv8[:, :, 1], ACT.Ln, bias=const("eps")[:, 0:1]).then_inc(fin_act, 1)
            act.wait_ge(fin_act, 1)
            act.activation(rstd8[:], rstd8[:], ACT.Exp, scale=-0.5).then_inc(fin["rstd"], 1)

        @block.sync
        def _(eng):
            for prefix in w_in:
                sp.wait_ge(*weights(prefix))
            sp.wait_ge(fin["normed"], B)
            sp.dma_start(out.rearrange("b t d -> t b d"), y_all).then_inc(stored, 16)
            sp.wait_ge(stored, 16)


def layouts(i):
    def rows(v):
        return np.broadcast_to(v.reshape(1, -1), (P, v.size))

    def chunks(w):
        return w.reshape(-1, P, w.shape[-1]).transpose(1, 0, 2).reshape(P, -1)

    def experts_in(*w):
        return np.concatenate(w, axis=0).transpose(1, 0, 2).reshape(P, -1)

    def experts_out(*w):
        w = np.concatenate(w, axis=0)
        return chunks(w.reshape(-1, D))

    proj = np.zeros((H, DH, H, 32), np.float32)
    proj[np.arange(H), :, np.arange(H), :] = i["L2_attn_proj"]
    g = np.stack([i["L3_xattn_igate_kernel"], i["L3_xattn_fgate_kernel"]], axis=1)
    t = np.swapaxes
    return {
        "consts": shape_constants(),
        "L0a_qkv": i["L0_attn_W_qkv"].T, "L0a_o": i["L0_attn_W_out"].T,
        "L0x_q": i["L0_xattn_Wq"], "L0x_kv": i["L0_xattn_Wkv"], "L0x_o": i["L0_xattn_Wout"],
        "L0x_bo": i["L0_xattn_bout"][None],
        "L0f_gate": i["L0_ffn_gate_w"].T, "L0f_gb": rows(i["L0_ffn_gate_bias"]),
        "L0f_w1": experts_in(i["L0_ffn_sw1"].T[None], t(i["L0_ffn_w1"], 1, 2)),
        "L0f_w3": experts_in(i["L0_ffn_sw3"].T[None], t(i["L0_ffn_w3"], 1, 2)),
        "L0f_w2": experts_out(i["L0_ffn_sw2"].T[None], t(i["L0_ffn_w2"], 1, 2)),
        "L1a_qkv": np.concatenate([i["L1_attn_Wq"].T, i["L1_attn_Wk"].T, i["L1_attn_Wv"].T], axis=1),
        "L1a_b": i["L1_attn_Wb"].T, "L1a_bb": i["L1_attn_bb"][:, None], "L1a_o": i["L1_attn_Wo"].T,
        "L1a_bo": i["L1_attn_bo"][None], "L1a_scale": rows(i["L1_attn_scale"]),
        "L1x_q": i["L1_xattn_w_q"], "L1x_kv": i["L1_xattn_w_kv"], "L1x_o": chunks(i["L1_xattn_w_out"]),
        "L1x_bo": i["L1_xattn_b_out"][None],
        "L1f_gate": i["L1_ffn_gate_w"], "L1f_w1": experts_in(i["L1_ffn_w1"]), "L1f_w2": experts_out(i["L1_ffn_w2"]),
        "L2a_qkv": i["L2_attn_w_qkv"].T, "L2a_proj": proj.reshape(P, H * 32), "L2a_o": i["L2_attn_w_out"].T,
        "L2a_bo": i["L2_attn_b_out"][None], "L2a_gamma": rows(i["L2_attn_gamma"]), "L2a_beta": rows(i["L2_attn_beta"]),
        "L2a_w1": i["L2_attn_w1"].T, "L2a_b1": i["L2_attn_b1"].reshape(4, P).T, "L2a_w2": chunks(i["L2_attn_w2"].T),
        "L2a_b2": i["L2_attn_b2"][None],
        "L2x_q": i["L2_xattn_Wq"], "L2x_k": i["L2_xattn_Wk"], "L2x_v": i["L2_xattn_Wv"], "L2x_o": i["L2_xattn_Wo"],
        "L2x_bq": i["L2_xattn_bq"][:, None], "L2x_bk": i["L2_xattn_bk"][:, None], "L2x_bv": i["L2_xattn_bv"][None],
        "L2x_bo": i["L2_xattn_bo"][None],
        "L2f_gate": i["L2_ffn_gate_w"].T, "L2f_gb": rows(i["L2_ffn_beta"]),
        "L2f_w1": experts_in(i["L2_ffn_shared_gate_w"], i["L2_ffn_gate_proj_w"]),
        "L2f_w3": experts_in(i["L2_ffn_shared_up_w"], i["L2_ffn_up_proj_w"]),
        "L2f_w2": experts_out(i["L2_ffn_shared_down_w"], i["L2_ffn_down_proj_w"]),
        "L3a_basis": np.concatenate([i["L3_attn_basis_w"].T] * 2, axis=1), "L3m_core": i["L3_attn_core"],
        "L3m_coreT": i["L3_attn_core"].T, "L3m_mats": i["L3_attn_head_residual"].transpose(1, 0, 2).reshape(R, H * R),
        "L3a_v": i["L3_attn_v_w"].T, "L3a_vb": i["L3_attn_v_b"][None], "L3a_o": i["L3_attn_o_w"].T,
        "L3a_bo": i["L3_attn_o_b"][None],
        "L3x_gates": chunks(g.reshape(3 * P, 16)), "L3x_ib": i["L3_xattn_igate_bias"][:, None],
        "L3x_fb": i["L3_xattn_fgate_bias"][:, None], "L3x_w": rows(i["L3_xattn_outnorm_weight"]),
        "L3f_w": i["L3_ffn_weight"].T, "L3f_b": rows(i["L3_ffn_bias"]),
    }


def kernel(**inputs):
    import concourse.bacc as bacc
    from concourse.bass_utils import run_bass_kernel_spmd

    i = {n: np.asarray(v) for n, v in inputs.items()}
    arrays = {n: np.ascontiguousarray(v) for n, v in layouts(i).items()}
    for n, v in (("x", i["x"]), ("ctx", i["ctx_1024"])):
        pairs = v.reshape(B // NS, NS, T, D)
        arrays[f"{n}_tok"] = np.ascontiguousarray(pairs.transpose(0, 2, 1, 3))
        arrays[f"{n}T"] = np.ascontiguousarray(pairs.transpose(0, 3, 1, 2).reshape(B // NS, D, NT))
    for n, p, w in WEIGHTS:
        assert arrays[n].shape == (p, w) and arrays[n].dtype == np.float32, (n, arrays[n].shape)

    nc = bacc.Bacc("TRN2", target_bir_lowering=False, num_devices=1)
    arrays = {f"in_{n}": a for n, a in arrays.items()}
    dram = {n[3:]: nc.dram_tensor(n, a.shape, F32, kind="ExternalInput").ap() for n, a in arrays.items()}
    out = nc.dram_tensor("y", (B, T, D), F32, kind="ExternalOutput").ap()
    build(nc, dram, out)
    r = run_bass_kernel_spmd(nc, [arrays], core_ids=[0])
    return r.results[0]["y"]
```

```python
from contextlib import ExitStack

import numpy as np

import concourse.bass as bass
from concourse import mybir

F32 = mybir.dt.float32
BF16 = mybir.dt.bfloat16
ACT = mybir.ActivationFunctionType
ALU = mybir.AluOpType
X = mybir.AxisListType.X

P = 128
T = 128
D = 128
B = 8
NS = 2
NT = NS * T
H = 16
DH = D // H
HC = 8
DC = D // HC
R = 64
E = 8
BANK = 512
EXP_LN = "natural_log_exp_and_others"
NEG = -float(2 ** 100)
LN_EPS = 1e-5
STAGES = 12
WARM_X, WARM_A, WARM_Y = (8, 1), (4, 1), (3, 0)
WARM_UNIT = {"L0x": 0, "L1x": 2, "L2x": 0, "L3a": 1}
WARM_DECAY, WARM_RMS, WARM_Q, WARM_K = 2, 6, 3, 4

CONST = {}
_at = 0
for _n, _w in [("ident", 128), ("neg_causal", 128), ("neg_causal_t", 128), ("causal_t", 128),
               ("head8", 16), ("head8in32", 4), ("head16in64", 4), ("feat32", 4), ("late", 1),
               ("cos", 8), ("sin", 8), ("delta8", 8), ("ones", 128), ("eps", 4)]:
    CONST[_n] = (_at, _w)
    _at += _w
NCONST = _at


def shape_constants():
    c = np.zeros((P, NCONST), np.float32)
    p = np.arange(P)

    def put(name, v):
        a, w = CONST[name]
        c[:v.shape[0], a:a + w] = v.reshape(v.shape[0], w)

    put("ident", np.eye(P, dtype=np.float32))
    put("neg_causal", np.where(p[None, :] > p[:, None], NEG, 0).astype(np.float32))
    put("neg_causal_t", np.where(p[:, None] > p[None, :], NEG, 0).astype(np.float32))
    put("causal_t", (p[:, None] <= p[None, :]).astype(np.float32))
    put("head8", (p[:, None] // 8 == np.arange(16)).astype(np.float32))
    put("head8in32", (p[:, None] % 32 // 8 == np.arange(4)).astype(np.float32))
    put("head16in64", (p[:, None] % 64 // 16 == np.arange(4)).astype(np.float32))
    put("feat32", (p[:, None] // 32 == np.arange(4)).astype(np.float32))
    put("late", (p[:, None] >= 64).astype(np.float32))
    inv = np.float32(1.0) / np.float32(10000.0) ** (np.arange(0, 8, 2, dtype=np.float32) / np.float32(8))
    ang = np.concatenate([p.astype(np.float32)[:, None] * inv[None, :]] * 2, axis=1)
    sin = np.sin(ang)
    sin[:, :4] *= -1
    put("cos", np.cos(ang))
    put("sin", sin)
    put("delta8", np.eye(8, dtype=np.float32))
    put("ones", np.ones((P, 128), np.float32))
    put("eps", np.tile(np.array([1e-5, 1e-6, 1.0, 0.0], np.float32), (P, 1)))
    return c


WEIGHTS = [
    ("con_sts", P, NCONST), ("L3m_core", R, 64), ("L3m_coreT", R, 64), ("L3m_mats", R, 1024),
    ("L0a_qkv", P, 384), ("L0a_o", P, 128),
    ("L0x_q", P, 128), ("L0x_kv", P, 256), ("L0x_o", P, 128), ("L0x_bo", 1, 128),
    ("L0f_gate", P, 8), ("L0f_gb", P, 8), ("L0f_w1", P, 9 * 256), ("L0f_w3", P, 9 * 256), ("L0f_w2", P, 9 * 256),
    ("L1a_qkv", P, 384), ("L1a_b", P, 16), ("L1a_bb", 16, 1), ("L1a_o", P, 128), ("L1a_bo", 1, 128),
    ("L1a_scale", P, 128),
    ("L1x_q", P, 1024), ("L1x_kv", P, 2048), ("L1x_o", P, 1024), ("L1x_bo", 1, 128),
    ("L1f_gate", P, 8), ("L1f_w1", P, 8 * 512), ("L1f_w2", P, 8 * 512),
    ("L2a_qkv", P, 384), ("L2a_proj", P, 512), ("L2a_o", P, 128), ("L2a_bo", 1, 128),
    ("L2a_gamma", P, 128), ("L2a_beta", P, 128), ("L2a_w1", P, 512), ("L2a_b1", P, 4), ("L2a_w2", P, 512),
    ("L2a_b2", 1, 128),
    ("L2x_q", P, 128), ("L2x_k", P, 128), ("L2x_v", P, 128), ("L2x_o", P, 128),
    ("L2x_bq", P, 1), ("L2x_bk", P, 1), ("L2x_bv", 1, 128), ("L2x_bo", 1, 128),
    ("L2f_gate", P, 8), ("L2f_gb", P, 8), ("L2f_w1", P, 9 * 256), ("L2f_w3", P, 9 * 256), ("L2f_w2", P, 9 * 256),
    ("L3a_basis", P, 128), 
    ("L3a_v", P, 128), ("L3a_vb", 1, 128), ("L3a_o", P, 128), ("L3a_bo", 1, 128),
    ("L3x_gates", P, 3 * 16), ("L3x_ib", 8, 1), ("L3x_fb", 8, 1), ("L3x_w", P, 128),
    ("L3f_w", P, 128), ("L3f_b", P, 128),
]


SWAPPED = ("w1", "w3", "w2")


def group_of(name):
    st, w = name.split("_")
    return st + "_experts" if st in ("L0f", "L2f") and w in SWAPPED else st


GROUPS = {}
for _n, _p, _w in WEIGHTS:
    _g = GROUPS.setdefault(group_of(_n), {})
    _at = max((e for _, _, e in _g.values()), default=0)
    _g[_n] = (_p, _at, _at + _w)


def group_words(g):
    return max(e for _, _, e in GROUPS[g].values())


def build(nc, dram, out):
    with ExitStack() as ctx:
        _build(nc, ctx, dram, out)


def _build(nc, ctx, dram, out):
    def sb(name, shape, dt=F32):
        return ctx.enter_context(nc.sbuf_tensor(name, shape, dt))

    pe, dve, act, sp = nc.tensor, nc.vector, nc.scalar, nc.sync

    group_tile, w_in = {}, {}
    for g in GROUPS:
        if g != "L2f_experts":
            group_tile[g] = sb("weights_" + g, [P, group_words(g)])
            w_in[g] = ctx.enter_context(nc.semaphore("weights_in_" + g))
    group_tile["L2f_experts"] = group_tile["L0f_experts"]
    W = {n: group_tile[g][0:p, a:e] for g, members in GROUPS.items() for n, (p, a, e) in members.items()}
    head_mats = W["L3m_mats"]

    def weights(prefix):
        return w_in[prefix], 16

    def const(name, rows=P):
        a, w = CONST[name]
        return W["con_sts"][0:rows, a:a + w]

    IDENT = const("ident")
    ident_bf = sb("ident_bf", [P, P], BF16)
    neg_wide_bf = sb("neg_wide_bf", [P, 2 * P], BF16)
    neg_causal_bf = neg_wide_bf[:, P:2 * P]
    neg_causal_t_bf = sb("neg_causal_t_bf", [P, P], BF16)
    ones_row = const("ones", 1)[:, 0:128]
    core_sym = sb("core_sym", [R, R])
    res_mean = sb("res_mean", [R, R])
    neg_bb = sb("neg_bb", [H, 1])
    a_tok = sb("a_tok", [P, NS, HC])

    x_tok = sb("x_tok", [P, NS, D])
    xT = sb("xT", [P, NT])
    ctx_tok = sb("ctx_tok", [P, NS, D])
    ctxT = sb("ctxT", [P, NT])
    x_raw = sb("x_raw", [P, NS, D])
    inputs = {"xT": xT, "x_tok": x_raw, "ctxT": ctxT, "ctx_tok": ctx_tok}
    x_all = sb("x_all", [P, B, D])
    xT_all = sb("xT_all", [P, B * T])

    res = sb("res", [P, NS, D])
    stats = sb("stats", [P, NS, 6])
    mv = sb("mv", [P, NS, 2])
    lnv = sb("lnv", [P, NS, 1])
    rstd = sb("rstd", [P, NS, 1])
    qs = sb("qs", [P, NS, D])
    ks = sb("ks", [P, NS, D])
    qk2 = sb("qk2", [P, NS, 2, D])
    qk3 = sb("qk3", [P, NS, 2, D])
    zeros = sb("zeros", [H, T])
    qT = sb("qT", [P, 2, NT])
    kT = sb("kT", [P, NT])
    share_a = sb("share_a", [P, NS * H * (R + 1)])
    bd = share_a[:, 0:NS * 4 * 2 * T].rearrange("p (u j t) -> p u j t", u=NS, j=4)
    vaug_r = share_a[:].rearrange("p (u h d) -> p u h d", u=NS, h=H)
    small = sb("small", [P, NS, 64])
    small2 = sb("small2", [P, NS, 64])
    vaug = sb("vaug", [P, NS, 2, H, DH + 1])
    vaug_c = sb("vaug_c", [P, NS, HC, DC + 1])
    ctxbd = sb("ctxbd", [P, NS, H, DH + 1])
    attn = sb("attn", [P, NS, D])
    attnT = sb("attnT", [P, NS, D])
    NPB = 3
    probs = sb("probs", [P, NPB, BANK])
    probsT = sb("probsT", [P, NPB, BANK])
    q64 = sb("q64", [P, 8, NT])
    k64 = sb("k64", [P, 8, NT])
    NHB = 4
    gact = sb("gact", [P, NHB, BANK])
    hT = sb("hT", [P, NHB, BANK])
    attn64 = gact[:].rearrange("p b (c r d) -> p (b c) r d", c=4, r=2).rearrange("p (u c) r d -> p u c r d", u=NS)
    attn64T = hT[:].rearrange("p b (c t) -> p (b c) t", c=4).rearrange("p (u c) t -> p u c t", u=NS)
    feats_q = q64
    pad4 = q64[:, 0:4, :]
    lat_pad = k64[:, 0:2, :]
    bq4 = sb("bq4", [P, 4])
    gateT = sb("gateT", [H, 6, NT])
    mdiag = k64[0:8].rearrange("p (u h) (a t) -> p u (h a) t", u=NS, a=2)

    psum = [ctx.enter_context(nc.psum_tensor(f"bank{i}", [P, BANK], F32)) for i in range(8)]

    setup_dve = ctx.enter_context(nc.semaphore("setup_dve"))
    first_in = ctx.enter_context(nc.semaphore("first_in"))
    stored = ctx.enter_context(nc.semaphore("stored"))

    sems = {}

    def S(name):
        if name not in sems:
            sems[name] = ctx.enter_context(nc.semaphore(name))
        return sems[name]

    counted = {}

    def nth(eng, name, n=1):
        counted[eng, name] = counted.get((eng, name), 0) + n
        return S(name), counted[eng, name]

    class Ring:

        def __init__(self):
            self.fills = [0] * 8
            self.frees = [{"dve": 0, "act": 0} for _ in range(8)]
            self.last = [None] * 8
            self.at = {}
            self.n = 0

        def open(self, key, by, bank=None):
            if bank is None:
                bank, self.n = self.n % 6, self.n + 1
            if self.last[bank]:
                pe.wait_ge(S(f"bank{bank}_freed_{self.last[bank]}"), self.frees[bank][self.last[bank]])
            self.fills[bank] += 1
            self.frees[bank][by] += 1
            self.last[bank] = by
            assert key not in self.at, key
            self.at[key] = (bank, self.fills[bank], by, self.frees[bank][by])
            return psum[bank]

        def filled(self, key):
            return S(f"bank{self.at[key][0]}_full")

        def full(self, key):
            b, n, _, _ = self.at[key]
            return S(f"bank{b}_full"), n

        def freed(self, key):
            b, _, by, n = self.at[key]
            return S(f"bank{b}_freed_{by}"), n

        def free(self, key):
            b, _, by, _ = self.at[key]
            return S(f"bank{b}_freed_{by}")

        def bank(self, key):
            return psum[self.at[key][0]]

    ring = Ring()

    class Order:

        def __init__(self, eng, name):
            self.eng, self.name, self.n = eng, name, {}

        def count(self, ins, sem=None):
            sem = sem or S(f"{self.name}_step")
            self.n[id(sem)] = self.n.get(id(sem), 0) + 1
            ins.then_inc(sem, 1)
            return sem

        def link(self, ins, sem=None):
            sem = self.count(ins, sem)
            self.eng.wait_ge(sem, self.n[id(sem)])

        def settle(self, sem=None):
            sem = sem or S(f"{self.name}_step")
            self.eng.wait_ge(sem, self.n[id(sem)])

        def each(self, ins_of, sem=None):
            used = [self.count(ins_of(u), sem(u) if callable(sem) else sem) for u in range(NS)]
            for sem in {id(x): x for x in used}.values():
                self.eng.wait_ge(sem, self.n[id(sem)])

    def heads(ap, n):
        return ap.rearrange("p (h d) -> p h d", h=n)

    def over(ap, n):
        return ap.unsqueeze(2).to_broadcast([ap.shape[0], ap.shape[1], n])

    def among(ap, n):
        return ap.unsqueeze(1).to_broadcast([ap.shape[0], n, ap.shape[1]])

    def hidden(e, k, per):
        if per == 2:
            return hT[:, (2 * e + k) % NHB, 0:NT]
        return hT[:, (2 * e + k // 2) % NHB, (k % 2) * NT:(k % 2 + 1) * NT]

    def tk(u):
        return slice(u * T, u * T + T)

    with nc.Block(name="setup") as block:
        @block.sync
        def _(eng):
            for g in w_in:
                sp.dma_start(group_tile[g][:], dram[g]).then_inc(w_in[g], 16)
                if g == "con":
                    for name, dst in inputs.items():
                        sp.dma_start(dst[:], dram[name][0]).then_inc(first_in, 16)
            sp.wait_ge(first_in, len(inputs) * 16)

        @block.vector
        def _(eng):
            o = Order(dve, "setup")
            dve.wait_ge(*weights("con"))
            o.link(dve.tensor_copy(ident_bf[:], IDENT), setup_dve)
            o.link(dve.memset(neg_wide_bf[:, 0:P], 0.0), setup_dve)
            o.link(dve.tensor_copy(neg_causal_bf, const("neg_causal")), setup_dve)
            o.link(dve.tensor_copy(neg_causal_t_bf[:], const("neg_causal_t")), setup_dve)
            o.link(dve.memset(zeros[:], 0.0), setup_dve)
            o.link(dve.memset(vaug[:], 1.0), setup_dve)
            o.link(dve.memset(vaug_c[:], 1.0), setup_dve)
            dve.wait_ge(*weights("L3m"))
            hr = head_mats[:].rearrange("p (h s) -> p h s", h=H)
            o.link(dve.tensor_tensor(core_sym[:], W["L3m_core"][:], W["L3m_coreT"][:], ALU.add), setup_dve)
            o.link(dve.tensor_reduce(res_mean[:], hr.rearrange("p h s -> p s h"), X, ALU.add), setup_dve)
            o.link(dve.tensor_scalar(res_mean[:], res_mean[:], -1.0 / H, None, ALU.mult), setup_dve)
            o.link(dve.scalar_tensor_tensor(core_sym[:], core_sym[:], 0.5 / H, res_mean[:], ALU.mult, ALU.add), setup_dve)
            o.link(dve.tensor_tensor(hr, hr, among(core_sym[:], H), ALU.add), setup_dve)

    STAGES_RUN = STAGES
    with nc.Fori(0, B // NS) as pair:
        with nc.Block(name="pair") as block:
            @block.tensor
            def _(eng):
                mm, tr = pe.matmul, pe.transpose

                def warm(bank, n):
                    for _ in range(n):
                        mm(heads(bank[:], 2), ident_bf[:], among(neg_wide_bf[:], 2), start=True, stop=True)

                def transpose_x(fill=WARM_X):
                    for u in range(NS):
                        b = ring.open(("xT", stage[0], u), "act")
                        warm(b, fill[u])
                        pe.wait_ge(*nth("pe", "x_new"))
                        tr(b[:, 0:T], x_tok[:, u, :], IDENT).then_inc(ring.filled(("xT", stage[0], u)), 1)

                def wait_xT():
                    for u in range(NS):
                        pe.wait_ge(*ring.freed(("xT", stage[0] - 1, u)))

                def row_bias(out_ap, row):
                    mm(out_ap, ones_row, row, start=False, stop=True)

                def turn_attn(st, u, n=0):
                    b = ring.open((st, "aT", u), "act")
                    warm(b, n)
                    pe.wait_ge(*ring.freed((st, "o", u)))
                    tr(b[:, 0:T], attn[:, u, :], IDENT).then_inc(ring.filled((st, "aT", u)), 1)

                def project_attn(st, u, w, bias, n=0):
                    b = ring.open((st, "y", u), "dve")
                    warm(b, n)
                    pe.wait_ge(*ring.freed((st, "aT", u)))
                    m = mm(b[:, 0:D], attnT[:, u, :], w, start=True, stop=bias is None)
                    if bias is not None:
                        m = mm(b[:, 0:D], ones_row, bias, start=False, stop=True)
                    m.then_inc(ring.filled((st, "y", u)), 1)

                def attn_out(st, w, bias, slots=range(NS)):
                    for u in slots:
                        turn_attn(st, u, WARM_A[u])
                    for u in slots:
                        project_attn(st, u, w, bias, WARM_Y[u])

                def softmax_units(st, n_units, score, value, acc, w=None, bias=None):
                    total = NS * n_units
                    for step in range(total + 3):
                        if step < total:
                            b = ring.open((st, "s", step), "dve")
                            score(step // n_units, step % n_units, b).then_inc(ring.filled((st, "s", step)), 1)
                        i = step - 2
                        if 0 <= i < total:
                            b = ring.open((st, "pT", i), "act")
                            warm(b, WARM_UNIT[st] + (2 if step >= total else 0))
                            pe.wait_ge(*nth("pe", "probs_ready"))
                            for k in range(4):
                                t_ = tr(b[:, k * T:k * T + T], probs[:, i % NPB, k * T:k * T + T], IDENT)
                            t_.then_inc(ring.filled((st, "pT", i)), 1)
                        i = step - 3
                        if 0 <= i < total:
                            pe.wait_ge(*ring.freed((st, "pT", i)))
                            u, n = i // n_units, i % n_units
                            if acc == "slot":
                                b = psum[6 + u] if n else ring.open((st, "o", u), "dve", 6 + u)
                            else:
                                b = ring.open((st, "o", i), "dve")
                            last = value(u, n, i % NPB, b)
                            if acc == "unit":
                                last.then_inc(ring.filled((st, "o", i)), 1)
                            elif n == n_units - 1:
                                last.then_inc(ring.filled((st, "o", u)), 1)
                        if w is not None and step == n_units + 5:
                            turn_attn(st, 0)
                        if w is not None and step == n_units + 6:
                            project_attn(st, 0, w, bias)
                    if w is not None:
                        attn_out(st, w, bias, [1])

                stage = [0]
                pe.wait_ge(*weights("con"))
                pe.wait_ge(setup_dve, 4)

                if STAGES_RUN > 0:
                    pe.wait_ge(*weights("L0a"))
                    for u in range(NS):
                        b = ring.open(("L0a", "qv", u), "dve")
                        mm(b[:, 0:D], xT[:, tk(u)], W["L0a_qkv"][:, 0:D], start=True, stop=True)
                        mm(b[:, D:2 * D], xT[:, tk(u)], W["L0a_qkv"][:, 2 * D:3 * D], start=True, stop=True)\
                            .then_inc(ring.filled(("L0a", "qv", u)), 1)
                        b = ring.open(("L0a", "k", u), "act")
                        mm(b[:, 0:D], xT[:, tk(u)], W["L0a_qkv"][:, D:2 * D], start=True, stop=True)\
                            .then_inc(ring.filled(("L0a", "k", u)), 1)
                    for u in range(NS):
                        pe.wait_ge(*nth("pe", "L0a_v"))
                        pe.wait_ge(*ring.freed(("L0a", "k", u)))
                        b = ring.open(("L0a", "ctx", u), "dve")
                        mm(b[:, 0:H * 9], ks[0:64, u, :], vaug[0:64, u, 0].rearrange("p h d -> p (h d)"),
                           start=True, stop=True).then_inc(ring.filled(("L0a", "ctx", u)), 1)
                        pe.wait_ge(*nth("pe", "L0a_qs"))
                        b = ring.open(("L0a", "qsT", u), "act")
                        tr(b[:, 0:T], qs[:, u, :], IDENT).then_inc(ring.filled(("L0a", "qsT", u)), 1)
                    for u in range(NS):
                        pe.wait_ge(*ring.freed(("L0a", "ctx", u)))
                        pe.wait_ge(*ring.freed(("L0a", "qsT", u)))
                        b = ring.open(("L0a", "o", u), "dve", 6 + u)
                        mm(b[:, 0:H * 9], qT[:, 0, tk(u)], ctxbd[:, u].rearrange("p h d -> p (h d)"),
                           start=True, stop=True).then_inc(ring.filled(("L0a", "o", u)), 1)
                    attn_out("L0a", W["L0a_o"][:], None)
                    pe.wait_ge(*weights("L0x"))
                    b = ring.open(("L0x", "k"), "dve")
                    mm(b[:, 0:NT], W["L0x_kv"][:, 0:D], ctxT[:], start=True, stop=True)
                    b = ring.open(("L0x", "v"), "dve")
                    for u in range(NS):
                        c = 2 * u * D
                        mm(b[:, c:c + D], ctxT[:, tk(u)], W["L0x_kv"][:, D:2 * D], start=True, stop=True)
                    transpose_x()

                def qkT_products(st, pairs_, key, by):
                    b = ring.open((st, key), by)
                    for i, (w, src) in enumerate(pairs_):
                        m = mm(b[:, i * NT:(i + 1) * NT], w, src, start=True, stop=True)
                    m.then_inc(ring.filled((st, key)), 1)

                if STAGES_RUN > 1:
                    stage[0] = 1
                    wait_xT()
                    qkT_products("L0x", [(W["L0x_q"][:], xT[:])], "q", "act")
                    b = ring.bank(("L0x", "k"))
                    mm(b[:, NT:2 * NT], W["L0x_kv"][:, 0:D], xT[:], start=True, stop=True)\
                        .then_inc(ring.filled(("L0x", "k")), 1)
                    b = ring.bank(("L0x", "v"))
                    for u in range(NS):
                        c = (2 * u + 1) * D
                        m = mm(b[:, c:c + D], xT[:, tk(u)], W["L0x_kv"][:, D:2 * D], start=True, stop=True)
                    m.then_inc(ring.filled(("L0x", "v")), 1)
                    pe.wait_ge(*ring.freed(("L0x", "q")))
                    pe.wait_ge(*ring.freed(("L0x", "k")))

                    def score(u, n, b):
                        c, j = n // 2, 2 * (n % 2)
                        mm(heads(b[:], 2), ident_bf[:], among(neg_wide_bf[:], 2), start=True, stop=False)
                        return mm(heads(b[:], 2), pad4[:, c, tk(u)], bd[:, u, j:j + 2, :], start=False, stop=True)

                    def value(u, n, buf, b):
                        for k in range(2):
                            h = 2 * n + k
                            for s_ in range(2):
                                c = (2 * k + s_) * T
                                m = mm(b[:, 9 * h:9 * h + 9], probsT[:, buf, c:c + T], vaug[:, u, s_, h, :],
                                       start=s_ == 0, stop=s_ == 1)
                        return m

                    pe.wait_ge(*ring.freed(("L0x", "v")))
                    softmax_units("L0x", 8, score, value, "slot", W["L0x_o"][:], W["L0x_bo"][:])
                    transpose_x()

                def gate_logits(st, w):
                    b = ring.open((st, "logits"), "dve")
                    for u in range(NS):
                        m = mm(b[:, 8 * u:8 * u + 8], xT[:, tk(u)], w, start=True, stop=True)
                    m.then_inc(ring.filled((st, "logits")), 1)

                def expert_up(st, i, parts):
                    b = ring.open((st, "up", i), "dve" if st != "L1f" else "act")
                    for k, w in enumerate(parts):
                        m = mm(b[:, k * NT:(k + 1) * NT], w, xT[:], start=True, stop=True)
                    m.then_inc(ring.filled((st, "up", i)), 1)

                def expert_down(st, e, per):
                    b = ring.open((st, "y", e), "dve")
                    for u in range(NS):
                        for k in range(per):
                            m = mm(b[:, u * D:(u + 1) * D], hidden(e, k, per)[:, tk(u)],
                                   W[st + "_w2"][:, (per * e + k) * P:(per * e + k + 1) * P],
                                   start=k == 0, stop=k == per - 1)
                    m.then_inc(ring.filled((st, "y", e)), 1)

                def swiglu(st):
                    pe.wait_ge(*weights(st))
                    wait_xT()
                    gate_logits(st, W[st + "_gate"][:])
                    if st == "L2f":
                        pe.wait_ge(S("L2f_in"), 16)
                    else:
                        pe.wait_ge(*weights("L0f_experts"))
                    for i in range(20):
                        if i < 18:
                            f = i * 128
                            expert_up(st, i, (W[st + "_w1"][:, f:f + 128], W[st + "_w3"][:, f:f + 128]))
                        if i % 2 == 1 and i >= 3:
                            pe.wait_ge(*ring.freed((st, "up", i - 3)))
                            pe.wait_ge(*ring.freed((st, "up", i - 2)))
                            expert_down(st, (i - 3) // 2, 2)
                    transpose_x()

                if STAGES_RUN > 2:
                    stage[0] = 2
                    swiglu("L0f")

                if STAGES_RUN > 3:
                    stage[0] = 3
                    pe.wait_ge(*weights("L1a"))
                    wait_xT()
                    b = ring.open(("L1a", "beta"), "act")
                    mm(b[0:H, 0:NT], W["L1a_b"][:], xT[:], start=True, stop=True)\
                        .then_inc(ring.filled(("L1a", "beta")), 1)
                    for u in range(NS):
                        b = ring.open(("L1a", "qkv", u), "dve")
                        mm(b[:, 0:3 * D], xT[:, tk(u)], W["L1a_qkv"][:], start=True, stop=True)\
                            .then_inc(ring.filled(("L1a", "qkv", u)), 1)
                    pe.wait_ge(*weights("L1x"))
                    for c in range(0, 8, 2):
                        qkT_products("L1x", [(W["L1x_kv"][:, (c + k) * P:(c + k + 1) * P], ctxT[:]) for k in range(2)],
                                     f"k{c}", "act")
                    b = ring.open(("L1a", "decay"), "dve")
                    warm(b, WARM_DECAY)
                    for u in range(NS):
                        pe.wait_ge(*nth("pe", "L1a_decay"))
                        m = tr(b[:, u * H:u * H + H], gateT[0:H, 2, tk(u)], IDENT[0:H, 0:H])
                    m.then_inc(ring.filled(("L1a", "decay")), 1)
                    for u in range(NS):
                        b = ring.open(("L1a", "qT", u), "dve")
                        warm(b, WARM_Q)
                        pe.wait_ge(*nth("pe", "L1a_q"))
                        tr(b[:, 0:T], qk2[:, u, 0, :], IDENT).then_inc(ring.filled(("L1a", "qT", u)), 1)
                    for u in range(NS):
                        b = ring.open(("L1a", "kT", u), "act")
                        warm(b, WARM_K)
                        pe.wait_ge(*nth("pe", "L1a_k"))
                        tr(b[:, 0:T], ks[:, u, :], IDENT).then_inc(ring.filled(("L1a", "kT", u)), 1)
                    for u in range(NS):
                        pe.wait_ge(*ring.freed(("L1a", "qT", u)))
                        pe.wait_ge(*ring.freed(("L1a", "kT", u)))
                    for i in range(2 * 4 + 1):
                        if i < 8:
                            u, c = i // 4, i % 4
                            b = ring.open(("L1a", "s", i), "dve")
                            mm(heads(b[:], 4), pad4[:, c, tk(u)], bd[:, u, :, 0:T],
                               start=True, stop=True).then_inc(ring.filled(("L1a", "s", i)), 1)
                        if i >= 1:
                            u, c = (i - 1) // 4, (i - 1) % 4
                            pe.wait_ge(*ring.freed(("L1a", "s", i - 1)))
                            b = psum[6 + u] if c else ring.open(("L1a", "o", u), "dve", 6 + u)
                            for j in range(4):
                                h = 4 * c + j
                                m = mm(b[:, 9 * h:9 * h + 9], probs[:, (i - 1) % NPB, j * T:j * T + T],
                                       vaug[:, u, 0, h, :], start=True, stop=True)
                            m.then_inc(ring.filled(("L1a", "o", u)) if c == 3 else S("L1a_used"), 1)
                    attn_out("L1a", W["L1a_o"][:], W["L1a_bo"][:])
                    for u in range(NS):
                        for c in range(2):
                            b = ring.open(("L1x", "v", u, c), "dve")
                            mm(b[:], ctxT[:, tk(u)], W["L1x_kv"][:, 1024 + c * BANK:1024 + (c + 1) * BANK],
                               start=True, stop=True).then_inc(ring.filled(("L1x", "v", u, c)), 1)
                    transpose_x((WARM_RMS, 0))

                def score64(rhs_of):
                    def score(u, n, b, first=True):
                        r, c0 = n % 2, 4 * (n // 2)
                        for j in range(4):
                            rows, rhs = rhs_of(r, c0 + j, u)
                            m = mm(b[:, j * T:j * T + T], q64[rows, c0 + j, tk(u)], rhs,
                                   start=first, stop=first or j == 3)
                        return m
                    return score

                if STAGES_RUN > 4:
                    stage[0] = 4
                    wait_xT()
                    for c in range(0, 8, 2):
                        qkT_products("L1x", [(W["L1x_q"][:, (c + k) * P:(c + k + 1) * P], xT[:]) for k in range(2)],
                                     f"q{c}", "act")
                    for c in range(0, 8, 2):
                        pe.wait_ge(*ring.freed(("L1x", f"k{c}")))
                        pe.wait_ge(*ring.freed(("L1x", f"q{c}")))
                    for u in range(NS):
                        for c in range(2):
                            pe.wait_ge(*ring.freed(("L1x", "v", u, c)))

                    def value64(u, n, buf, b):
                        r, c0 = n % 2, 4 * (n // 2)
                        for j in range(4):
                            h = 2 * (c0 + j) + r
                            m = mm(b[:, j * (R + 1):(j + 1) * (R + 1)], probsT[:, buf, j * T:j * T + T],
                                   vaug_r[:, u, h, :], start=True, stop=True)
                        return m

                    softmax_units("L1x", 4, score64(lambda r, c, u: (slice(64 * r, 64 * r + 64), k64[64 * r:64 * r + 64, c, tk(u)])),
                                  value64, "unit")
                    for u in range(NS):
                        for n in range(4):
                            pe.wait_ge(*ring.freed(("L1x", "o", 4 * u + n)))
                        for c in range(0, 8, 4):
                            b = ring.open(("L1x", "aT", u, c), "act")
                            for k in range(4):
                                m = tr(b[:, k * T:k * T + T], attn64[:, u, c + k].rearrange("p r d -> p (r d)"), IDENT)
                            m.then_inc(ring.filled(("L1x", "aT", u, c)), 1)
                    for u in range(NS):
                        for c in range(0, 8, 4):
                            pe.wait_ge(*ring.freed(("L1x", "aT", u, c)))
                        b = ring.open(("L1x", "y", u), "dve")
                        for c in range(8):
                            mm(b[:, 0:D], attn64T[:, u, c, :], W["L1x_o"][:, c * P:(c + 1) * P], start=c == 0, stop=False)
                        mm(b[:, 0:D], ones_row, W["L1x_bo"][:], start=False, stop=True)\
                            .then_inc(ring.filled(("L1x", "y", u)), 1)
                    transpose_x()

                if STAGES_RUN > 5:
                    stage[0] = 5
                    pe.wait_ge(*weights("L1f"))
                    wait_xT()
                    gate_logits("L1f", W["L1f_gate"][:])
                    for i in range(16 + 3):
                        if i < 16:
                            f = i * 256
                            expert_up("L1f", i, (W["L1f_w1"][:, f:f + 128], W["L1f_w1"][:, f + 128:f + 256]))
                        if i % 2 == 1 and i >= 3:
                            pe.wait_ge(*ring.freed(("L1f", "up", i - 3)))
                            pe.wait_ge(*ring.freed(("L1f", "up", i - 2)))
                            expert_down("L1f", (i - 3) // 2, 4)
                    transpose_x()

                if STAGES_RUN > 6:
                    stage[0] = 6
                    pe.wait_ge(*weights("L2a"))
                    wait_xT()
                    qkT_products("L2a", [(W["L2a_qkv"][:, 0:D], xT[:]), (W["L2a_qkv"][:, D:2 * D], xT[:])], "qk", "act")
                    b = ring.open(("L2a", "v"), "dve")
                    for u in range(NS):
                        m = mm(b[:, u * D:(u + 1) * D], xT[:, tk(u)], W["L2a_qkv"][:, 2 * D:3 * D], start=True, stop=True)
                    m.then_inc(ring.filled(("L2a", "v")), 1)
                    pe.wait_ge(*ring.freed(("L2a", "qk")))
                    for u in range(NS):
                        b = ring.open(("L2a", "kf", u), "dve")
                        mm(b[:], qT[:, 1, tk(u)], W["L2a_proj"][:], start=True, stop=True)\
                            .then_inc(ring.filled(("L2a", "kf", u)), 1)
                    for c in range(0, 4, 2):
                        b = ring.open(("L2a", "qf", c), "dve")
                        for k in range(2):
                            m = mm(b[:, k * NT:(k + 1) * NT], W["L2a_proj"][:, (c + k) * P:(c + k + 1) * P], qT[:, 0, :],
                                   start=True, stop=True)
                        m.then_inc(ring.filled(("L2a", "qf", c)), 1)
                    pe.wait_ge(*ring.freed(("L2a", "v")))
                    for u in range(NS):
                        b = ring.open(("L2a", "kv", u), "dve")
                        warm(b, 2)
                        pe.wait_ge(*ring.freed(("L2a", "kf", u)))
                        for c in range(4):
                            m = mm(b[:, 36 * c:36 * c + 36], probs[:, u, c * P:(c + 1) * P],
                                   vaug[:, u, 0, 4 * c:4 * c + 4, :], start=True, stop=True)
                        m.then_inc(ring.filled(("L2a", "kv", u)), 1)
                    for c in range(0, 4, 2):
                        pe.wait_ge(*ring.freed(("L2a", "qf", c)))
                    for u in range(NS):
                        pe.wait_ge(*ring.freed(("L2a", "kv", u)))
                        b = ring.open(("L2a", "o", u), "dve", 6 + u)
                        for c in range(4):
                            m = mm(b[:, 36 * c:36 * c + 36], feats_q[:, c, tk(u)], ctxbd[:, u, 4 * c:4 * c + 4, :],
                                   start=True, stop=True)
                        m.then_inc(ring.filled(("L2a", "o", u)), 1)
                    attn_out("L2a", W["L2a_o"][:], W["L2a_bo"][:])
                    for u in range(NS):
                        b = ring.open(("L2a", "x1T", u), "act")
                        warm(b, WARM_X[u])
                        pe.wait_ge(*nth("pe", "L2a_x1"))
                        tr(b[:, 0:T], qs[:, u, :], IDENT).then_inc(ring.filled(("L2a", "x1T", u)), 1)
                    for u in range(NS):
                        pe.wait_ge(*ring.freed(("L2a", "x1T", u)))
                    for c in range(0, 4, 2):
                        qkT_products("L2a", [(W["L2a_w1"][:, (c + k) * P:(c + k + 1) * P], kT[:]) for k in range(2)],
                                     f"h{c}", "act")
                    for c in range(0, 4, 2):
                        pe.wait_ge(*ring.freed(("L2a", f"h{c}")))
                    for u in range(NS):
                        b = ring.open(("L2a", "y2", u), "dve")
                        for c in range(4):
                            mm(b[:, 0:D], gact[:, c // 2, (c % 2) * NT + u * T:(c % 2) * NT + u * T + T],
                               W["L2a_w2"][:, c * P:(c + 1) * P], start=c == 0, stop=False)
                        mm(b[:, 0:D], ones_row, W["L2a_b2"][:], start=False, stop=True)\
                            .then_inc(ring.filled(("L2a", "y2", u)), 1)
                    pe.wait_ge(*weights("L2x"))
                    qkT_products("L2x", [(W["L2x_k"][:], ctxT[:])], "k", "dve")
                    b = ring.open(("L2x", "v"), "dve")
                    for u in range(NS):
                        mm(b[:, u * D:(u + 1) * D], ctxT[:, tk(u)], W["L2x_v"][:], start=True, stop=False)
                        m = mm(b[:, u * D:(u + 1) * D], ones_row, W["L2x_bv"][:], start=False, stop=True)
                    m.then_inc(ring.filled(("L2x", "v")), 1)
                    transpose_x()

                def score8(u, n, b):
                    return mm(heads(b[:], 4), pad4[:, n, tk(u)], bd[:, u, :, 0:T], start=True, stop=True)

                def value8(u, n, buf, b):
                    for j in range(4):
                        h = 4 * n + j
                        m = mm(b[:, 9 * h:9 * h + 9], probsT[:, buf, j * T:j * T + T], vaug[:, u, 0, h, :],
                               start=True, stop=True)
                    return m

                if STAGES_RUN > 7:
                    stage[0] = 7
                    wait_xT()
                    qkT_products("L2x", [(W["L2x_q"][:], xT[:])], "q", "act")
                    pe.wait_ge(*ring.freed(("L2x", "k")))
                    pe.wait_ge(*ring.freed(("L2x", "v")))
                    pe.wait_ge(*ring.freed(("L2x", "q")))
                    softmax_units("L2x", 4, score8, value8, "slot", W["L2x_o"][:], W["L2x_bo"][:])
                    transpose_x()

                if STAGES_RUN > 8:
                    stage[0] = 8
                    swiglu("L2f")

                if STAGES_RUN > 9:
                    stage[0] = 9
                    pe.wait_ge(*weights("L3a"))
                    wait_xT()
                    qkT_products("L3a", [(W["L3a_basis"][:], xT[:])], "lat", "act")
                    b = ring.open(("L3a", "v"), "dve")
                    for u in range(NS):
                        mm(b[:, u * D:(u + 1) * D], xT[:, tk(u)], W["L3a_v"][:], start=True, stop=False)
                        m = mm(b[:, u * D:(u + 1) * D], ones_row, W["L3a_vb"][:], start=False, stop=True)
                    m.then_inc(ring.filled(("L3a", "v")), 1)
                    pe.wait_ge(*ring.freed(("L3a", "lat")))
                    for c in range(0, 8, 2):
                        qkT_products("L3a", [(head_mats[:, (c + k) * P:(c + k + 1) * P], lat_pad[0:R, 0, :]) for k in range(2)],
                                     f"q{c}", "act")
                    for c in range(0, 8, 2):
                        pe.wait_ge(*ring.freed(("L3a", f"q{c}")))
                    pe.wait_ge(*ring.freed(("L3a", "v")))
                    latent = score64(lambda r, c, u: (slice(0, P), lat_pad[:, r, tk(u)]))

                    def score_causal(u, n, b):
                        mm(heads(b[:], 4), ident_bf[:], among(neg_causal_bf, 4), start=True, stop=False)
                        return latent(u, n, b, first=False)

                    def value_latent(u, n, buf, b):
                        r, c0 = n % 2, 4 * (n // 2)
                        for j in range(4):
                            h = 2 * (c0 + j) + r
                            m = mm(b[:, 9 * h:9 * h + 9], probsT[:, buf, j * T:j * T + T], vaug[:, u, 0, h, :],
                                   start=True, stop=True)
                        return m

                    softmax_units("L3a", 4, score_causal, value_latent, "slot", W["L3a_o"][:], W["L3a_bo"][:])
                    transpose_x()

                if STAGES_RUN > 10:
                    stage[0] = 10
                    pe.wait_ge(*weights("L3x"))
                    wait_xT()
                    b = ring.open(("L3x", "gates"), "dve")
                    for g in range(2):
                        for k, src in enumerate((xT, ctxT, ctxT)):
                            m = mm(b[0:8, g * NT:(g + 1) * NT], W["L3x_gates"][:, 16 * k + 8 * g:16 * k + 8 * g + 8],
                                   src[:], start=k == 0, stop=k == 2)
                    m.then_inc(ring.filled(("L3x", "gates")), 1)
                    pe.wait_ge(*nth("pe", "L3x_gates"))
                    b = ring.open(("L3x", "mx"), "act")
                    for k, row in enumerate((4, 2)):
                        for u in range(NS):
                            m = tr(b[:, 16 * k + u * 8:16 * k + u * 8 + 8], gateT[0:8, row, tk(u)], IDENT[0:8, 0:8])
                    m.then_inc(ring.filled(("L3x", "mx")), 1)
                    for i in range(2 * 2 + 1):
                        if i < 4:
                            u, g = i // 2, i % 2
                            pe.wait_ge(*nth("pe", "L3x_bd")) if g == 0 else None
                            b = ring.open(("L3x", "D", i), "act")
                            warm(b, 1)
                            mm(heads(b[:], 4), ident_bf[:], among(neg_causal_t_bf[:], 4), start=True, stop=False)
                            mm(heads(b[:], 4), const("ones", 8)[:, 0:T], mdiag[:, u, 4 * g:4 * g + 4, :],
                               start=False, stop=True).then_inc(ring.filled(("L3x", "D", i)), 1)
                            b = ring.open(("L3x", "s", i), "dve")
                            mm(heads(b[:], 4), ctxT[64 * g:64 * g + 64, tk(u)], bd[64 * g:64 * g + 64, u, :, 0:T],
                               start=True, stop=True).then_inc(ring.filled(("L3x", "s", i)), 1)
                        if i >= 1:
                            u, g = (i - 1) // 2, (i - 1) % 2
                            pe.wait_ge(*ring.freed(("L3x", "s", i - 1)))
                            b = psum[6 + u] if g else ring.open(("L3x", "o", u), "dve", 6 + u)
                            for j in range(4):
                                h = 4 * g + j
                                m = mm(b[:, 17 * h:17 * h + 17], probsT[:, (i - 1) % NPB, j * T:j * T + T],
                                       vaug_c[:, u, h, :], start=True, stop=True)
                            m.then_inc(ring.filled(("L3x", "o", u)) if g else S("L3x_used"), 1)
                    transpose_x()

            @block.vector
            def _(eng):
                o = Order(dve, "dve")
                link, each = o.link, o.each

                def layer_norm(dst, affine=None, told=None):
                    each(lambda u: dve.bn_stats(stats[:, u, :], res[:, u, :]))
                    each(lambda u: dve.bn_aggr(mv[:, u, :], stats[:, u, :]), S("var_ready"))
                    for u in range(NS):
                        dve.wait_ge(*nth("dve", "rstd_ready"))
                        o.count(dve.tensor_scalar(dst(u), res[:, u, :], mv[:, u, 0:1], rstd[:, u, :],
                                                  ALU.subtract, ALU.mult), told if affine is None else None)
                    o.settle(told if affine is None else None)
                    if affine is not None:
                        each(lambda u: dve.tensor_tensor(dst(u), dst(u), affine[0], ALU.mult))
                        each(lambda u: dve.tensor_tensor(dst(u), dst(u), affine[1], ALU.add), told)

                def new_x():
                    layer_norm(lambda u: x_tok[:, u, :], told=S("x_new"))

                def add_product(key, base):
                    for u in range(NS):
                        dve.wait_ge(*ring.full(key(u)))
                        o.count(dve.tensor_tensor(res[:, u, :], ring.bank(key(u))[:, 0:D], base[:, u, :], ALU.add),
                                ring.free(key(u)))
                    for u in range(NS):
                        o.settle(ring.free(key(u)))

                def post_norm(st, base=x_tok):
                    add_product(lambda u: (st, "y", u), base)
                    new_x()

                def divide_heads(st, floor=None, add=None, rows=None, slots=range(NS)):
                    b = {u: heads(ring.bank((st, "o", u))[:, 0:H * 9], H) for u in slots}

                    def step(ins_of, sem=None):
                        used = [o.count(ins_of(u), sem and sem(u)) for u in slots]
                        for x in used:
                            o.settle(x)

                    for u in slots:
                        dve.wait_ge(*ring.full((st, "o", u)))
                    den, inv = (lambda u: small[:, u, 0:H]), (lambda u: small2[:, u, 0:H])
                    if floor is not None:
                        step(lambda u: dve.tensor_scalar(den(u), b[u][:, :, 8], floor, None, ALU.max))
                    elif add is not None:
                        step(lambda u: dve.tensor_scalar(den(u), b[u][:, :, 8], add, None, ALU.add))
                    else:
                        step(lambda u: dve.tensor_copy(den(u), b[u][:, :, 8]))
                    step(lambda u: dve.reciprocal(inv(u), den(u)))
                    if rows is not None:
                        step(lambda u: dve.tensor_scalar(inv(u), inv(u), rows, None, ALU.mult))
                    step(lambda u: dve.tensor_tensor(heads(attn[:, u, :], H), b[u][:, :, 0:8], over(inv(u), 8), ALU.mult),
                         lambda u: ring.free((st, "o", u)))

                def softmax_units(st, n_units, keys, after=None):
                    nh = BANK // keys
                    total = NS * n_units
                    for i in range(total):
                        s_ = heads(ring.bank((st, "s", i))[:], nh)
                        dve.wait_ge(*ring.full((st, "s", i)))
                        mx = small[:, i % 2, 32:32 + nh]
                        link(dve.tensor_reduce(mx, s_, X, ALU.max))
                        if i >= NPB:
                            dve.wait_ge(*ring.full((st, "pT", i - NPB)))
                        link(dve.tensor_tensor(heads(probs[:, i % NPB, :], nh), s_, over(mx, keys), ALU.subtract),
                             ring.free((st, "s", i)))
                        if after:
                            after(i)

                def early_divide(st, n_units):
                    return lambda i: divide_heads(st, slots=[0]) if i == n_units + 3 else None

                if STAGES_RUN > 0:
                    dve.wait_ge(*weights("L0a"))
                    for u in range(NS):
                        b = ring.bank(("L0a", "qv", u))
                        dve.wait_ge(*ring.full(("L0a", "qv", u)))
                        q3 = heads(b[:, 0:D], H)
                        link(dve.tensor_copy(vaug[:, u, 0, :, 0:8], heads(b[:, D:2 * D], H)), S("L0a_v"))
                        link(dve.tensor_reduce(small[:, u, 0:H], q3, X, ALU.max))
                        link(dve.tensor_tensor(heads(qs[:, u, :], H), q3, over(small[:, u, 0:H], 8), ALU.subtract),
                             ring.free(("L0a", "qv", u)))
                    for u in range(NS):
                        dve.wait_ge(*nth("dve", "L0a_expq"))
                        link(dve.tensor_reduce(small[:, u, 0:H], heads(qs[:, u, :], H), X, ALU.add))
                        link(dve.reciprocal(small2[:, u, 0:H], small[:, u, 0:H]))
                        link(dve.tensor_scalar(small2[:, u, 0:H], small2[:, u, 0:H], DH ** -0.5, None, ALU.mult))
                        link(dve.tensor_tensor(heads(qs[:, u, :], H), heads(qs[:, u, :], H), over(small2[:, u, 0:H], 8),
                                               ALU.mult), S("L0a_qs"))
                        dve.wait_ge(*ring.full(("L0a", "ctx", u)))
                        link(dve.tensor_tensor(ctxbd[:, u], heads(ring.bank(("L0a", "ctx", u))[:, 0:H * 9], H),
                                               over(const("head8"), 9), ALU.mult), ring.free(("L0a", "ctx", u)))
                    divide_heads("L0a", floor=1e-6, rows=const("late"))
                    post_norm("L0a", x_raw)

                if STAGES_RUN > 1:
                    b = ring.bank(("L0x", "k"))
                    dve.wait_ge(*ring.full(("L0x", "k")))
                    for u in range(NS):
                        for s_ in range(2):
                            ins = dve.tensor_tensor(bd[:, u, :, s_ * T:(s_ + 1) * T],
                                                    among(b[:, s_ * NT + u * T:s_ * NT + u * T + T], 4),
                                                    over(const("head8in32"), T), ALU.mult)
                            link(ins, ring.free(("L0x", "k")) if u == 1 and s_ == 1 else None)
                    b = ring.bank(("L0x", "v"))
                    dve.wait_ge(*ring.full(("L0x", "v")))
                    for u in range(NS):
                        for s_ in range(2):
                            c = (2 * u + s_) * D
                            last = u == 1 and s_ == 1
                            link(dve.tensor_copy(vaug[:, u, s_, :, 0:8], heads(b[:, c:c + D], H)),
                                 ring.free(("L0x", "v")) if last else None)
                    softmax_units("L0x", 8, 2 * T, early_divide("L0x", 8))
                    divide_heads("L0x", slots=[1])
                    post_norm("L0x")

                lg, mx, pr, pick = small2[:, :, 0:8], small2[:, :, 8], small2[:, :, 16:24], small2[:, :, 24:32]
                comb = small[:, :, 0:8]

                def gates_in(st, kind):
                    b = ring.bank((st, "logits"))
                    dve.wait_ge(*ring.full((st, "logits")))
                    link(dve.tensor_copy(lg, b[:, 0:16].rearrange("p (u e) -> p u e", u=2)), ring.free((st, "logits")))
                    if kind == "sigmoid":
                        link(dve.tensor_copy(pr, lg), S("gates_in"))
                    else:
                        link(dve.tensor_reduce(mx, lg, X, ALU.max))
                        link(dve.tensor_tensor(pr, lg, over(mx, 8), ALU.subtract), S("gates_in"))

                def gates(st, kind):
                    dve.wait_ge(*nth("dve", "gates_exp"))
                    if kind == "sigmoid":
                        link(dve.tensor_scalar(pr, pr, 1.0, None, ALU.add))
                        link(dve.reciprocal(pr, pr))
                    else:
                        link(dve.tensor_reduce(mx, pr, X, ALU.add))
                        link(dve.reciprocal(mx, mx))
                        link(dve.tensor_tensor(pr, pr, over(mx, 8), ALU.mult))
                    if kind == "softmax":
                        link(dve.tensor_tensor(pick, pr, among(W[st + "_gb"][:], 2), ALU.add))
                    elif kind == "sigmoid":
                        link(dve.tensor_tensor(pick, lg, among(W[st + "_gb"][:], 2), ALU.add))
                    else:
                        link(dve.tensor_copy(pick, pr))
                    for u in range(NS):
                        link(dve.max(small2[:, u, 32:40], small2[:, u, 24:32]))
                        link(dve.tensor_scalar(small2[:, u, 34:40], small2[:, u, 34:40], 0.0, -3e38, ALU.mult, ALU.add))
                        link(dve.match_replace(small2[:, u, 40:48], small2[:, u, 32:40], small2[:, u, 24:32], -2e38))
                    link(dve.tensor_scalar(small2[:, :, 48:56], small2[:, :, 40:48], -2e38, None, ALU.is_equal))
                    link(dve.tensor_tensor(comb, small2[:, :, 48:56], pr, ALU.mult))
                    if kind == "softmax_top":
                        link(dve.tensor_reduce(mx, comb, X, ALU.add))
                        link(dve.reciprocal(mx, mx))
                        link(dve.tensor_tensor(comb, comb, over(mx, 8), ALU.mult))

                def add_expert(st, i, e):
                    b = ring.bank((st, "y", i))
                    dve.wait_ge(*ring.full((st, "y", i)))
                    for u in range(NS):
                        y, r = b[:, u * D:(u + 1) * D], res[:, u, :]
                        ins = (dve.tensor_tensor(r, y, x_tok[:, u, :], ALU.add) if e < 0 else
                               dve.scalar_tensor_tensor(r, y, comb[:, u, e:e + 1], x_tok[:, u, :] if i == 0 else r,
                                                        ALU.mult, ALU.add))
                        link(ins, ring.free((st, "y", i)) if u else None)

                def swiglu(st, kind):
                    dve.wait_ge(*weights(st))
                    gates_in(st, kind)
                    for i in range(18 + 2):
                        if i < 18:
                            if i >= NHB:
                                dve.wait_ge(*ring.full((st, "y", (i - NHB) // 2)))
                            dve.wait_ge(*nth("dve", "gact_ready"))
                            link(dve.tensor_tensor(hT[:, i % NHB, 0:NT], gact[:, i % NHB, 0:NT],
                                                   ring.bank((st, "up", i))[:, NT:2 * NT], ALU.mult),
                                 ring.free((st, "up", i)))
                        if i == 1:
                            gates(st, kind)
                        if i % 2 == 1 and i >= 3:
                            add_expert(st, (i - 3) // 2, (i - 3) // 2 - 1)
                    new_x()

                if STAGES_RUN > 2:
                    swiglu("L0f", "softmax")

                if STAGES_RUN > 3:
                    dve.wait_ge(*weights("L1a"))
                    link(dve.tensor_scalar(neg_bb[:], W["L1a_bb"][:], -1.0, None, ALU.mult), S("L1a_negbb"))
                    t1 = [heads(qk2[:, u].rearrange("p a d -> p (a d)"), 2 * H) for u in range(NS)]
                    t2 = [heads(qk3[:, u].rearrange("p a d -> p (a d)"), 2 * H) for u in range(NS)]
                    cos, sin = const("cos"), const("sin")
                    for u in range(NS):
                        dve.wait_ge(*ring.full(("L1a", "qkv", u)))
                    qkv = [ring.bank(("L1a", "qkv", u)) for u in range(NS)]
                    qk = [heads(qkv[u][:, 0:2 * D], 2 * H) for u in range(NS)]
                    each(lambda u: dve.tensor_tensor(t1[u], qk[u], among(cos, 2 * H), ALU.mult))
                    each(lambda u: dve.tensor_tensor(t2[u][:, :, 0:4], qk[u][:, :, 4:8], among(sin[:, 0:4], 2 * H), ALU.mult))
                    each(lambda u: dve.tensor_tensor(t2[u][:, :, 4:8], qk[u][:, :, 0:4], among(sin[:, 4:8], 2 * H), ALU.mult))
                    each(lambda u: dve.tensor_tensor(t1[u], t1[u], t2[u], ALU.add))
                    each(lambda u: dve.tensor_scalar(t2[u], t1[u], 0.0, None, ALU.min), S("L1a_min"))
                    each(lambda u: dve.tensor_copy(vaug[:, u, 0, :, 0:8], heads(qkv[u][:, 2 * D:3 * D], H)),
                         lambda u: ring.free(("L1a", "qkv", u)))
                    dve.wait_ge(*ring.freed(("L1a", "beta")))
                    g = gateT
                    link(dve.tensor_scalar(g[:, 1, :], g[:, 0, :], 1.0, None, ALU.add))
                    link(dve.reciprocal(g[:, 1, :], g[:, 1, :]))
                    link(dve.tensor_scalar(g[:, 1, :], g[:, 1, :], 0.8, 0.999, ALU.max, ALU.min))
                    each(lambda u: dve.tensor_tensor_scan(g[:, 2, tk(u)], g[:, 1, tk(u)], zeros[:], 1.0,
                                                          ALU.mult, ALU.add), S("L1a_decay"))
                    for u in range(NS):
                        dve.wait_ge(*nth("dve", "L1a_exp"))
                        o.count(dve.scalar_tensor_tensor(t1[u], t1[u], 0.0, t2[u], ALU.max, ALU.add), S("L1a_q"))
                    o.settle(S("L1a_q"))
                    dve.wait_ge(*ring.full(("L1a", "decay")))
                    iv = [small2[:, u, 16:32] for u in range(NS)]
                    each(lambda u: dve.reciprocal(iv[u], ring.bank(("L1a", "decay"))[:, u * H:u * H + H]),
                         lambda u: ring.free(("L1a", "decay")) if u else None)
                    each(lambda u: dve.tensor_tensor(heads(ks[:, u, :], H), t1[u][:, H:2 * H, :], over(iv[u], 8), ALU.mult),
                         S("L1a_k"))
                    for u in range(NS):
                        dve.wait_ge(*ring.full(("L1a", "qT", u)))
                        link(dve.tensor_tensor(bd[:, u, :, 0:T], among(ring.bank(("L1a", "qT", u))[:, 0:T], 4),
                                               over(const("head8in32"), T), ALU.mult), ring.free(("L1a", "qT", u)))
                    for i in range(8):
                        dve.wait_ge(*ring.full(("L1a", "s", i)))
                        if i >= NPB:
                            k = i - NPB
                            if k == 3:
                                dve.wait_ge(*ring.full(("L1a", "o", 0)))
                            else:
                                dve.wait_ge(*nth("dve", "L1a_used"))
                        link(dve.tensor_tensor(heads(probs[:, i % NPB, :], 4), heads(ring.bank(("L1a", "s", i))[:], 4),
                                               among(const("causal_t"), 4), ALU.mult), ring.free(("L1a", "s", i)))
                    ob = [heads(ring.bank(("L1a", "o", u))[:, 0:H * 9], H) for u in range(NS)]
                    for u in range(NS):
                        dve.wait_ge(*ring.full(("L1a", "o", u)))
                    den, inv = (lambda u: small[:, u, 0:H]), (lambda u: small[:, u, 16:32])
                    each(lambda u: dve.scalar_tensor_tensor(den(u), iv[u], 1e-6, ob[u][:, :, 8], ALU.mult, ALU.add))
                    each(lambda u: dve.reciprocal(inv(u), den(u)))
                    each(lambda u: dve.tensor_tensor(heads(attn[:, u, :], H), ob[u][:, :, 0:8], over(inv(u), 8), ALU.mult),
                         lambda u: ring.free(("L1a", "o", u)))
                    add_product(lambda u: ("L1a", "y", u), x_tok)
                    each(lambda u: dve.tensor_tensor(attn[:, u, :], res[:, u, :], res[:, u, :], ALU.mult))
                    each(lambda u: dve.tensor_reduce(mv[:, u, 1:2], attn[:, u, :], X, ALU.add), S("ms_ready"))
                    for u in range(NS):
                        dve.wait_ge(*nth("dve", "rstd_ready"))
                        o.count(dve.scalar_tensor_tensor(res[:, u, :], res[:, u, :], rstd[:, u, :], W["L1a_scale"][:],
                                                         ALU.mult, ALU.mult))
                    o.settle()
                    each(lambda u: dve.tensor_tensor(res[:, u, :], res[:, u, :], x_tok[:, u, :], ALU.add))
                    new_x()

                if STAGES_RUN > 4:
                    link(dve.memset(vaug_r[:, :, :, R:R + 1], 1.0))
                    for u in range(NS):
                        for c in range(2):
                            dve.wait_ge(*ring.full(("L1x", "v", u, c)))
                            link(dve.tensor_copy(vaug_r[:, u, 8 * c:8 * c + 8, 0:R], heads(ring.bank(("L1x", "v", u, c))[:], 8)),
                                 ring.free(("L1x", "v", u, c)))

                    def finish_unit(k):
                        u, n = k // 4, k % 4
                        r, c0 = n % 2, 4 * (n // 2)
                        b = heads(ring.bank(("L1x", "o", k))[:, 0:4 * (R + 1)], 4)
                        dve.wait_ge(*ring.full(("L1x", "o", k)))
                        link(dve.reciprocal(small2[:, u, 0:4], b[:, :, R]))
                        link(dve.tensor_tensor(attn64[:, u, c0:c0 + 4, r, :], b[:, :, 0:R], over(small2[:, u, 0:4], R),
                                               ALU.mult), ring.free(("L1x", "o", k)))

                    softmax_units("L1x", 4, T, lambda i: finish_unit(i - 4) if i >= 4 else None)
                    for k in range(4, 8):
                        finish_unit(k)
                    post_norm("L1x")

                if STAGES_RUN > 5:
                    gates_in("L1f", "softmax_top")
                    gates("L1f", "softmax_top")
                    for e in range(E):
                        add_expert("L1f", e, e)
                    new_x()

                if STAGES_RUN > 6:
                    dve.wait_ge(*weights("L2a"))
                    b = ring.bank(("L2a", "v"))
                    dve.wait_ge(*ring.full(("L2a", "v")))
                    for u in range(NS):
                        link(dve.tensor_copy(vaug[:, u, 0, :, 0:8], heads(b[:, u * D:(u + 1) * D], H)),
                             ring.free(("L2a", "v")) if u else None)
                    keys = [("L2a", "kf", 0), ("L2a", "kf", 1), ("L2a", "qf", 0), ("L2a", "qf", 2)]
                    for i in range(4 + 1):
                        if i < 4:
                            dve.wait_ge(*ring.full(keys[i]))
                            link(dve.tensor_scalar(gact[:, i, :], ring.bank(keys[i])[:], 0.0, None, ALU.min), S("L2a_min"))
                        if i >= 1:
                            k = i - 1
                            dst = probs[:, k, :] if k < 2 else \
                                feats_q[:, 2 * (k - 2):2 * (k - 2) + 2, :].rearrange("p c t -> p (c t)")
                            dve.wait_ge(*nth("dve", "L2a_exp"))
                            link(dve.scalar_tensor_tensor(dst, ring.bank(keys[k])[:], 0.0, gact[:, k, :], ALU.max, ALU.add),
                                 ring.free(keys[k]))
                    for u in range(NS):
                        dve.wait_ge(*ring.full(("L2a", "kv", u)))
                        m = const("feat32").unsqueeze(1).unsqueeze(3).to_broadcast([P, 4, 4, 9])
                        link(dve.tensor_tensor(ctxbd[:, u].rearrange("p (c j) d -> p c j d", c=4),
                                               ring.bank(("L2a", "kv", u))[:, 0:144].rearrange("p (c j d) -> p c j d", c=4, j=4),
                                               m, ALU.mult), ring.free(("L2a", "kv", u)))
                    divide_heads("L2a", add=1e-8)
                    aff = (W["L2a_gamma"][:], W["L2a_beta"][:])
                    add_product(lambda u: ("L2a", "y", u), x_tok)
                    layer_norm(lambda u: qs[:, u, :], aff, S("L2a_x1"))
                    add_product(lambda u: ("L2a", "y2", u), qs)
                    layer_norm(lambda u: qs[:, u, :], aff)
                    each(lambda u: dve.tensor_tensor(res[:, u, :], qs[:, u, :], x_tok[:, u, :], ALU.add))
                    new_x()

                if STAGES_RUN > 7:
                    dve.wait_ge(*weights("L2x"))
                    link(dve.tensor_tensor(bq4[:], const("feat32"), W["L2x_bq"][:].to_broadcast([P, 4]), ALU.mult),
                         S("L2x_bias"))
                    b = ring.bank(("L2x", "k"))
                    dve.wait_ge(*ring.full(("L2x", "k")))
                    for u in range(NS):
                        ins = dve.scalar_tensor_tensor(bd[:, u, :, 0:T], among(b[:, tk(u)], 4), W["L2x_bk"][:],
                                                       over(const("head8in32"), T), ALU.add, ALU.mult)
                        link(ins, ring.free(("L2x", "k")) if u else None)
                    b = ring.bank(("L2x", "v"))
                    dve.wait_ge(*ring.full(("L2x", "v")))
                    for u in range(NS):
                        link(dve.tensor_copy(vaug[:, u, 0, :, 0:8], heads(b[:, u * D:(u + 1) * D], H)),
                             ring.free(("L2x", "v")) if u else None)
                    softmax_units("L2x", 4, T, early_divide("L2x", 4))
                    divide_heads("L2x", slots=[1])
                    post_norm("L2x")

                if STAGES_RUN > 8:
                    swiglu("L2f", "sigmoid")

                if STAGES_RUN > 9:
                    dve.wait_ge(*weights("L3a"))
                    for r in range(2):
                        link(dve.memset(lat_pad[64 - 64 * r:128 - 64 * r, r, :], 0.0), S("L3a_zeros") if r else None)
                    b = ring.bank(("L3a", "v"))
                    dve.wait_ge(*ring.full(("L3a", "v")))
                    for u in range(NS):
                        link(dve.tensor_copy(vaug[:, u, 0, :, 0:8], heads(b[:, u * D:(u + 1) * D], H)),
                             ring.free(("L3a", "v")) if u else None)
                    softmax_units("L3a", 4, T, early_divide("L3a", 4))
                    divide_heads("L3a", slots=[1])
                    post_norm("L3a")

                if STAGES_RUN > 10:
                    dve.wait_ge(*weights("L3x"))
                    g = gateT
                    b = ring.bank(("L3x", "gates"))
                    dve.wait_ge(*ring.full(("L3x", "gates")))
                    link(dve.tensor_scalar(g[0:8, 0, :], b[0:8, 0:NT], W["L3x_ib"][:], None, ALU.add))
                    link(dve.tensor_scalar(g[0:8, 1, :], b[0:8, NT:2 * NT], W["L3x_fb"][:], None, ALU.add),
                         ring.free(("L3x", "gates")))
                    link(dve.scalar_tensor_tensor(g[0:8, 5, :], g[0:8, 1, :], -1.0, g[0:8, 1, :], ALU.mult, ALU.min),
                         S("L3x_absf"))
                    dve.wait_ge(*nth("dve", "L3x_softplus"))
                    link(dve.scalar_tensor_tensor(g[0:8, 1, :], g[0:8, 1, :], 0.0, g[0:8, 5, :], ALU.min, ALU.subtract))
                    ones8 = const("ones", 8)[:, 0:T]
                    for u in range(NS):
                        link(dve.tensor_tensor_scan(g[0:8, 3, tk(u)], ones8, g[0:8, 1, tk(u)], 0.0, ALU.mult, ALU.add))
                    link(dve.tensor_tensor(g[0:8, 2, :], g[0:8, 0, :], g[0:8, 3, :], ALU.subtract))
                    for u in range(NS):
                        link(dve.tensor_tensor_scan(g[0:8, 5, tk(u)], ones8, g[0:8, 2, tk(u)], -3.0e38, ALU.mult, ALU.max))
                    link(dve.tensor_tensor(g[0:8, 4, :], g[0:8, 3, :], g[0:8, 5, :], ALU.add), S("L3x_gates"))
                    for u in range(NS):
                        link(dve.scalar_tensor_tensor(mdiag[:, u], among(g[0:8, 5, tk(u)], 8), -1.0,
                                                      over(const("delta8", 8), T), ALU.mult, ALU.mult))
                        link(dve.tensor_tensor(bd[:, u, :, 0:T], among(xT[:, tk(u)], 4),
                                               over(const("head16in64"), T), ALU.mult), S("L3x_bd"))
                        link(dve.tensor_copy(vaug_c[:, u, :, 0:DC], heads(ctx_tok[:, u, :], HC)))
                    for i in range(4):
                        dve.wait_ge(*ring.full(("L3x", "s", i)))
                        dve.wait_ge(*ring.freed(("L3x", "D", i)))
                        if i >= NPB:
                            dve.wait_ge(*nth("dve", "L3x_used"))
                        link(dve.scalar_tensor_tensor(probsT[:, i % NPB, :], ring.bank(("L3x", "s", i))[:], DC ** -0.5,
                                                      probs[:, i % NPB, :], ALU.mult, ALU.mult), ring.free(("L3x", "s", i)))
                    dve.wait_ge(*ring.freed(("L3x", "mx")))
                    ob = [heads(ring.bank(("L3x", "o", u))[:, 0:HC * 17], HC) for u in range(NS)]
                    for u in range(NS):
                        dve.wait_ge(*ring.full(("L3x", "o", u)))
                    n, m = (lambda u: small[:, u, 0:8]), (lambda u: small[:, u, 8:16])
                    h3 = lambda u: heads(attn[:, u, :], HC)
                    each(lambda u: dve.tensor_copy(n(u), ob[u][:, :, DC]))
                    each(lambda u: dve.scalar_tensor_tensor(n(u), n(u), -1.0, n(u), ALU.mult, ALU.max))
                    each(lambda u: dve.tensor_tensor(n(u), n(u), small2[:, u, 32:40], ALU.max))
                    each(lambda u: dve.tensor_scalar(n(u), n(u), 1e-6, None, ALU.add))
                    each(lambda u: dve.reciprocal(n(u), n(u)))
                    each(lambda u: dve.tensor_tensor(h3(u), ob[u][:, :, 0:DC], over(n(u), DC), ALU.mult),
                         lambda u: ring.free(("L3x", "o", u)))
                    each(lambda u: dve.tensor_reduce(m(u), h3(u), X, ALU.add))
                    each(lambda u: dve.tensor_scalar(m(u), m(u), 1.0 / DC, None, ALU.mult))
                    each(lambda u: dve.tensor_tensor(h3(u), h3(u), over(m(u), DC), ALU.subtract))
                    each(lambda u: dve.tensor_tensor(qs[:, u, :], attn[:, u, :], attn[:, u, :], ALU.mult))
                    each(lambda u: dve.tensor_reduce(small[:, u, 16:24], heads(qs[:, u, :], HC), X, ALU.add), S("L3x_var"))
                    for u in range(NS):
                        dve.wait_ge(*nth("dve", "L3x_rstd"))
                        o.count(dve.tensor_tensor(h3(u), h3(u), over(small[:, u, 24:32], DC), ALU.mult))
                    o.settle()
                    each(lambda u: dve.tensor_tensor(attn[:, u, :], attn[:, u, :], W["L3x_w"][:], ALU.mult))
                    each(lambda u: dve.tensor_tensor(res[:, u, :], attn[:, u, :], x_tok[:, u, :], ALU.add))
                    new_x()

                link(dve.tensor_copy(x_all[:, bass.ds(pair * NS, NS), :], x_tok[:]))

            @block.scalar
            def _(eng):
                o = Order(act, "act")
                link, each = o.link, o.each
                eps5, eps6, one, _z = (const("eps")[:, i:i + 1] for i in range(4))

                def inv_sqrt(dst, src, tmp, eps, scale=1.0, told=None):
                    link(act.activation(tmp, src, ACT.Ln, bias=eps[0:src.shape[0]], scale=scale))
                    link(act.activation(dst, tmp, ACT.Exp, scale=-0.5), told)

                def norm_rstd():
                    for u in range(NS):
                        act.wait_ge(*nth("act", "var_ready"))
                        o.count(act.activation(lnv[:, u, :], mv[:, u, 1:2], ACT.Ln, bias=eps5))
                    o.settle()
                    each(lambda u: act.activation(rstd[:, u, :], lnv[:, u, :], ACT.Exp, scale=-0.5), S("rstd_ready"))

                def keep_xT(st):
                    for u in range(NS):
                        act.wait_ge(*ring.full(("xT", st, u)))
                        link(act.copy(xT[:, tk(u)], ring.bank(("xT", st, u))[:, 0:T]), ring.free(("xT", st, u)))

                def attnT_copy(st, slots=range(NS)):
                    for u in slots:
                        act.wait_ge(*ring.full((st, "aT", u)))
                        link(act.copy(attnT[:, u, :], ring.bank((st, "aT", u))[:, 0:T]), ring.free((st, "aT", u)))

                def softmax_units(st, n_units, scale):
                    total = NS * n_units
                    for step in range(total + 2):
                        if step < total:
                            i = step
                            act.wait_ge(*ring.freed((st, "s", i)))
                            link(act.activation(probs[:, i % NPB, :], probs[:, i % NPB, :], ACT.Exp, scale=scale),
                                 S("probs_ready"))
                        i = step - 2
                        if 0 <= i < total:
                            act.wait_ge(*ring.full((st, "pT", i)))
                            link(act.copy(probsT[:, i % NPB, :], ring.bank((st, "pT", i))[:]), ring.free((st, "pT", i)))
                        if (st, "aT", 0) in ring.at and step == n_units + 5:
                            attnT_copy(st, [0])

                def to_sbuf(key, dst, bias=None, shape=None):
                    src = ring.bank(key)[:]
                    act.wait_ge(*ring.full(key))
                    src = src[:, 0:NT] if shape is None else shape(src)
                    if bias is None:
                        link(act.copy(dst, src), ring.free(key))
                    else:
                        link(act.activation(dst, src, ACT.Identity, bias=bias), ring.free(key))

                def to_pad4(key, tokens, n, bias=None):
                    act.wait_ge(*ring.full(key))
                    for c in range(4):
                        ins = act.activation(pad4[:, c, tokens], ring.bank(key)[:, 0:n], ACT.Identity,
                                             scale=const("feat32")[:, c:c + 1],
                                             **({} if bias is None else {"bias": bias[:, c:c + 1]}))
                        link(ins, ring.free(key) if c == 3 else None)

                act.preload_act_table_set(EXP_LN)

                if STAGES_RUN > 0:
                    for u in range(NS):
                        act.wait_ge(*ring.full(("L0a", "k", u)))
                        link(act.activation(ks[:, u, :], ring.bank(("L0a", "k", u))[:, 0:D], ACT.Exp),
                             ring.free(("L0a", "k", u)))
                        act.wait_ge(*ring.freed(("L0a", "qv", u)))
                        link(act.activation(qs[:, u, :], qs[:, u, :], ACT.Exp), S("L0a_expq"))
                    for u in range(NS):
                        to_sbuf(("L0a", "qsT", u), qT[:, 0, tk(u)], shape=lambda s: s[:, 0:T])
                    attnT_copy("L0a")
                    norm_rstd()
                    keep_xT(0)
                if STAGES_RUN > 1:
                    to_pad4(("L0x", "q"), slice(0, NT), NT)
                    softmax_units("L0x", 8, DH ** -0.5)
                    attnT_copy("L0x", [1])
                    norm_rstd()
                    keep_xT(1)

                def gates_exp(scale):
                    act.wait_ge(*nth("act", "gates_in"))
                    pr = small2[:, :, 16:24]
                    link(act.activation(pr, pr, ACT.Exp, scale=scale), S("gates_exp"))

                def swiglu(st, scale):
                    gates_exp(scale)
                    for i in range(18):
                        act.wait_ge(*ring.full((st, "up", i)))
                        if i >= NHB:
                            act.wait_ge(*ring.freed((st, "up", i - NHB)))
                        link(act.activation(gact[:, i % NHB, 0:NT], ring.bank((st, "up", i))[:, 0:NT], ACT.Silu),
                             S("gact_ready"))
                    act.preload_act_table_set(EXP_LN)
                    norm_rstd()

                if STAGES_RUN > 2:
                    swiglu("L0f", 1.0)
                    keep_xT(2)

                if STAGES_RUN > 3:
                    act.wait_ge(*nth("act", "L1a_negbb"))
                    act.wait_ge(*ring.full(("L1a", "beta")))
                    link(act.activation(gateT[0:H, 0, :], ring.bank(("L1a", "beta"))[0:H, 0:NT], ACT.Exp,
                                        bias=neg_bb[:], scale=-1.0), ring.free(("L1a", "beta")))
                    for c in range(0, 8, 2):
                        to_sbuf(("L1x", f"k{c}"), k64[:, c:c + 2, :], shape=lambda s: heads(s, 2))
                    for u in range(NS):
                        act.wait_ge(*nth("act", "L1a_min"))
                        link(act.activation(qk3[:, u], qk3[:, u], ACT.Exp), S("L1a_exp"))
                    for u in range(NS):
                        to_pad4(("L1a", "kT", u), tk(u), T)
                    attnT_copy("L1a")
                    for u in range(NS):
                        act.wait_ge(*nth("act", "ms_ready"))
                        inv_sqrt(rstd[:, u, :], mv[:, u, 1:2], lnv[:, u, :], eps6, scale=1.0 / D, told=S("rstd_ready"))
                    norm_rstd()
                    keep_xT(3)

                if STAGES_RUN > 4:
                    for c in range(0, 8, 2):
                        to_sbuf(("L1x", f"q{c}"), q64[:, c:c + 2, :], shape=lambda s: heads(s, 2))
                    softmax_units("L1x", 4, R ** -0.5)
                    for u in range(NS):
                        for c in range(0, 8, 4):
                            to_sbuf(("L1x", "aT", u, c), attn64T[:, u, c:c + 4, :], shape=lambda s: heads(s, 4))
                    norm_rstd()
                    keep_xT(4)

                if STAGES_RUN > 5:
                    gates_exp(1.0)
                    for i in range(16):
                        act.wait_ge(*ring.full(("L1f", "up", i)))
                        if i >= NHB:
                            act.wait_ge(*ring.full(("L1f", "y", (i - NHB) // 2)))
                        link(act.activation(hT[:, i % NHB, :], ring.bank(("L1f", "up", i))[:], ACT.Gelu_apprx_tanh),
                             ring.free(("L1f", "up", i)))
                    act.preload_act_table_set(EXP_LN)
                    norm_rstd()
                    keep_xT(5)

                if STAGES_RUN > 6:
                    to_sbuf(("L2a", "qk"), qT[:], shape=lambda s: heads(s, 2))
                    for i in range(4):
                        act.wait_ge(*nth("act", "L2a_min"))
                        link(act.activation(gact[:, i, :], gact[:, i, :], ACT.Exp), S("L2a_exp"))
                    attnT_copy("L2a")
                    norm_rstd()
                    for u in range(NS):
                        to_sbuf(("L2a", "x1T", u), kT[:, tk(u)], shape=lambda s: s[:, 0:T])
                    act.preload_act_table_set("gelu_and_others")
                    for c in range(4):
                        key = ("L2a", f"h{c // 2 * 2}")
                        act.wait_ge(*ring.full(key))
                        half = slice((c % 2) * NT, (c % 2 + 1) * NT)
                        ins = act.activation(gact[:, c // 2, half], ring.bank(key)[:, half], ACT.Gelu,
                                             bias=W["L2a_b1"][:, c:c + 1])
                        link(ins, ring.free(key) if c % 2 else None)
                    act.preload_act_table_set(EXP_LN)
                    norm_rstd()
                    norm_rstd()
                    keep_xT(6)

                if STAGES_RUN > 7:
                    act.wait_ge(*nth("act", "L2x_bias"))
                    to_pad4(("L2x", "q"), slice(0, NT), NT, bias=bq4)
                    softmax_units("L2x", 4, DH ** -0.5)
                    attnT_copy("L2x", [1])
                    norm_rstd()
                    keep_xT(7)

                if STAGES_RUN > 8:
                    swiglu("L2f", -1.0)
                    keep_xT(8)

                if STAGES_RUN > 9:
                    act.wait_ge(*nth("act", "L3a_zeros"))
                    act.wait_ge(*ring.full(("L3a", "lat")))
                    for r in range(2):
                        rows = slice(64 * r, 64 * r + 64)
                        link(act.copy(lat_pad[rows, r, :], ring.bank(("L3a", "lat"))[rows, 0:NT]),
                             ring.free(("L3a", "lat")) if r else None)
                    for c in range(0, 8, 2):
                        to_sbuf(("L3a", f"q{c}"), q64[:, c:c + 2, :], shape=lambda s: heads(s, 2))
                    softmax_units("L3a", 4, R ** -0.5)
                    attnT_copy("L3a", [1])
                    norm_rstd()
                    keep_xT(9)

                if STAGES_RUN > 10:
                    act.wait_ge(*nth("act", "L3x_absf"))
                    link(act.activation(gateT[0:8, 5, :], gateT[0:8, 5, :], ACT.Exp))
                    link(act.activation(gateT[0:8, 5, :], gateT[0:8, 5, :], ACT.Ln, bias=one[0:8]), S("L3x_softplus"))
                    act.wait_ge(*ring.full(("L3x", "mx")))
                    link(act.activation(small2[:, :, 32:40], ring.bank(("L3x", "mx"))[:, 0:16].rearrange("p (u h) -> p u h", u=2),
                                        ACT.Exp, scale=-1.0))
                    link(act.copy(a_tok[:], ring.bank(("L3x", "mx"))[:, 16:32].rearrange("p (u h) -> p u h", u=2)),
                         ring.free(("L3x", "mx")))
                    for i in range(4):
                        act.wait_ge(*ring.full(("L3x", "D", i)))
                        if i >= NPB:
                            act.wait_ge(*ring.freed(("L3x", "s", i - NPB)))
                        for j in range(4):
                            cols = slice(j * T, j * T + T)
                            ins = act.activation(probs[:, i % NPB, cols], ring.bank(("L3x", "D", i))[:, cols], ACT.Exp,
                                                 bias=a_tok[:, i // 2, 4 * (i % 2) + j:4 * (i % 2) + j + 1])
                            link(ins, ring.free(("L3x", "D", i)) if j == 3 else None)
                    for u in range(NS):
                        act.wait_ge(*nth("act", "L3x_var"))
                        inv_sqrt(small[:, u, 24:32], small[:, u, 16:24], small[:, u, 32:40], eps6, scale=1.0 / DC,
                                 told=S("L3x_rstd"))
                    norm_rstd()
                    for u in range(NS):
                        act.wait_ge(*ring.full(("xT", 10, u)))
                        link(act.copy(xT_all[:, bass.ds(pair * NT + u * T, T)], ring.bank(("xT", 10, u))[:, 0:T]),
                             ring.free(("xT", 10, u)))

            @block.sync
            def _(eng):
                def load_next(name):
                    sp.dma_start(inputs[name][:], dram[name][pair + 1]).then_inc(S("next_in"), 16)

                sp.wait_ge(*ring.freed(("L0a", "y", 0)))
                sp.wait_ge(*ring.freed(("L0a", "y", 1)))
                load_next("x_tok")
                if STAGES_RUN > 8:
                    for done, st in (("L0f", "L2f"), ("L2f", "L0f")):
                        sp.wait_ge(*ring.full((done, "y", 8)))
                        sp.dma_start(group_tile[st + "_experts"][:], dram[st + "_experts"]).then_inc(S(st + "_in"), 16)
                if STAGES_RUN > 10:
                    sp.wait_ge(*ring.full(("L3x", "gates")))
                    sp.wait_ge(S("L3x_bd"), NS)
                    load_next("xT")
                    sp.wait_ge(*ring.freed(("L3x", "s", 0)))
                    load_next("ctx_tok")
                    sp.wait_ge(*ring.full(("L3x", "s", 3)))
                    load_next("ctxT")
                    sp.wait_ge(S("next_in"), len(inputs) * 16)
                if STAGES_RUN > 8:
                    sp.wait_ge(S("L0f_in"), 16)

        with nc.Block(name="reset") as block:
            @block.sync
            def _(eng):
                nums = sorted(s.num for s in sems.values())
                assert nums == list(range(nums[0], nums[-1] + 1))
                sp.sem_clear(range(nums[0], nums[-1] + 1))

    amax = sb("amax", [P, 4])
    q_in = k64[:, 0:4, :].rearrange("p c t -> p (c t)")
    q_bf = sb("q_bf", [P, B * T], BF16)
    w_bf = sb("w_bf", [P, D], BF16)
    y_all = q64[:, 0:4, :].rearrange("p c t -> p (c t)").rearrange("p (b d) -> p b d", b=B)
    stats8 = sb("stats8", [P, B, 6])
    mv8 = sb("mv8", [P, B, 2])
    rstd8 = sb("rstd8", [P, B])
    fin = {n: ctx.enter_context(nc.semaphore(f"ffn_{n}")) for n in
           ("partial", "turned", "whole", "spread", "operands", "products", "var", "rstd", "normed")}
    fin_step = ctx.enter_context(nc.semaphore("ffn_dve_step"))
    fin_act = ctx.enter_context(nc.semaphore("ffn_act_step"))
    ROUND = float(1.5 * 2 ** 23)

    with nc.Block(name="last_ffn") as block:
        @block.tensor
        def _(eng):
            pe.wait_ge(fin["partial"], 2)
            pe.matmul(psum[1][:, 0:1], const("ones")[:, 0:P], amax[:, 1:2], start=True, stop=True)
            pe.transpose(psum[0][0:1, 0:P], amax[:, 0:1], IDENT).then_inc(fin["turned"], 1)
            pe.wait_ge(fin["whole"], 1)
            pe.matmul(psum[2][:, 0:1], ones_row, amax[0:1, 2:3], start=True, stop=True).then_inc(fin["spread"], 1)
            pe.wait_ge(fin["operands"], 1)
            for b in range(B):
                m = pe.matmul(psum[3 + b // 4][:, b % 4 * D:b % 4 * D + D], q_bf[:, b * T:(b + 1) * T], w_bf[:],
                              start=True, stop=True)
                if b % 4 == 3:
                    m.then_inc(fin["products"], 1)

        @block.vector
        def _(eng):
            link = Order(dve, "ffn").link
            st = fin_step
            dve.wait_ge(*weights("L3f"))
            link(dve.tensor_reduce(amax[:, 0:1], xT_all[:], X, ALU.max, apply_absolute_value=True), fin["partial"])
            link(dve.tensor_reduce(amax[:, 1:2], W["L3f_w"][:], X, ALU.add, apply_absolute_value=True), fin["partial"])
            link(dve.tensor_tensor(x_all[:], x_all[:], among(W["L3f_b"][:], B), ALU.add), st)
            dve.wait_ge(fin["turned"], 1)
            link(dve.tensor_reduce(amax[0:1, 2:3], psum[0][0:1, 0:P], X, ALU.max), fin["whole"])
            dve.wait_ge(fin["spread"], 1)
            s = small[:, 0, :]
            link(dve.tensor_scalar(s[:, 0:1], psum[2][:, 0:1], 1.0 / 127.0, None, ALU.mult), st)
            link(dve.reciprocal(s[:, 1:2], s[:, 0:1]), st)
            link(dve.tensor_scalar(s[:, 2:3], psum[1][:, 0:1], 1.0 / (D * D), None, ALU.mult), st)
            link(dve.tensor_scalar(s[:, 3:4], s[:, 2:3], 0.5, None, ALU.mult), st)
            link(dve.tensor_scalar(s[:, 4:5], s[:, 2:3], -0.5, None, ALU.mult), st)
            link(dve.tensor_tensor(s[:, 5:6], s[:, 2:3], s[:, 0:1], ALU.mult), st)
            link(dve.tensor_scalar(qs[:, 0, :], W["L3f_w"][:], s[:, 3:4], None, ALU.is_gt), st)
            link(dve.tensor_scalar(qs[:, 1, :], W["L3f_w"][:], s[:, 4:5], None, ALU.is_lt), st)
            link(dve.tensor_tensor(w_bf[:], qs[:, 0, :], qs[:, 1, :], ALU.subtract), st)
            link(dve.tensor_scalar(q_in, xT_all[:], s[:, 1:2], ROUND, ALU.mult, ALU.add), st)
            link(dve.tensor_scalar(q_in, q_in, ROUND, 127.0, ALU.subtract, ALU.min), st)
            link(dve.tensor_scalar(q_bf[:], q_in, -128.0, None, ALU.max), fin["operands"])
            for g in range(2):
                dve.wait_ge(fin["products"], g + 1)
                xs = x_all[:, 4 * g:4 * g + 4, :].rearrange("p b d -> p (b d)")
                link(dve.scalar_tensor_tensor(xs, psum[3 + g][:], s[:, 5:6], xs, ALU.mult, ALU.add), st)
            for b in range(B):
                link(dve.bn_stats(stats8[:, b, :], x_all[:, b, :]), st)
                link(dve.bn_aggr(mv8[:, b, :], stats8[:, b, :]), fin["var"])
            dve.wait_ge(fin["rstd"], 1)
            for b in range(B):
                link(dve.tensor_scalar(y_all[:, b, :], x_all[:, b, :], mv8[:, b, 0:1], rstd8[:, b:b + 1],
                                       ALU.subtract, ALU.mult), fin["normed"])

        @block.scalar
        def _(eng):
            act.preload_act_table_set(EXP_LN)
            act.wait_ge(fin["var"], B)
            act.activation(rstd8[:], mv8[:, :, 1], ACT.Ln, bias=const("eps")[:, 0:1]).then_inc(fin_act, 1)
            act.wait_ge(fin_act, 1)
            act.activation(rstd8[:], rstd8[:], ACT.Exp, scale=-0.5).then_inc(fin["rstd"], 1)

        @block.sync
        def _(eng):
            for g in w_in:
                sp.wait_ge(*weights(g))
            sp.wait_ge(fin["normed"], B)
            sp.dma_start(out.rearrange("b t d -> t b d"), y_all).then_inc(stored, 16)
            sp.wait_ge(stored, 16)


def layouts(i):
    def rows(v):
        return np.broadcast_to(v.reshape(1, -1), (P, v.size))

    def chunks(w):
        return w.reshape(-1, P, w.shape[-1]).transpose(1, 0, 2).reshape(P, -1)

    def experts_in(*w):
        return np.concatenate(w, axis=0).transpose(1, 0, 2).reshape(P, -1)

    def experts_out(*w):
        w = np.concatenate(w, axis=0)
        return chunks(w.reshape(-1, D))

    proj = np.zeros((H, DH, H, 32), np.float32)
    proj[np.arange(H), :, np.arange(H), :] = i["L2_attn_proj"]
    g = np.stack([i["L3_xattn_igate_kernel"], i["L3_xattn_fgate_kernel"]], axis=1)
    t = np.swapaxes
    return {
        "con_sts": shape_constants(),
        "L0a_qkv": i["L0_attn_W_qkv"].T, "L0a_o": i["L0_attn_W_out"].T,
        "L0x_q": i["L0_xattn_Wq"], "L0x_kv": i["L0_xattn_Wkv"], "L0x_o": i["L0_xattn_Wout"],
        "L0x_bo": i["L0_xattn_bout"][None],
        "L0f_gate": i["L0_ffn_gate_w"].T, "L0f_gb": rows(i["L0_ffn_gate_bias"]),
        "L0f_w1": experts_in(i["L0_ffn_sw1"].T[None], t(i["L0_ffn_w1"], 1, 2)),
        "L0f_w3": experts_in(i["L0_ffn_sw3"].T[None], t(i["L0_ffn_w3"], 1, 2)),
        "L0f_w2": experts_out(i["L0_ffn_sw2"].T[None], t(i["L0_ffn_w2"], 1, 2)),
        "L1a_qkv": np.concatenate([i["L1_attn_Wq"].T, i["L1_attn_Wk"].T, i["L1_attn_Wv"].T], axis=1),
        "L1a_b": i["L1_attn_Wb"].T, "L1a_bb": i["L1_attn_bb"][:, None], "L1a_o": i["L1_attn_Wo"].T,
        "L1a_bo": i["L1_attn_bo"][None], "L1a_scale": rows(i["L1_attn_scale"]),
        "L1x_q": i["L1_xattn_w_q"], "L1x_kv": i["L1_xattn_w_kv"], "L1x_o": chunks(i["L1_xattn_w_out"]),
        "L1x_bo": i["L1_xattn_b_out"][None],
        "L1f_gate": i["L1_ffn_gate_w"], "L1f_w1": experts_in(i["L1_ffn_w1"]), "L1f_w2": experts_out(i["L1_ffn_w2"]),
        "L2a_qkv": i["L2_attn_w_qkv"].T, "L2a_proj": proj.reshape(P, H * 32), "L2a_o": i["L2_attn_w_out"].T,
        "L2a_bo": i["L2_attn_b_out"][None], "L2a_gamma": rows(i["L2_attn_gamma"]), "L2a_beta": rows(i["L2_attn_beta"]),
        "L2a_w1": i["L2_attn_w1"].T, "L2a_b1": i["L2_attn_b1"].reshape(4, P).T, "L2a_w2": chunks(i["L2_attn_w2"].T),
        "L2a_b2": i["L2_attn_b2"][None],
        "L2x_q": i["L2_xattn_Wq"], "L2x_k": i["L2_xattn_Wk"], "L2x_v": i["L2_xattn_Wv"], "L2x_o": i["L2_xattn_Wo"],
        "L2x_bq": i["L2_xattn_bq"][:, None], "L2x_bk": i["L2_xattn_bk"][:, None], "L2x_bv": i["L2_xattn_bv"][None],
        "L2x_bo": i["L2_xattn_bo"][None],
        "L2f_gate": i["L2_ffn_gate_w"].T, "L2f_gb": rows(i["L2_ffn_beta"]),
        "L2f_w1": experts_in(i["L2_ffn_shared_gate_w"], i["L2_ffn_gate_proj_w"]),
        "L2f_w3": experts_in(i["L2_ffn_shared_up_w"], i["L2_ffn_up_proj_w"]),
        "L2f_w2": experts_out(i["L2_ffn_shared_down_w"], i["L2_ffn_down_proj_w"]),
        "L3a_basis": np.concatenate([i["L3_attn_basis_w"].T] * 2, axis=1), "L3m_core": i["L3_attn_core"],
        "L3m_coreT": i["L3_attn_core"].T, "L3m_mats": i["L3_attn_head_residual"].transpose(1, 0, 2).reshape(R, H * R),
        "L3a_v": i["L3_attn_v_w"].T, "L3a_vb": i["L3_attn_v_b"][None], "L3a_o": i["L3_attn_o_w"].T,
        "L3a_bo": i["L3_attn_o_b"][None],
        "L3x_gates": chunks(g.reshape(3 * P, 16)), "L3x_ib": i["L3_xattn_igate_bias"][:, None],
        "L3x_fb": i["L3_xattn_fgate_bias"][:, None], "L3x_w": rows(i["L3_xattn_outnorm_weight"]),
        "L3f_w": i["L3_ffn_weight"].T, "L3f_b": rows(i["L3_ffn_bias"]),
    }


def kernel(**inputs):
    import concourse.bacc as bacc
    from concourse.bass_utils import run_bass_kernel_spmd

    i = {n: np.asarray(v) for n, v in inputs.items()}
    laid = layouts(i)
    arrays = {g: np.zeros((P, group_words(g)), np.float32) for g in GROUPS}
    for g, members in GROUPS.items():
        for n, (p, a, e) in members.items():
            assert laid[n].shape == (p, e - a) and laid[n].dtype == np.float32, (n, laid[n].shape)
            arrays[g][0:p, a:e] = laid[n]
    for n, v in (("x", i["x"]), ("ctx", i["ctx_1024"])):
        pairs = v.reshape(B // NS, NS, T, D)
        arrays[f"{n}_tok"] = np.ascontiguousarray(pairs.transpose(0, 2, 1, 3))
        arrays[f"{n}T"] = np.ascontiguousarray(pairs.transpose(0, 3, 1, 2).reshape(B // NS, D, NT))
    for n in ("x_tok", "xT", "ctx_tok", "ctxT"):
        arrays[n] = np.concatenate([arrays[n], arrays[n][:1]])

    nc = bacc.Bacc("TRN2", target_bir_lowering=False, num_devices=1)
    arrays = {f"in_{n}": a for n, a in arrays.items()}
    dram = {n[3:]: nc.dram_tensor(n, a.shape, F32, kind="ExternalInput").ap() for n, a in arrays.items()}
    out = nc.dram_tensor("y", (B, T, D), F32, kind="ExternalOutput").ap()
    build(nc, dram, out)
    r = run_bass_kernel_spmd(nc, [arrays], core_ids=[0])
    return r.results[0]["y"]
```

```python
from contextlib import ExitStack

import numpy as np

import concourse.bass as bass
from concourse import mybir

F32 = mybir.dt.float32
BF16 = mybir.dt.bfloat16
ACT = mybir.ActivationFunctionType
ALU = mybir.AluOpType
X = mybir.AxisListType.X

P = 128
T = 128
D = 128
B = 8
NS = 2
NT = NS * T
H = 16
DH = D // H
HC = 8
DC = D // HC
R = 64
E = 8
BANK = 512
EXP_LN = "natural_log_exp_and_others"
NEG = -float(2 ** 100)
WARM = {
    "new_x": 9,
    "new_x_filled": 5,
    "xT": 3,
    "attn": (4, 1),
    "attnT": (2, 0),
    "drain": 4,
    "decay": 6, "rms": 8, "rotated": 3, "keys": 4,
    "features": 2, "inner_x": 9, "norms": 14,
    "latent": 2,
    "gates": 13, "head_norms": 20,
}

CONST = {}
_at = 0
for _n, _w in [("ident", 128), ("neg_causal", 128), ("neg_causal_t", 128), ("causal_t", 128),
               ("head8", 16), ("head8in32", 4), ("head16in64", 4), ("feat32", 4), ("late", 1),
               ("cos", 8), ("sin", 8), ("delta8", 8), ("ones", 128), ("eps", 4)]:
    CONST[_n] = (_at, _w)
    _at += _w
NCONST = _at


def shape_constants():
    c = np.zeros((P, NCONST), np.float32)
    p = np.arange(P)

    def put(name, v):
        a, w = CONST[name]
        c[:v.shape[0], a:a + w] = v.reshape(v.shape[0], w)

    put("ident", np.eye(P, dtype=np.float32))
    put("neg_causal", np.where(p[None, :] > p[:, None], NEG, 0).astype(np.float32))
    put("neg_causal_t", np.where(p[:, None] > p[None, :], NEG, 0).astype(np.float32))
    put("causal_t", (p[:, None] <= p[None, :]).astype(np.float32))
    put("head8", (p[:, None] // 8 == np.arange(16)).astype(np.float32))
    put("head8in32", (p[:, None] % 32 // 8 == np.arange(4)).astype(np.float32))
    put("head16in64", (p[:, None] % 64 // 16 == np.arange(4)).astype(np.float32))
    put("feat32", (p[:, None] // 32 == np.arange(4)).astype(np.float32))
    put("late", (p[:, None] >= 64).astype(np.float32))
    inv = np.float32(1.0) / np.float32(10000.0) ** (np.arange(0, 8, 2, dtype=np.float32) / np.float32(8))
    ang = np.concatenate([p.astype(np.float32)[:, None] * inv[None, :]] * 2, axis=1)
    sin = np.sin(ang)
    sin[:, :4] *= -1
    put("cos", np.cos(ang))
    put("sin", sin)
    put("delta8", np.eye(8, dtype=np.float32))
    put("ones", np.ones((P, 128), np.float32))
    put("eps", np.tile(np.array([1e-5, 1e-6, 1.0, 0.0], np.float32), (P, 1)))
    return c


WEIGHTS = [
    ("con_sts", P, NCONST), ("L3m_core", R, 64), ("L3m_coreT", R, 64), ("L3m_mats", R, 1024),
    ("L0a_qkv", P, 384), ("L0a_o", P, 128),
    ("L0x_q", P, 128), ("L0x_kv", P, 256), ("L0x_o", P, 128), ("L0x_bo", 1, 128),
    ("L0f_gate", P, 8), ("L0f_gb", P, 8), ("L0f_w1", P, 9 * 256), ("L0f_w3", P, 9 * 256), ("L0f_w2", P, 9 * 256),
    ("L1a_qkv", P, 384), ("L1a_b", P, 16), ("L1a_bb", 16, 1), ("L1a_o", P, 128), ("L1a_bo", 1, 128),
    ("L1a_scale", P, 128),
    ("L1x_q", P, 1024), ("L1x_kv", P, 2048), ("L1x_o", P, 1024), ("L1x_bo", 1, 128),
    ("L1f_gate", P, 8), ("L1f_w1", P, 8 * 512), ("L1f_w2", P, 8 * 512),
    ("L2a_qkv", P, 384), ("L2a_proj", P, 512), ("L2a_o", P, 128), ("L2a_bo", 1, 128),
    ("L2a_gamma", P, 128), ("L2a_beta", P, 128), ("L2a_w1", P, 512), ("L2a_b1", P, 4), ("L2a_w2", P, 512),
    ("L2a_b2", 1, 128),
    ("L2x_q", P, 128), ("L2x_k", P, 128), ("L2x_v", P, 128), ("L2x_o", P, 128),
    ("L2x_bq", P, 1), ("L2x_bk", P, 1), ("L2x_bv", 1, 128), ("L2x_bo", 1, 128),
    ("L2f_gate", P, 8), ("L2f_gb", P, 8), ("L2f_w1", P, 9 * 256), ("L2f_w3", P, 9 * 256), ("L2f_w2", P, 9 * 256),
    ("L3a_basis", P, 128), 
    ("L3a_v", P, 128), ("L3a_vb", 1, 128), ("L3a_o", P, 128), ("L3a_bo", 1, 128),
    ("L3x_gates", P, 3 * 16), ("L3x_ib", 8, 1), ("L3x_fb", 8, 1), ("L3x_w", P, 128),
    ("L3f_w", P, 128), ("L3f_b", P, 128),
]


SWAPPED = ("w1", "w3", "w2")


def group_of(name):
    st, w = name.split("_")
    return st + "_experts" if st in ("L0f", "L2f") and w in SWAPPED else st


GROUPS = {}
for _n, _p, _w in WEIGHTS:
    _g = GROUPS.setdefault(group_of(_n), {})
    _at = max((e for _, _, e in _g.values()), default=0)
    _g[_n] = (_p, _at, _at + _w)


def group_words(g):
    return max(e for _, _, e in GROUPS[g].values())


def build(nc, dram, out):
    with ExitStack() as ctx:
        _build(nc, ctx, dram, out)


def _build(nc, ctx, dram, out):
    def sb(name, shape, dt=F32):
        return ctx.enter_context(nc.sbuf_tensor(name, shape, dt))

    pe, dve, act, sp = nc.tensor, nc.vector, nc.scalar, nc.sync

    group_tile, w_in = {}, {}
    for g in GROUPS:
        if g != "L2f_experts":
            group_tile[g] = sb("weights_" + g, [P, group_words(g)])
            w_in[g] = ctx.enter_context(nc.semaphore("weights_in_" + g))
    group_tile["L2f_experts"] = group_tile["L0f_experts"]
    W = {n: group_tile[g][0:p, a:e] for g, members in GROUPS.items() for n, (p, a, e) in members.items()}
    head_mats = W["L3m_mats"]

    def weights(prefix):
        return w_in[prefix], 16

    def const(name, rows=P):
        a, w = CONST[name]
        return W["con_sts"][0:rows, a:a + w]

    IDENT = const("ident")
    ident_bf = sb("ident_bf", [P, P], BF16)
    neg_wide_bf = sb("neg_wide_bf", [P, 2 * P], BF16)
    neg_causal_bf = neg_wide_bf[:, P:2 * P]
    neg_causal_t_bf = sb("neg_causal_t_bf", [P, P], BF16)
    ones_row = const("ones", 1)[:, 0:128]
    core_sym = sb("core_sym", [R, R])
    res_mean = sb("res_mean", [R, R])
    neg_bb = sb("neg_bb", [H, 1])
    a_tok = sb("a_tok", [P, NS, HC])

    x_tok = sb("x_tok", [P, NS, D])
    xT = sb("xT", [P, NT])
    ctx_tok = sb("ctx_tok", [P, NS, D])
    ctxT = sb("ctxT", [P, NT])
    x_raw = sb("x_raw", [P, NS, D])
    inputs = {"xT": xT, "x_tok": x_raw, "ctxT": ctxT, "ctx_tok": ctx_tok}
    x_all = sb("x_all", [P, B, D])
    xT_all = sb("xT_all", [P, B * T])

    res = sb("res", [P, NS, D])
    stats = sb("stats", [P, NS, 6])
    mv = sb("mv", [P, NS, 2])
    lnv = sb("lnv", [P, NS, 1])
    rstd = sb("rstd", [P, NS, 1])
    qs = sb("qs", [P, NS, D])
    ks = sb("ks", [P, NS, D])
    qk2 = sb("qk2", [P, NS, 2, D])
    qk3 = sb("qk3", [P, NS, 2, D])
    zeros = sb("zeros", [H, T])
    qT = sb("qT", [P, 2, NT])
    kT = sb("kT", [P, NT])
    share_a = sb("share_a", [P, NS * H * (R + 1)])
    bd = share_a[:, 0:NS * 4 * 2 * T].rearrange("p (u j t) -> p u j t", u=NS, j=4)
    vaug_r = share_a[:].rearrange("p (u h d) -> p u h d", u=NS, h=H)
    small = sb("small", [P, NS, 64])
    small2 = sb("small2", [P, NS, 64])
    vaug = sb("vaug", [P, NS, 2, H, DH + 1])
    vaug_c = sb("vaug_c", [P, NS, HC, DC + 1])
    ctxbd = sb("ctxbd", [P, NS, H, DH + 1])
    attn = sb("attn", [P, NS, D])
    attnT = sb("attnT", [P, NS, D])
    NPB = 3
    probs = sb("probs", [P, NPB, BANK])
    probsT = sb("probsT", [P, NPB, BANK])
    q64 = sb("q64", [P, 8, NT])
    k64 = sb("k64", [P, 8, NT])
    NHB = 4
    gact = sb("gact", [P, NHB, BANK])
    hT = sb("hT", [P, NHB, BANK])
    attn64 = gact[:].rearrange("p b (c r d) -> p (b c) r d", c=4, r=2).rearrange("p (u c) r d -> p u c r d", u=NS)
    attn64T = hT[:].rearrange("p b (c t) -> p (b c) t", c=4).rearrange("p (u c) t -> p u c t", u=NS)
    feats_q = q64
    pad4 = q64[:, 0:4, :]
    lat_pad = k64[:, 0:2, :]
    bq4 = sb("bq4", [P, 4])
    gateT = sb("gateT", [H, 6, NT])
    mdiag = k64[0:8].rearrange("p (u h) (a t) -> p u (h a) t", u=NS, a=2)

    psum = [ctx.enter_context(nc.psum_tensor(f"bank{i}", [P, BANK], F32)) for i in range(8)]

    setup_dve = ctx.enter_context(nc.semaphore("setup_dve"))
    first_in = ctx.enter_context(nc.semaphore("first_in"))
    stored = ctx.enter_context(nc.semaphore("stored"))

    sems = {}

    def S(name):
        if name not in sems:
            sems[name] = ctx.enter_context(nc.semaphore(name))
        return sems[name]

    counted = {}

    def nth(eng, name, n=1):
        counted[eng, name] = counted.get((eng, name), 0) + n
        return S(name), counted[eng, name]

    class Ring:

        def __init__(self):
            self.fills = [0] * 8
            self.frees = [{"dve": 0, "act": 0} for _ in range(8)]
            self.last = [None] * 8
            self.at = {}
            self.n = 0

        def open(self, key, by, bank=None):
            if bank is None:
                bank, self.n = self.n % 6, self.n + 1
            if self.last[bank]:
                pe.wait_ge(S(f"bank{bank}_freed_{self.last[bank]}"), self.frees[bank][self.last[bank]])
            self.fills[bank] += 1
            self.frees[bank][by] += 1
            self.last[bank] = by
            assert key not in self.at, key
            self.at[key] = (bank, self.fills[bank], by, self.frees[bank][by])
            return psum[bank]

        def filled(self, key):
            return S(f"bank{self.at[key][0]}_full")

        def full(self, key):
            b, n, _, _ = self.at[key]
            return S(f"bank{b}_full"), n

        def freed(self, key):
            b, _, by, n = self.at[key]
            return S(f"bank{b}_freed_{by}"), n

        def free(self, key):
            b, _, by, _ = self.at[key]
            return S(f"bank{b}_freed_{by}")

        def bank(self, key):
            return psum[self.at[key][0]]

    ring = Ring()

    class Order:

        def __init__(self, eng, name):
            self.eng, self.name, self.n = eng, name, {}

        def count(self, ins, sem=None):
            sem = sem or S(f"{self.name}_step")
            self.n[id(sem)] = self.n.get(id(sem), 0) + 1
            ins.then_inc(sem, 1)
            return sem

        def link(self, ins, sem=None):
            sem = self.count(ins, sem)
            self.eng.wait_ge(sem, self.n[id(sem)])

        def settle(self, sem=None):
            sem = sem or S(f"{self.name}_step")
            self.eng.wait_ge(sem, self.n[id(sem)])

        def chain(self, *steps):
            due = [None] * NS
            for ins_of, sem in steps:
                for u in range(NS):
                    if due[u]:
                        self.eng.wait_ge(*due[u])
                    used = self.count(ins_of(u), sem(u) if callable(sem) else sem)
                    due[u] = (used, self.n[id(used)])
            for u in range(NS):
                self.eng.wait_ge(*due[u])

        def each(self, ins_of, sem=None):
            used = [self.count(ins_of(u), sem(u) if callable(sem) else sem) for u in range(NS)]
            for sem in {id(x): x for x in used}.values():
                self.eng.wait_ge(sem, self.n[id(sem)])

    def heads(ap, n):
        return ap.rearrange("p (h d) -> p h d", h=n)

    def over(ap, n):
        return ap.unsqueeze(2).to_broadcast([ap.shape[0], ap.shape[1], n])

    def among(ap, n):
        return ap.unsqueeze(1).to_broadcast([ap.shape[0], n, ap.shape[1]])

    def hidden(e, k, per):
        if per == 2:
            return hT[:, (2 * e + k) % NHB, 0:NT]
        return hT[:, (2 * e + k // 2) % NHB, (k % 2) * NT:(k % 2 + 1) * NT]

    def tk(u):
        return slice(u * T, u * T + T)

    with nc.Block(name="setup") as block:
        @block.sync
        def _(eng):
            for g in w_in:
                sp.dma_start(group_tile[g][:], dram[g]).then_inc(w_in[g], 16)
                if g == "con":
                    for name, dst in inputs.items():
                        sp.dma_start(dst[:], dram[name][0]).then_inc(first_in, 16)
            sp.wait_ge(first_in, len(inputs) * 16)

        @block.vector
        def _(eng):
            o = Order(dve, "setup")
            dve.wait_ge(*weights("con"))
            o.link(dve.tensor_copy(ident_bf[:], IDENT), setup_dve)
            o.link(dve.memset(neg_wide_bf[:, 0:P], 0.0), setup_dve)
            o.link(dve.tensor_copy(neg_causal_bf, const("neg_causal")), setup_dve)
            o.link(dve.tensor_copy(neg_causal_t_bf[:], const("neg_causal_t")), setup_dve)
            o.link(dve.memset(zeros[:], 0.0), setup_dve)
            o.link(dve.memset(vaug[:], 1.0), setup_dve)
            o.link(dve.memset(vaug_c[:], 1.0), setup_dve)
            dve.wait_ge(*weights("L3m"))
            hr = head_mats[:].rearrange("p (h s) -> p h s", h=H)
            o.link(dve.tensor_tensor(core_sym[:], W["L3m_core"][:], W["L3m_coreT"][:], ALU.add), setup_dve)
            o.link(dve.tensor_reduce(res_mean[:], hr.rearrange("p h s -> p s h"), X, ALU.add), setup_dve)
            o.link(dve.tensor_scalar(res_mean[:], res_mean[:], -1.0 / H, None, ALU.mult), setup_dve)
            o.link(dve.scalar_tensor_tensor(core_sym[:], core_sym[:], 0.5 / H, res_mean[:], ALU.mult, ALU.add), setup_dve)
            o.link(dve.tensor_tensor(hr, hr, among(core_sym[:], H), ALU.add), setup_dve)

    with nc.Fori(0, B // NS) as pair:
        with nc.Block(name="pair") as block:
            @block.tensor
            def _(eng):
                mm, tr = pe.matmul, pe.transpose

                def warm(bank, n):
                    for _ in range(n):
                        mm(heads(bank[:], 2), ident_bf[:], among(neg_wide_bf[:], 2), start=True, stop=True)

                def transpose_x(fill=WARM["new_x"]):
                    for u in range(NS):
                        b = ring.open(("xT", stage[0], u), "act")
                        warm(b, 0 if u else fill)
                        pe.wait_ge(*nth("pe", "x_new"))
                        tr(b[:, 0:T], x_tok[:, u, :], IDENT).then_inc(ring.filled(("xT", stage[0], u)), 1)

                def wait_xT(n=WARM["xT"]):
                    warm(psum[7], n)
                    for u in range(NS):
                        pe.wait_ge(*ring.freed(("xT", stage[0] - 1, u)))

                def row_bias(out_ap, row):
                    mm(out_ap, ones_row, row, start=True, stop=False)

                def turn_attn(st, u, n=0):
                    b = ring.open((st, "aT", u), "act")
                    warm(b, n)
                    pe.wait_ge(*ring.freed((st, "o", u)))
                    tr(b[:, 0:T], attn[:, u, :], IDENT).then_inc(ring.filled((st, "aT", u)), 1)

                def project_attn(st, u, w, bias, n=0):
                    b = ring.open((st, "y", u), "dve")
                    warm(b, n)
                    if bias is not None:
                        row_bias(b[:, 0:D], bias)
                    pe.wait_ge(*ring.freed((st, "aT", u)))
                    mm(b[:, 0:D], attnT[:, u, :], w, start=bias is None, stop=True)\
                        .then_inc(ring.filled((st, "y", u)), 1)

                def attn_out(st, w, bias, slots=range(NS)):
                    for u in slots:
                        turn_attn(st, u, WARM["attn"][u])
                    for u in slots:
                        project_attn(st, u, w, bias, WARM["attnT"][u])

                def softmax_units(st, n_units, score, value, acc, w=None, bias=None):
                    total = NS * n_units
                    for step in range(total + 3):
                        if step < total:
                            b = ring.open((st, "s", step), "dve")
                            score(step // n_units, step % n_units, b).then_inc(ring.filled((st, "s", step)), 1)
                        i = step - 2
                        if 0 <= i < total:
                            b = ring.open((st, "pT", i), "act")
                            warm(b, WARM["drain"] if step >= total else 0)
                            pe.wait_ge(*nth("pe", "probs_ready"))
                            for k in range(4):
                                t_ = tr(b[:, k * T:k * T + T], probs[:, i % NPB, k * T:k * T + T], IDENT)
                            t_.then_inc(ring.filled((st, "pT", i)), 1)
                        i = step - 3
                        if 0 <= i < total:
                            pe.wait_ge(*ring.freed((st, "pT", i)))
                            u, n = i // n_units, i % n_units
                            if acc == "slot":
                                b = psum[6 + u] if n else ring.open((st, "o", u), "dve", 6 + u)
                            else:
                                b = ring.open((st, "o", i), "dve")
                            last = value(u, n, i % NPB, b)
                            if acc == "unit":
                                last.then_inc(ring.filled((st, "o", i)), 1)
                            elif n == n_units - 1:
                                last.then_inc(ring.filled((st, "o", u)), 1)
                        if w is not None and step == n_units + 5:
                            turn_attn(st, 0)
                        if w is not None and step == n_units + 6:
                            project_attn(st, 0, w, bias)
                    if w is not None:
                        attn_out(st, w, bias, [1])

                stage = [0]
                pe.wait_ge(*weights("con"))
                pe.wait_ge(setup_dve, 4)

                pe.wait_ge(*weights("L0a"))
                for u in range(NS):
                    b = ring.open(("L0a", "qv", u), "dve")
                    mm(b[:, 0:D], xT[:, tk(u)], W["L0a_qkv"][:, 0:D], start=True, stop=True)
                    mm(b[:, D:2 * D], xT[:, tk(u)], W["L0a_qkv"][:, 2 * D:3 * D], start=True, stop=True)\
                        .then_inc(ring.filled(("L0a", "qv", u)), 1)
                    b = ring.open(("L0a", "k", u), "act")
                    mm(b[:, 0:D], xT[:, tk(u)], W["L0a_qkv"][:, D:2 * D], start=True, stop=True)\
                        .then_inc(ring.filled(("L0a", "k", u)), 1)
                for u in range(NS):
                    pe.wait_ge(*ring.freed(("L0a", "qv", u)))
                    pe.wait_ge(*ring.freed(("L0a", "k", u)))
                    b = ring.open(("L0a", "ctx", u), "dve")
                    mm(b[:, 0:H * 9], ks[0:64, u, :], vaug[0:64, u, 0].rearrange("p h d -> p (h d)"),
                       start=True, stop=True).then_inc(ring.filled(("L0a", "ctx", u)), 1)
                    pe.wait_ge(*nth("pe", "L0a_qs"))
                    b = ring.open(("L0a", "qsT", u), "act")
                    tr(b[:, 0:T], qs[:, u, :], IDENT).then_inc(ring.filled(("L0a", "qsT", u)), 1)
                for u in range(NS):
                    pe.wait_ge(*ring.freed(("L0a", "ctx", u)))
                    pe.wait_ge(*ring.freed(("L0a", "qsT", u)))
                    b = ring.open(("L0a", "o", u), "dve", 6 + u)
                    mm(b[:, 0:H * 9], qT[:, 0, tk(u)], ctxbd[:, u].rearrange("p h d -> p (h d)"),
                       start=True, stop=True).then_inc(ring.filled(("L0a", "o", u)), 1)
                attn_out("L0a", W["L0a_o"][:], None)
                pe.wait_ge(*weights("L0x"))
                b = ring.open(("L0x", "kc"), "dve")
                mm(b[:, 0:NT], W["L0x_kv"][:, 0:D], ctxT[:], start=True, stop=True)\
                    .then_inc(ring.filled(("L0x", "kc")), 1)
                b = ring.open(("L0x", "vc"), "dve")
                for u in range(NS):
                    m = mm(b[:, tk(u)], ctxT[:, tk(u)], W["L0x_kv"][:, D:2 * D], start=True, stop=True)
                m.then_inc(ring.filled(("L0x", "vc")), 1)
                transpose_x()

                def wait_pad4(st, key, c):
                    if c < 3:
                        pe.wait_ge(*nth("pe", st + "_pad4"))
                    else:
                        pe.wait_ge(*ring.freed((st, *key)))

                def qkT_products(st, pairs_, key, by):
                    b = ring.open((st, key), by)
                    for i, (w, src) in enumerate(pairs_):
                        m = mm(b[:, i * NT:(i + 1) * NT], w, src, start=True, stop=True)
                    m.then_inc(ring.filled((st, key)), 1)

                stage[0] = 1
                wait_xT()
                qkT_products("L0x", [(W["L0x_q"][:], xT[:])], "q", "act")
                qkT_products("L0x", [(W["L0x_kv"][:, 0:D], xT[:])], "k", "dve")
                b = ring.open(("L0x", "v"), "dve")
                for u in range(NS):
                    m = mm(b[:, tk(u)], xT[:, tk(u)], W["L0x_kv"][:, D:2 * D], start=True, stop=True)
                m.then_inc(ring.filled(("L0x", "v")), 1)

                def score(u, n, b):
                    c, j = n // 2, 2 * (n % 2)
                    if u == 0 and n % 2 == 0:
                        wait_pad4("L0x", ("q",), c)
                    if u == 0 and n == 0:
                        pe.wait_ge(*ring.freed(("L0x", "kc")))
                        pe.wait_ge(*nth("pe", "L0x_bd0", 2))
                    if u == 1 and n == 0:
                        pe.wait_ge(*ring.freed(("L0x", "k")))
                    own, context = heads(b[:], 2)[:, :, T:2 * T], heads(b[:], 2)[:, :, 0:T]
                    mm(own, ident_bf[:], among(neg_causal_bf, 2), start=True, stop=False)
                    mm(own, pad4[:, c, tk(u)], bd[:, u, j:j + 2, T:2 * T], start=False, stop=True)
                    return mm(context, pad4[:, c, tk(u)], bd[:, u, j:j + 2, 0:T], start=True, stop=True)

                def value(u, n, buf, b):
                    if u == 0 and n == 0:
                        pe.wait_ge(*ring.freed(("L0x", "v")))
                    for k in range(2):
                        h = 2 * n + k
                        for s_ in range(2):
                            c = (2 * k + s_) * T
                            m = mm(b[:, 9 * h:9 * h + 9], probsT[:, buf, c:c + T], vaug[:, u, s_, h, :],
                                   start=s_ == 0, stop=s_ == 1)
                    return m

                softmax_units("L0x", 8, score, value, "slot", W["L0x_o"][:], W["L0x_bo"][:])
                transpose_x()

                def gate_logits(st, w):
                    b = ring.open((st, "logits"), "dve")
                    for u in range(NS):
                        m = mm(b[:, 8 * u:8 * u + 8], xT[:, tk(u)], w, start=True, stop=True)
                    m.then_inc(ring.filled((st, "logits")), 1)

                def expert_up(st, i, parts):
                    b = ring.open((st, "up", i), "dve" if st != "L1f" else "act")
                    for k, w in enumerate(parts):
                        m = mm(b[:, k * NT:(k + 1) * NT], w, xT[:], start=True, stop=True)
                    m.then_inc(ring.filled((st, "up", i)), 1)

                def expert_down(st, e, per):
                    b = ring.open((st, "y", e), "dve")
                    for u in range(NS):
                        for k in range(per):
                            m = mm(b[:, u * D:(u + 1) * D], hidden(e, k, per)[:, tk(u)],
                                   W[st + "_w2"][:, (per * e + k) * P:(per * e + k + 1) * P],
                                   start=k == 0, stop=k == per - 1)
                    m.then_inc(ring.filled((st, "y", e)), 1)

                def swiglu(st):
                    pe.wait_ge(*weights(st))
                    wait_xT()
                    gate_logits(st, W[st + "_gate"][:])
                    if st == "L2f":
                        pe.wait_ge(S("L2f_in"), 16)
                    else:
                        pe.wait_ge(*weights("L0f_experts"))
                    for i in range(20):
                        if i < 18:
                            f = i * 128
                            expert_up(st, i, (W[st + "_w1"][:, f:f + 128], W[st + "_w3"][:, f:f + 128]))
                        if i % 2 == 1 and i >= 3:
                            pe.wait_ge(*ring.freed((st, "up", i - 3)))
                            pe.wait_ge(*ring.freed((st, "up", i - 2)))
                            expert_down(st, (i - 3) // 2, 2)
                    transpose_x()

                stage[0] = 2
                swiglu("L0f")

                stage[0] = 3
                pe.wait_ge(*weights("L1a"))
                wait_xT()
                b = ring.open(("L1a", "beta"), "act")
                mm(b[0:H, 0:NT], W["L1a_b"][:], xT[:], start=True, stop=True)\
                    .then_inc(ring.filled(("L1a", "beta")), 1)
                for u in range(NS):
                    b = ring.open(("L1a", "qkv", u), "dve")
                    mm(b[:, 0:3 * D], xT[:, tk(u)], W["L1a_qkv"][:], start=True, stop=True)\
                        .then_inc(ring.filled(("L1a", "qkv", u)), 1)
                pe.wait_ge(*weights("L1x"))
                for c in range(0, 8, 2):
                    qkT_products("L1x", [(W["L1x_kv"][:, (c + k) * P:(c + k + 1) * P], ctxT[:]) for k in range(2)],
                                 f"k{c}", "act")
                b = ring.open(("L1a", "decay"), "dve")
                warm(b, WARM["decay"])
                for u in range(NS):
                    pe.wait_ge(*nth("pe", "L1a_decay"))
                    m = tr(b[:, u * H:u * H + H], gateT[0:H, 2, tk(u)], IDENT[0:H, 0:H])
                m.then_inc(ring.filled(("L1a", "decay")), 1)
                for u in range(NS):
                    b = ring.open(("L1a", "qT", u), "dve")
                    warm(b, WARM["rotated"])
                    pe.wait_ge(*nth("pe", "L1a_q"))
                    tr(b[:, 0:T], qk2[:, u, 0, :], IDENT).then_inc(ring.filled(("L1a", "qT", u)), 1)
                for u in range(NS):
                    b = ring.open(("L1a", "kT", u), "act")
                    warm(b, WARM["keys"])
                    pe.wait_ge(*nth("pe", "L1a_k"))
                    tr(b[:, 0:T], ks[:, u, :], IDENT).then_inc(ring.filled(("L1a", "kT", u)), 1)
                for i in range(2 * 4 + 1):
                    if i < 8:
                        u, c = i // 4, i % 4
                        b = ring.open(("L1a", "s", i), "dve")
                        if c == 0:
                            pe.wait_ge(*ring.freed(("L1a", "qT", u)))
                        wait_pad4("L1a", ("kT", u), c)
                        mm(heads(b[:], 4), pad4[:, c, tk(u)], bd[:, u, :, 0:T],
                           start=True, stop=True).then_inc(ring.filled(("L1a", "s", i)), 1)
                    if i >= 1:
                        u, c = (i - 1) // 4, (i - 1) % 4
                        pe.wait_ge(*ring.freed(("L1a", "s", i - 1)))
                        b = psum[6 + u] if c else ring.open(("L1a", "o", u), "dve", 6 + u)
                        for j in range(4):
                            h = 4 * c + j
                            m = mm(b[:, 9 * h:9 * h + 9], probs[:, (i - 1) % NPB, j * T:j * T + T],
                                   vaug[:, u, 0, h, :], start=True, stop=True)
                        m.then_inc(ring.filled(("L1a", "o", u)) if c == 3 else S("L1a_used"), 1)
                attn_out("L1a", W["L1a_o"][:], W["L1a_bo"][:])
                for u in range(NS):
                    for c in range(2):
                        b = ring.open(("L1x", "v", u, c), "dve")
                        mm(b[:], ctxT[:, tk(u)], W["L1x_kv"][:, 1024 + c * BANK:1024 + (c + 1) * BANK],
                           start=True, stop=True).then_inc(ring.filled(("L1x", "v", u, c)), 1)
                transpose_x(WARM["rms"])

                def score64(st, rhs_of):
                    def score(u, n, b, first=True):
                        r, c0 = n % 2, 4 * (n // 2)
                        if u == 0 and r == 0:
                            for c in (c0, c0 + 2):
                                pe.wait_ge(*ring.freed((st, f"q{c}")))
                        for j in range(4):
                            rows, rhs = rhs_of(r, c0 + j, u)
                            m = mm(b[:, j * T:j * T + T], q64[rows, c0 + j, tk(u)], rhs,
                                   start=first, stop=first or j == 3)
                        return m
                    return score

                stage[0] = 4
                wait_xT()
                for c in range(0, 8, 2):
                    qkT_products("L1x", [(W["L1x_q"][:, (c + k) * P:(c + k + 1) * P], xT[:]) for k in range(2)],
                                 f"q{c}", "act")
                for c in range(0, 8, 2):
                    pe.wait_ge(*ring.freed(("L1x", f"k{c}")))

                def value64(u, n, buf, b):
                    r, c0 = n % 2, 4 * (n // 2)
                    if n == 0:
                        for c in range(2):
                            pe.wait_ge(*ring.freed(("L1x", "v", u, c)))
                    for j in range(4):
                        h = 2 * (c0 + j) + r
                        m = mm(b[:, j * (R + 1):(j + 1) * (R + 1)], probsT[:, buf, j * T:j * T + T],
                               vaug_r[:, u, h, :], start=True, stop=True)
                    return m

                softmax_units("L1x", 4, score64("L1x", lambda r, c, u: (slice(64 * r, 64 * r + 64), k64[64 * r:64 * r + 64, c, tk(u)])),
                              value64, "unit")
                for u in range(NS):
                    for n in range(4):
                        pe.wait_ge(*ring.freed(("L1x", "o", 4 * u + n)))
                    for c in range(0, 8, 4):
                        b = ring.open(("L1x", "aT", u, c), "act")
                        for k in range(4):
                            m = tr(b[:, k * T:k * T + T], attn64[:, u, c + k].rearrange("p r d -> p (r d)"), IDENT)
                        m.then_inc(ring.filled(("L1x", "aT", u, c)), 1)
                    b = ring.open(("L1x", "y", u), "dve")
                    row_bias(b[:, 0:D], W["L1x_bo"][:])
                    for c in range(8):
                        if c % 4 == 0:
                            pe.wait_ge(*ring.freed(("L1x", "aT", u, c)))
                        m = mm(b[:, 0:D], attn64T[:, u, c, :], W["L1x_o"][:, c * P:(c + 1) * P],
                               start=False, stop=c == 7)
                    m.then_inc(ring.filled(("L1x", "y", u)), 1)
                transpose_x()

                stage[0] = 5
                pe.wait_ge(*weights("L1f"))
                wait_xT()
                gate_logits("L1f", W["L1f_gate"][:])
                for i in range(16 + 3):
                    if i < 16:
                        f = i * 256
                        expert_up("L1f", i, (W["L1f_w1"][:, f:f + 128], W["L1f_w1"][:, f + 128:f + 256]))
                    if i % 2 == 1 and i >= 3:
                        pe.wait_ge(*ring.freed(("L1f", "up", i - 3)))
                        pe.wait_ge(*ring.freed(("L1f", "up", i - 2)))
                        expert_down("L1f", (i - 3) // 2, 4)
                transpose_x()

                stage[0] = 6
                pe.wait_ge(*weights("L2a"))
                wait_xT()
                qkT_products("L2a", [(W["L2a_qkv"][:, 0:D], xT[:]), (W["L2a_qkv"][:, D:2 * D], xT[:])], "qk", "act")
                b = ring.open(("L2a", "v"), "dve")
                for u in range(NS):
                    m = mm(b[:, u * D:(u + 1) * D], xT[:, tk(u)], W["L2a_qkv"][:, 2 * D:3 * D], start=True, stop=True)
                m.then_inc(ring.filled(("L2a", "v")), 1)
                pe.wait_ge(*ring.freed(("L2a", "qk")))
                for u in range(NS):
                    b = ring.open(("L2a", "kf", u), "dve")
                    mm(b[:], qT[:, 1, tk(u)], W["L2a_proj"][:], start=True, stop=True)\
                        .then_inc(ring.filled(("L2a", "kf", u)), 1)
                for c in range(0, 4, 2):
                    b = ring.open(("L2a", "qf", c), "dve")
                    for k in range(2):
                        m = mm(b[:, k * NT:(k + 1) * NT], W["L2a_proj"][:, (c + k) * P:(c + k + 1) * P], qT[:, 0, :],
                               start=True, stop=True)
                    m.then_inc(ring.filled(("L2a", "qf", c)), 1)
                pe.wait_ge(*ring.freed(("L2a", "v")))
                for u in range(NS):
                    b = ring.open(("L2a", "kv", u), "dve")
                    warm(b, WARM["features"])
                    pe.wait_ge(*ring.freed(("L2a", "kf", u)))
                    for c in range(4):
                        m = mm(b[:, 36 * c:36 * c + 36], probs[:, u, c * P:(c + 1) * P],
                               vaug[:, u, 0, 4 * c:4 * c + 4, :], start=True, stop=True)
                    m.then_inc(ring.filled(("L2a", "kv", u)), 1)
                for c in range(0, 4, 2):
                    pe.wait_ge(*ring.freed(("L2a", "qf", c)))
                for u in range(NS):
                    pe.wait_ge(*ring.freed(("L2a", "kv", u)))
                    b = ring.open(("L2a", "o", u), "dve", 6 + u)
                    for c in range(4):
                        m = mm(b[:, 36 * c:36 * c + 36], feats_q[:, c, tk(u)], ctxbd[:, u, 4 * c:4 * c + 4, :],
                               start=True, stop=True)
                    m.then_inc(ring.filled(("L2a", "o", u)), 1)
                attn_out("L2a", W["L2a_o"][:], W["L2a_bo"][:])
                for u in range(NS):
                    b = ring.open(("L2a", "x1T", u), "act")
                    warm(b, 0 if u else WARM["inner_x"])
                    pe.wait_ge(*nth("pe", "L2a_x1"))
                    tr(b[:, 0:T], qs[:, u, :], IDENT).then_inc(ring.filled(("L2a", "x1T", u)), 1)
                for u in range(NS):
                    pe.wait_ge(*ring.freed(("L2a", "x1T", u)))
                for c in range(0, 4, 2):
                    qkT_products("L2a", [(W["L2a_w1"][:, (c + k) * P:(c + k + 1) * P], kT[:]) for k in range(2)],
                                 f"h{c}", "act")
                for u in range(NS):
                    b = ring.open(("L2a", "y2", u), "dve")
                    row_bias(b[:, 0:D], W["L2a_b2"][:])
                for c in range(0, 4, 2):
                    pe.wait_ge(*ring.freed(("L2a", f"h{c}")))
                for u in range(NS):
                    b = ring.bank(("L2a", "y2", u))
                    for c in range(4):
                        m = mm(b[:, 0:D], gact[:, c // 2, (c % 2) * NT + u * T:(c % 2) * NT + u * T + T],
                               W["L2a_w2"][:, c * P:(c + 1) * P], start=False, stop=c == 3)
                    m.then_inc(ring.filled(("L2a", "y2", u)), 1)
                pe.wait_ge(*weights("L2x"))
                qkT_products("L2x", [(W["L2x_k"][:], ctxT[:])], "k", "dve")
                b = ring.open(("L2x", "v"), "dve")
                for u in range(NS):
                    mm(b[:, u * D:(u + 1) * D], ctxT[:, tk(u)], W["L2x_v"][:], start=True, stop=False)
                    m = mm(b[:, u * D:(u + 1) * D], ones_row, W["L2x_bv"][:], start=False, stop=True)
                m.then_inc(ring.filled(("L2x", "v")), 1)
                transpose_x(WARM["norms"])

                def score8(u, n, b):
                    if u == 0:
                        wait_pad4("L2x", ("q",), n)
                    return mm(heads(b[:], 4), pad4[:, n, tk(u)], bd[:, u, :, 0:T], start=True, stop=True)

                def value8(u, n, buf, b):
                    for j in range(4):
                        h = 4 * n + j
                        m = mm(b[:, 9 * h:9 * h + 9], probsT[:, buf, j * T:j * T + T], vaug[:, u, 0, h, :],
                               start=True, stop=True)
                    return m

                stage[0] = 7
                wait_xT()
                qkT_products("L2x", [(W["L2x_q"][:], xT[:])], "q", "act")
                pe.wait_ge(*ring.freed(("L2x", "k")))
                pe.wait_ge(*ring.freed(("L2x", "v")))
                softmax_units("L2x", 4, score8, value8, "slot", W["L2x_o"][:], W["L2x_bo"][:])
                transpose_x()

                stage[0] = 8
                swiglu("L2f")

                stage[0] = 9
                pe.wait_ge(*weights("L3a"))
                wait_xT()
                qkT_products("L3a", [(W["L3a_basis"][:], xT[:])], "lat", "act")
                b = ring.open(("L3a", "v"), "dve")
                for u in range(NS):
                    mm(b[:, u * D:(u + 1) * D], xT[:, tk(u)], W["L3a_v"][:], start=True, stop=False)
                    m = mm(b[:, u * D:(u + 1) * D], ones_row, W["L3a_vb"][:], start=False, stop=True)
                m.then_inc(ring.filled(("L3a", "v")), 1)
                warm(psum[6], WARM["latent"])
                pe.wait_ge(*ring.freed(("L3a", "lat")))
                for c in range(0, 8, 2):
                    qkT_products("L3a", [(head_mats[:, (c + k) * P:(c + k + 1) * P], lat_pad[0:R, 0, :]) for k in range(2)],
                                 f"q{c}", "act")
                pe.wait_ge(*ring.freed(("L3a", "v")))
                latent = score64("L3a", lambda r, c, u: (slice(0, P), lat_pad[:, r, tk(u)]))

                def score_causal(u, n, b):
                    mm(heads(b[:], 4), ident_bf[:], among(neg_causal_bf, 4), start=True, stop=False)
                    return latent(u, n, b, first=False)

                def value_latent(u, n, buf, b):
                    r, c0 = n % 2, 4 * (n // 2)
                    for j in range(4):
                        h = 2 * (c0 + j) + r
                        m = mm(b[:, 9 * h:9 * h + 9], probsT[:, buf, j * T:j * T + T], vaug[:, u, 0, h, :],
                               start=True, stop=True)
                    return m

                softmax_units("L3a", 4, score_causal, value_latent, "slot", W["L3a_o"][:], W["L3a_bo"][:])
                pe.wait_ge(*weights("L3x"))
                for g in range(2):
                    b = ring.open(("L3x", "gates", g), "dve", 6 + g)
                    for k in (1, 2):
                        mm(b[0:8, 0:NT], W["L3x_gates"][:, 16 * k + 8 * g:16 * k + 8 * g + 8], ctxT[:],
                           start=k == 1, stop=False)
                transpose_x(WARM["new_x_filled"])

                stage[0] = 10
                wait_xT(0)
                for g in range(2):
                    mm(ring.bank(("L3x", "gates", g))[0:8, 0:NT], W["L3x_gates"][:, 8 * g:8 * g + 8], xT[:],
                       start=False, stop=True).then_inc(ring.filled(("L3x", "gates", g)), 1)
                for i in range(4):
                    u, g = i // 2, i % 2
                    b = ring.open(("L3x", "s", i), "dve")
                    if g == 0:
                        pe.wait_ge(*nth("pe", "L3x_bd"))
                    mm(heads(b[:], 4), ctxT[64 * g:64 * g + 64, tk(u)], bd[64 * g:64 * g + 64, u, :, 0:T],
                       start=True, stop=True).then_inc(ring.filled(("L3x", "s", i)), 1)
                b = ring.open(("L3x", "mx"), "act", 7)
                warm(b, WARM["gates"])
                pe.wait_ge(*nth("pe", "L3x_gates"))
                for k, row in enumerate((4, 2)):
                    for u in range(NS):
                        m = tr(b[:, 16 * k + u * 8:16 * k + u * 8 + 8], gateT[0:8, row, tk(u)], IDENT[0:8, 0:8])
                m.then_inc(ring.filled(("L3x", "mx")), 1)
                for i in range(4 + 2):
                    if i < 4:
                        u, g = i // 2, i % 2
                        b = ring.open(("L3x", "D", i), "act")
                        mm(heads(b[:], 4), ident_bf[:], among(neg_causal_t_bf[:], 4), start=True, stop=False)
                        if g == 0:
                            pe.wait_ge(*nth("pe", "L3x_mdiag"))
                        mm(heads(b[:], 4), const("ones", 8)[:, 0:T], mdiag[:, u, 4 * g:4 * g + 4, :],
                           start=False, stop=True).then_inc(ring.filled(("L3x", "D", i)), 1)
                    if i >= 2:
                        u, g = (i - 2) // 2, (i - 2) % 2
                        pe.wait_ge(*ring.freed(("L3x", "s", i - 2)))
                        b = psum[6 + u] if g else ring.open(("L3x", "o", u), "dve", 6 + u)
                        for j in range(4):
                            h = 4 * g + j
                            m = mm(b[:, 17 * h:17 * h + 17], probsT[:, (i - 2) % NPB, j * T:j * T + T],
                                   vaug_c[:, u, h, :], start=True, stop=True)
                        m.then_inc(ring.filled(("L3x", "o", u)) if g else S("L3x_used"), 1)
                transpose_x(WARM["head_norms"])

            @block.vector
            def _(eng):
                o = Order(dve, "dve")
                link, each, chain = o.link, o.each, o.chain

                def layer_norm(dst, affine=None, told=None):
                    chain((lambda u: dve.bn_stats(stats[:, u, :], res[:, u, :]), None),
                          (lambda u: dve.bn_aggr(mv[:, u, :], stats[:, u, :]), S("var_ready")))
                    for u in range(NS):
                        dve.wait_ge(*nth("dve", "rstd_ready"))
                        o.count(dve.tensor_scalar(dst(u), res[:, u, :], mv[:, u, 0:1], rstd[:, u, :],
                                                  ALU.subtract, ALU.mult), told if affine is None else None)
                    o.settle(told if affine is None else None)
                    if affine is not None:
                        each(lambda u: dve.tensor_tensor(dst(u), dst(u), affine[0], ALU.mult))
                        each(lambda u: dve.tensor_tensor(dst(u), dst(u), affine[1], ALU.add), told)

                def new_x():
                    layer_norm(lambda u: x_tok[:, u, :], told=S("x_new"))

                def add_product(key, base):
                    for u in range(NS):
                        dve.wait_ge(*ring.full(key(u)))
                        o.count(dve.tensor_tensor(res[:, u, :], ring.bank(key(u))[:, 0:D], base[:, u, :], ALU.add),
                                ring.free(key(u)))
                    for u in range(NS):
                        o.settle(ring.free(key(u)))

                def post_norm(st, base=x_tok):
                    add_product(lambda u: (st, "y", u), base)
                    new_x()

                def divide_heads(st, floor=None, add=None, rows=None, slots=range(NS)):
                    b = {u: heads(ring.bank((st, "o", u))[:, 0:H * 9], H) for u in slots}

                    def step(ins_of, sem=None):
                        used = [o.count(ins_of(u), sem and sem(u)) for u in slots]
                        for x in used:
                            o.settle(x)

                    for u in slots:
                        dve.wait_ge(*ring.full((st, "o", u)))
                    den, inv = (lambda u: small[:, u, 0:H]), (lambda u: small2[:, u, 0:H])
                    if floor is not None:
                        step(lambda u: dve.tensor_scalar(den(u), b[u][:, :, 8], floor, None, ALU.max))
                    elif add is not None:
                        step(lambda u: dve.tensor_scalar(den(u), b[u][:, :, 8], add, None, ALU.add))
                    else:
                        den = lambda u: b[u][:, :, 8]
                    step(lambda u: dve.reciprocal(inv(u), den(u)))
                    if rows is None:
                        step(lambda u: dve.tensor_tensor(heads(attn[:, u, :], H), b[u][:, :, 0:8], over(inv(u), 8), ALU.mult),
                             lambda u: ring.free((st, "o", u)))
                    else:
                        step(lambda u: dve.scalar_tensor_tensor(heads(attn[:, u, :], H), b[u][:, :, 0:8], rows,
                                                                over(inv(u), 8), ALU.mult, ALU.mult),
                             lambda u: ring.free((st, "o", u)))

                def softmax_units(st, n_units, keys, after=None):
                    nh = BANK // keys
                    total = NS * n_units
                    for i in range(total):
                        s_ = heads(ring.bank((st, "s", i))[:], nh)
                        dve.wait_ge(*ring.full((st, "s", i)))
                        mx = small[:, i % 2, 32:32 + nh]
                        link(dve.tensor_reduce(mx, s_, X, ALU.max))
                        if i >= NPB:
                            dve.wait_ge(*ring.full((st, "pT", i - NPB)))
                        o.count(dve.tensor_tensor(heads(probs[:, i % NPB, :], nh), s_, over(mx, keys), ALU.subtract),
                             ring.free((st, "s", i)))
                        if after:
                            after(i)

                def early_divide(st, n_units):
                    return lambda i: divide_heads(st, slots=[0]) if i == n_units + 3 else None

                dve.wait_ge(*weights("L0a"))
                qv = [ring.bank(("L0a", "qv", u)) for u in range(NS)]
                for u in range(NS):
                    dve.wait_ge(*ring.full(("L0a", "qv", u)))
                    link(dve.tensor_reduce(small[:, u, 0:H], heads(qv[u][:, 0:D], H), X, ALU.max))
                    o.count(dve.tensor_tensor(heads(qs[:, u, :], H), heads(qv[u][:, 0:D], H), over(small[:, u, 0:H], 8),
                                              ALU.subtract), S("L0a_less_max"))
                each(lambda u: dve.tensor_copy(vaug[:, u, 0, :, 0:8], heads(qv[u][:, D:2 * D], H)),
                     lambda u: ring.free(("L0a", "qv", u)))
                for u in range(NS):
                    dve.wait_ge(*nth("dve", "L0a_expq"))
                    o.count(dve.tensor_reduce(small[:, u, 0:H], heads(qs[:, u, :], H), X, ALU.add))
                o.settle()
                each(lambda u: dve.reciprocal(small2[:, u, 0:H], small[:, u, 0:H]))
                each(lambda u: dve.scalar_tensor_tensor(heads(qs[:, u, :], H), heads(qs[:, u, :], H), DH ** -0.5,
                                                        over(small2[:, u, 0:H], 8), ALU.mult, ALU.mult), S("L0a_qs"))
                for u in range(NS):
                    dve.wait_ge(*ring.full(("L0a", "ctx", u)))
                    o.count(dve.tensor_tensor(ctxbd[:, u], heads(ring.bank(("L0a", "ctx", u))[:, 0:H * 9], H),
                                              over(const("head8"), 9), ALU.mult), ring.free(("L0a", "ctx", u)))
                divide_heads("L0a", floor=1e-6, rows=const("late"))
                post_norm("L0a", x_raw)

                for key, s_ in (("kc", 0), ("k", 1)):
                    dve.wait_ge(*ring.full(("L0x", key)))
                    for u in range(NS):
                        o.count(dve.tensor_tensor(bd[:, u, :, s_ * T:(s_ + 1) * T],
                                                  among(ring.bank(("L0x", key))[:, tk(u)], 4),
                                                  over(const("head8in32"), T), ALU.mult),
                                ring.free(("L0x", key)) if u else S("L0x_bd0"))
                    if key == "kc":
                        dve.wait_ge(*ring.full(("L0x", "vc")))
                        for u in range(NS):
                            o.count(dve.tensor_copy(vaug[:, u, 0, :, 0:8], heads(ring.bank(("L0x", "vc"))[:, tk(u)], H)),
                                    ring.free(("L0x", "vc")) if u else None)
                dve.wait_ge(*ring.full(("L0x", "v")))
                for u in range(NS):
                    o.count(dve.tensor_copy(vaug[:, u, 1, :, 0:8], heads(ring.bank(("L0x", "v"))[:, tk(u)], H)),
                            ring.free(("L0x", "v")) if u else None)
                softmax_units("L0x", 8, 2 * T, early_divide("L0x", 8))
                divide_heads("L0x", slots=[1])
                post_norm("L0x")

                lg, mx, pr, pick = small2[:, :, 0:8], small2[:, :, 8], small2[:, :, 16:24], small2[:, :, 24:32]
                comb = small[:, :, 0:8]

                def gates_in(st, kind):
                    b = ring.bank((st, "logits"))
                    dve.wait_ge(*ring.full((st, "logits")))
                    link(dve.tensor_copy(lg, b[:, 0:16].rearrange("p (u e) -> p u e", u=2)), ring.free((st, "logits")))
                    if kind == "sigmoid":
                        link(dve.tensor_copy(pr, lg), S("gates_in"))
                    else:
                        link(dve.tensor_reduce(mx, lg, X, ALU.max))
                        link(dve.tensor_tensor(pr, lg, over(mx, 8), ALU.subtract), S("gates_in"))

                def gates(st, kind):
                    dve.wait_ge(*nth("dve", "gates_exp"))
                    if kind == "sigmoid":
                        link(dve.tensor_scalar(pr, pr, 1.0, None, ALU.add))
                        link(dve.reciprocal(pr, pr))
                    else:
                        link(dve.tensor_reduce(mx, pr, X, ALU.add))
                        link(dve.reciprocal(mx, mx))
                        link(dve.tensor_tensor(pr, pr, over(mx, 8), ALU.mult))
                    if kind == "softmax":
                        link(dve.tensor_tensor(pick, pr, among(W[st + "_gb"][:], 2), ALU.add))
                    elif kind == "sigmoid":
                        link(dve.tensor_tensor(pick, lg, among(W[st + "_gb"][:], 2), ALU.add))
                    else:
                        link(dve.tensor_copy(pick, pr))
                    each(lambda u: dve.max(small2[:, u, 32:40], small2[:, u, 24:32]))
                    each(lambda u: dve.tensor_scalar(small2[:, u, 34:40], small2[:, u, 34:40], 0.0, -3e38, ALU.mult, ALU.add))
                    each(lambda u: dve.match_replace(small2[:, u, 40:48], small2[:, u, 32:40], small2[:, u, 24:32], -2e38))
                    link(dve.tensor_scalar(small2[:, :, 48:56], small2[:, :, 40:48], -2e38, None, ALU.is_equal))
                    link(dve.tensor_tensor(comb, small2[:, :, 48:56], pr, ALU.mult))
                    if kind == "softmax_top":
                        link(dve.tensor_reduce(mx, comb, X, ALU.add))
                        link(dve.reciprocal(mx, mx))
                        link(dve.tensor_tensor(comb, comb, over(mx, 8), ALU.mult))

                def add_expert(st, i, e):
                    b = ring.bank((st, "y", i))
                    dve.wait_ge(*ring.full((st, "y", i)))
                    for u in range(NS):
                        y, r = b[:, u * D:(u + 1) * D], res[:, u, :]
                        ins = (dve.tensor_tensor(r, y, x_tok[:, u, :], ALU.add) if e < 0 else
                               dve.scalar_tensor_tensor(r, y, comb[:, u, e:e + 1], x_tok[:, u, :] if i == 0 else r,
                                                        ALU.mult, ALU.add))
                        o.count(ins, ring.free((st, "y", i)) if u else None)
                    o.settle()
                    o.settle(ring.free((st, "y", i)))

                def swiglu(st, kind):
                    dve.wait_ge(*weights(st))
                    gates_in(st, kind)
                    for i in range(18 + 2):
                        if i < 18:
                            if i >= NHB:
                                dve.wait_ge(*ring.full((st, "y", (i - NHB) // 2)))
                            dve.wait_ge(*nth("dve", "gact_ready"))
                            o.count(dve.tensor_tensor(hT[:, i % NHB, 0:NT], gact[:, i % NHB, 0:NT],
                                                   ring.bank((st, "up", i))[:, NT:2 * NT], ALU.mult),
                                 ring.free((st, "up", i)))
                        if i == 1:
                            gates(st, kind)
                        if i % 2 == 1 and i >= 3:
                            add_expert(st, (i - 3) // 2, (i - 3) // 2 - 1)
                    new_x()

                swiglu("L0f", "softmax")

                dve.wait_ge(*weights("L1a"))
                link(dve.tensor_scalar(neg_bb[:], W["L1a_bb"][:], -1.0, None, ALU.mult), S("L1a_negbb"))
                t1 = [heads(qk2[:, u].rearrange("p a d -> p (a d)"), 2 * H) for u in range(NS)]
                t2 = [heads(qk3[:, u].rearrange("p a d -> p (a d)"), 2 * H) for u in range(NS)]
                cos, sin = const("cos"), const("sin")
                for u in range(NS):
                    dve.wait_ge(*ring.full(("L1a", "qkv", u)))
                qkv = [ring.bank(("L1a", "qkv", u)) for u in range(NS)]
                qk = [heads(qkv[u][:, 0:2 * D], 2 * H) for u in range(NS)]
                chain((lambda u: dve.tensor_tensor(t1[u], qk[u], among(cos, 2 * H), ALU.mult), None),
                      (lambda u: dve.tensor_tensor(t2[u][:, :, 0:4], qk[u][:, :, 4:8], among(sin[:, 0:4], 2 * H), ALU.mult), None),
                      (lambda u: dve.tensor_tensor(t2[u][:, :, 4:8], qk[u][:, :, 0:4], among(sin[:, 4:8], 2 * H), ALU.mult), None),
                      (lambda u: dve.tensor_tensor(t1[u], t1[u], t2[u], ALU.add), None),
                      (lambda u: dve.tensor_scalar(t2[u], t1[u], 0.0, None, ALU.min), S("L1a_min")))
                each(lambda u: dve.tensor_copy(vaug[:, u, 0, :, 0:8], heads(qkv[u][:, 2 * D:3 * D], H)),
                     lambda u: ring.free(("L1a", "qkv", u)))
                dve.wait_ge(*ring.freed(("L1a", "beta")))
                g = gateT
                link(dve.tensor_scalar(g[:, 1, :], g[:, 0, :], 1.0, None, ALU.add))
                link(dve.reciprocal(g[:, 1, :], g[:, 1, :]))
                link(dve.tensor_scalar(g[:, 1, :], g[:, 1, :], 0.8, 0.999, ALU.max, ALU.min))
                each(lambda u: dve.tensor_tensor_scan(g[:, 2, tk(u)], g[:, 1, tk(u)], zeros[:], 1.0,
                                                      ALU.mult, ALU.add), S("L1a_decay"))
                for u in range(NS):
                    dve.wait_ge(*nth("dve", "L1a_exp"))
                    o.count(dve.scalar_tensor_tensor(t1[u], t1[u], 0.0, t2[u], ALU.max, ALU.add), S("L1a_q"))
                o.settle(S("L1a_q"))
                dve.wait_ge(*ring.full(("L1a", "decay")))
                iv = [small2[:, u, 16:32] for u in range(NS)]
                each(lambda u: dve.reciprocal(iv[u], ring.bank(("L1a", "decay"))[:, u * H:u * H + H]),
                     lambda u: ring.free(("L1a", "decay")) if u else None)
                each(lambda u: dve.tensor_tensor(heads(ks[:, u, :], H), t1[u][:, H:2 * H, :], over(iv[u], 8), ALU.mult),
                     S("L1a_k"))
                for u in range(NS):
                    dve.wait_ge(*ring.full(("L1a", "qT", u)))
                    o.count(dve.tensor_tensor(bd[:, u, :, 0:T], among(ring.bank(("L1a", "qT", u))[:, 0:T], 4),
                                           over(const("head8in32"), T), ALU.mult), ring.free(("L1a", "qT", u)))
                for i in range(8):
                    dve.wait_ge(*ring.full(("L1a", "s", i)))
                    if i >= NPB:
                        k = i - NPB
                        if k == 3:
                            dve.wait_ge(*ring.full(("L1a", "o", 0)))
                        else:
                            dve.wait_ge(*nth("dve", "L1a_used"))
                    o.count(dve.tensor_tensor(heads(probs[:, i % NPB, :], 4), heads(ring.bank(("L1a", "s", i))[:], 4),
                                           among(const("causal_t"), 4), ALU.mult), ring.free(("L1a", "s", i)))
                ob = [heads(ring.bank(("L1a", "o", u))[:, 0:H * 9], H) for u in range(NS)]
                for u in range(NS):
                    dve.wait_ge(*ring.full(("L1a", "o", u)))
                den, inv = (lambda u: small[:, u, 0:H]), (lambda u: small[:, u, 16:32])
                chain((lambda u: dve.scalar_tensor_tensor(den(u), iv[u], 1e-6, ob[u][:, :, 8], ALU.mult, ALU.add), None),
                      (lambda u: dve.reciprocal(inv(u), den(u)), None),
                      (lambda u: dve.tensor_tensor(heads(attn[:, u, :], H), ob[u][:, :, 0:8], over(inv(u), 8), ALU.mult), lambda u: ring.free(("L1a", "o", u))))
                add_product(lambda u: ("L1a", "y", u), x_tok)
                chain((lambda u: dve.tensor_tensor(attn[:, u, :], res[:, u, :], res[:, u, :], ALU.mult), None),
                      (lambda u: dve.tensor_reduce(mv[:, u, 1:2], attn[:, u, :], X, ALU.add), S("ms_ready")))
                for u in range(NS):
                    dve.wait_ge(*nth("dve", "rstd_ready"))
                    o.count(dve.scalar_tensor_tensor(res[:, u, :], res[:, u, :], rstd[:, u, :], W["L1a_scale"][:],
                                                     ALU.mult, ALU.mult))
                o.settle()
                each(lambda u: dve.tensor_tensor(res[:, u, :], res[:, u, :], x_tok[:, u, :], ALU.add))
                new_x()

                link(dve.memset(vaug_r[:, :, :, R:R + 1], 1.0))
                for u in range(NS):
                    for c in range(2):
                        dve.wait_ge(*ring.full(("L1x", "v", u, c)))
                        o.count(dve.tensor_copy(vaug_r[:, u, 8 * c:8 * c + 8, 0:R], heads(ring.bank(("L1x", "v", u, c))[:], 8)),
                             ring.free(("L1x", "v", u, c)))

                def finish_unit(k):
                    u, n = k // 4, k % 4
                    r, c0 = n % 2, 4 * (n // 2)
                    b = heads(ring.bank(("L1x", "o", k))[:, 0:4 * (R + 1)], 4)
                    dve.wait_ge(*ring.full(("L1x", "o", k)))
                    link(dve.reciprocal(small2[:, u, 4 * n:4 * n + 4], b[:, :, R]))
                    o.count(dve.tensor_tensor(attn64[:, u, c0:c0 + 4, r, :], b[:, :, 0:R], over(small2[:, u, 4 * n:4 * n + 4], R),
                                           ALU.mult), ring.free(("L1x", "o", k)))

                softmax_units("L1x", 4, T, lambda i: finish_unit(i - 4) if i >= 4 else None)
                for k in range(4, 8):
                    finish_unit(k)
                post_norm("L1x")

                gates_in("L1f", "softmax_top")
                gates("L1f", "softmax_top")
                for e in range(E):
                    add_expert("L1f", e, e)
                new_x()

                dve.wait_ge(*weights("L2a"))
                b = ring.bank(("L2a", "v"))
                dve.wait_ge(*ring.full(("L2a", "v")))
                for u in range(NS):
                    o.count(dve.tensor_copy(vaug[:, u, 0, :, 0:8], heads(b[:, u * D:(u + 1) * D], H)),
                         ring.free(("L2a", "v")) if u else None)
                keys = [("L2a", "kf", 0), ("L2a", "kf", 1), ("L2a", "qf", 0), ("L2a", "qf", 2)]
                for i in range(4 + 1):
                    if i < 4:
                        dve.wait_ge(*ring.full(keys[i]))
                        o.count(dve.tensor_scalar(gact[:, i, :], ring.bank(keys[i])[:], 0.0, None, ALU.min), S("L2a_min"))
                    if i >= 1:
                        k = i - 1
                        dst = probs[:, k, :] if k < 2 else \
                            feats_q[:, 2 * (k - 2):2 * (k - 2) + 2, :].rearrange("p c t -> p (c t)")
                        dve.wait_ge(*nth("dve", "L2a_exp"))
                        o.count(dve.scalar_tensor_tensor(dst, ring.bank(keys[k])[:], 0.0, gact[:, k, :], ALU.max, ALU.add),
                             ring.free(keys[k]))
                for u in range(NS):
                    dve.wait_ge(*ring.full(("L2a", "kv", u)))
                    m = const("feat32").unsqueeze(1).unsqueeze(3).to_broadcast([P, 4, 4, 9])
                    o.count(dve.tensor_tensor(ctxbd[:, u].rearrange("p (c j) d -> p c j d", c=4),
                                           ring.bank(("L2a", "kv", u))[:, 0:144].rearrange("p (c j d) -> p c j d", c=4, j=4),
                                           m, ALU.mult), ring.free(("L2a", "kv", u)))
                divide_heads("L2a", add=1e-8)
                aff = (W["L2a_gamma"][:], W["L2a_beta"][:])
                add_product(lambda u: ("L2a", "y", u), x_tok)
                layer_norm(lambda u: qs[:, u, :], aff, S("L2a_x1"))
                add_product(lambda u: ("L2a", "y2", u), qs)
                layer_norm(lambda u: qs[:, u, :], aff)
                each(lambda u: dve.tensor_tensor(res[:, u, :], qs[:, u, :], x_tok[:, u, :], ALU.add))
                new_x()

                dve.wait_ge(*weights("L2x"))
                o.count(dve.tensor_tensor(bq4[:], const("feat32"), W["L2x_bq"][:].to_broadcast([P, 4]), ALU.mult),
                     S("L2x_bias"))
                b = ring.bank(("L2x", "k"))
                dve.wait_ge(*ring.full(("L2x", "k")))
                for u in range(NS):
                    ins = dve.scalar_tensor_tensor(bd[:, u, :, 0:T], among(b[:, tk(u)], 4), W["L2x_bk"][:],
                                                   over(const("head8in32"), T), ALU.add, ALU.mult)
                    o.count(ins, ring.free(("L2x", "k")) if u else None)
                b = ring.bank(("L2x", "v"))
                dve.wait_ge(*ring.full(("L2x", "v")))
                for u in range(NS):
                    o.count(dve.tensor_copy(vaug[:, u, 0, :, 0:8], heads(b[:, u * D:(u + 1) * D], H)),
                         ring.free(("L2x", "v")) if u else None)
                softmax_units("L2x", 4, T, early_divide("L2x", 4))
                divide_heads("L2x", slots=[1])
                post_norm("L2x")

                swiglu("L2f", "sigmoid")

                dve.wait_ge(*weights("L3a"))
                for r in range(2):
                    o.count(dve.memset(lat_pad[64 - 64 * r:128 - 64 * r, r, :], 0.0), S("L3a_zeros") if r else None)
                b = ring.bank(("L3a", "v"))
                dve.wait_ge(*ring.full(("L3a", "v")))
                for u in range(NS):
                    o.count(dve.tensor_copy(vaug[:, u, 0, :, 0:8], heads(b[:, u * D:(u + 1) * D], H)),
                         ring.free(("L3a", "v")) if u else None)
                softmax_units("L3a", 4, T, early_divide("L3a", 4))
                divide_heads("L3a", slots=[1])
                post_norm("L3a")

                dve.wait_ge(*weights("L3x"))
                g = gateT
                for u in range(NS):
                    dve.wait_ge(*ring.freed(("xT", 9, u)))
                for u in range(NS):
                    o.count(dve.tensor_tensor(bd[:, u, :, 0:T], among(xT[:, tk(u)], 4),
                                              over(const("head16in64"), T), ALU.mult), S("L3x_bd"))
                for row, bias in enumerate((W["L3x_ib"], W["L3x_fb"])):
                    dve.wait_ge(*ring.full(("L3x", "gates", row)))
                    link(dve.tensor_scalar(g[0:8, row, :], ring.bank(("L3x", "gates", row))[0:8, 0:NT], bias[:], None,
                                           ALU.add), ring.free(("L3x", "gates", row)))
                link(dve.scalar_tensor_tensor(g[0:8, 5, :], g[0:8, 1, :], -1.0, g[0:8, 1, :], ALU.mult, ALU.min),
                     S("L3x_absf"))
                dve.wait_ge(*nth("dve", "L3x_softplus"))
                link(dve.scalar_tensor_tensor(g[0:8, 1, :], g[0:8, 1, :], 0.0, g[0:8, 5, :], ALU.min, ALU.subtract))
                ones8 = const("ones", 8)[:, 0:T]
                for u in range(NS):
                    link(dve.tensor_tensor_scan(g[0:8, 3, tk(u)], ones8, g[0:8, 1, tk(u)], 0.0, ALU.mult, ALU.add))
                link(dve.tensor_tensor(g[0:8, 2, :], g[0:8, 0, :], g[0:8, 3, :], ALU.subtract))
                for u in range(NS):
                    link(dve.tensor_tensor_scan(g[0:8, 5, tk(u)], ones8, g[0:8, 2, tk(u)], -3.0e38, ALU.mult, ALU.max))
                link(dve.tensor_tensor(g[0:8, 4, :], g[0:8, 3, :], g[0:8, 5, :], ALU.add), S("L3x_gates"))
                for u in range(NS):
                    o.count(dve.scalar_tensor_tensor(mdiag[:, u], among(g[0:8, 5, tk(u)], 8), -1.0,
                                                  over(const("delta8", 8), T), ALU.mult, ALU.mult), S("L3x_mdiag"))
                    o.count(dve.tensor_copy(vaug_c[:, u, :, 0:DC], heads(ctx_tok[:, u, :], HC)))
                for i in range(4):
                    dve.wait_ge(*ring.full(("L3x", "s", i)))
                    dve.wait_ge(*ring.freed(("L3x", "D", i)))
                    if i >= NPB:
                        dve.wait_ge(*nth("dve", "L3x_used"))
                    o.count(dve.scalar_tensor_tensor(probsT[:, i % NPB, :], ring.bank(("L3x", "s", i))[:], DC ** -0.5,
                                                  probs[:, i % NPB, :], ALU.mult, ALU.mult), ring.free(("L3x", "s", i)))
                dve.wait_ge(*ring.freed(("L3x", "mx")))
                ob = [heads(ring.bank(("L3x", "o", u))[:, 0:HC * 17], HC) for u in range(NS)]
                for u in range(NS):
                    dve.wait_ge(*ring.full(("L3x", "o", u)))
                n, m = (lambda u: small[:, u, 0:8]), (lambda u: small[:, u, 8:16])
                h3 = lambda u: heads(attn[:, u, :], HC)
                chain((lambda u: dve.tensor_copy(n(u), ob[u][:, :, DC]), None),
                      (lambda u: dve.scalar_tensor_tensor(n(u), n(u), -1.0, n(u), ALU.mult, ALU.max), None),
                      (lambda u: dve.tensor_tensor(n(u), n(u), small2[:, u, 32:40], ALU.max), None),
                      (lambda u: dve.tensor_scalar(n(u), n(u), 1e-6, None, ALU.add), None),
                      (lambda u: dve.reciprocal(n(u), n(u)), None),
                      (lambda u: dve.tensor_tensor(h3(u), ob[u][:, :, 0:DC], over(n(u), DC), ALU.mult), lambda u: ring.free(("L3x", "o", u))),
                      (lambda u: dve.tensor_reduce(m(u), h3(u), X, ALU.add), None),
                      (lambda u: dve.scalar_tensor_tensor(h3(u), over(m(u), DC), -1.0 / DC, h3(u), ALU.mult, ALU.add), None),
                      (lambda u: dve.tensor_tensor(qs[:, u, :], attn[:, u, :], attn[:, u, :], ALU.mult), None),
                      (lambda u: dve.tensor_reduce(small[:, u, 16:24], heads(qs[:, u, :], HC), X, ALU.add), S("L3x_var")))
                for u in range(NS):
                    dve.wait_ge(*nth("dve", "L3x_rstd"))
                    o.count(dve.tensor_tensor(h3(u), h3(u), over(small[:, u, 24:32], DC), ALU.mult))
                o.settle()
                chain((lambda u: dve.tensor_tensor(attn[:, u, :], attn[:, u, :], W["L3x_w"][:], ALU.mult), None),
                      (lambda u: dve.tensor_tensor(res[:, u, :], attn[:, u, :], x_tok[:, u, :], ALU.add), None))
                new_x()

                link(dve.tensor_copy(x_all[:, bass.ds(pair * NS, NS), :], x_tok[:]))

            @block.scalar
            def _(eng):
                o = Order(act, "act")
                link, each = o.link, o.each
                eps5, eps6, one, _z = (const("eps")[:, i:i + 1] for i in range(4))

                def norm_rstd():
                    for u in range(NS):
                        act.wait_ge(*nth("act", "var_ready"))
                        o.count(act.activation(lnv[:, u, :], mv[:, u, 1:2], ACT.Ln, bias=eps5))
                    o.settle()
                    each(lambda u: act.activation(rstd[:, u, :], lnv[:, u, :], ACT.Exp, scale=-0.5), S("rstd_ready"))

                def keep_xT(st):
                    for u in range(NS):
                        act.wait_ge(*ring.full(("xT", st, u)))
                        o.count(act.copy(xT[:, tk(u)], ring.bank(("xT", st, u))[:, 0:T]), ring.free(("xT", st, u)))

                def attnT_copy(st, slots=range(NS)):
                    for u in slots:
                        act.wait_ge(*ring.full((st, "aT", u)))
                        o.count(act.copy(attnT[:, u, :], ring.bank((st, "aT", u))[:, 0:T]), ring.free((st, "aT", u)))

                def softmax_units(st, n_units, scale):
                    total = NS * n_units
                    for step in range(total + 2):
                        if step < total:
                            i = step
                            act.wait_ge(*ring.freed((st, "s", i)))
                            o.count(act.activation(probs[:, i % NPB, :], probs[:, i % NPB, :], ACT.Exp, scale=scale),
                                 S("probs_ready"))
                        i = step - 2
                        if 0 <= i < total:
                            act.wait_ge(*ring.full((st, "pT", i)))
                            o.count(act.copy(probsT[:, i % NPB, :], ring.bank((st, "pT", i))[:]), ring.free((st, "pT", i)))
                        if (st, "aT", 0) in ring.at and step == n_units + 5:
                            attnT_copy(st, [0])

                def to_sbuf(key, dst, bias=None, shape=None):
                    src = ring.bank(key)[:]
                    act.wait_ge(*ring.full(key))
                    src = src[:, 0:NT] if shape is None else shape(src)
                    if bias is None:
                        o.count(act.copy(dst, src), ring.free(key))
                    else:
                        o.count(act.activation(dst, src, ACT.Identity, bias=bias), ring.free(key))

                def to_pad4(key, tokens, n, bias=None):
                    act.wait_ge(*ring.full(key))
                    for c in range(4):
                        ins = act.activation(pad4[:, c, tokens], ring.bank(key)[:, 0:n], ACT.Identity,
                                             scale=const("feat32")[:, c:c + 1],
                                             **({} if bias is None else {"bias": bias[:, c:c + 1]}))
                        o.count(ins, ring.free(key) if c == 3 else S(key[0] + "_pad4"))

                act.preload_act_table_set(EXP_LN)

                for u in range(NS):
                    act.wait_ge(*ring.full(("L0a", "k", u)))
                    o.count(act.activation(ks[:, u, :], ring.bank(("L0a", "k", u))[:, 0:D], ACT.Exp),
                         ring.free(("L0a", "k", u)))
                    act.wait_ge(*nth("act", "L0a_less_max"))
                    o.count(act.activation(qs[:, u, :], qs[:, u, :], ACT.Exp), S("L0a_expq"))
                for u in range(NS):
                    to_sbuf(("L0a", "qsT", u), qT[:, 0, tk(u)], shape=lambda s: s[:, 0:T])
                attnT_copy("L0a")
                norm_rstd()
                keep_xT(0)
                to_pad4(("L0x", "q"), slice(0, NT), NT)
                softmax_units("L0x", 8, DH ** -0.5)
                attnT_copy("L0x", [1])
                norm_rstd()
                keep_xT(1)

                def gates_exp(scale):
                    act.wait_ge(*nth("act", "gates_in"))
                    pr = small2[:, :, 16:24]
                    o.count(act.activation(pr, pr, ACT.Exp, scale=scale), S("gates_exp"))

                def swiglu(st, scale):
                    gates_exp(scale)
                    for i in range(18):
                        act.wait_ge(*ring.full((st, "up", i)))
                        if i >= NHB:
                            act.wait_ge(*ring.freed((st, "up", i - NHB)))
                        o.count(act.activation(gact[:, i % NHB, 0:NT], ring.bank((st, "up", i))[:, 0:NT], ACT.Silu),
                             S("gact_ready"))
                    act.preload_act_table_set(EXP_LN)
                    norm_rstd()

                swiglu("L0f", 1.0)
                keep_xT(2)

                act.wait_ge(*nth("act", "L1a_negbb"))
                act.wait_ge(*ring.full(("L1a", "beta")))
                link(act.activation(gateT[0:H, 0, :], ring.bank(("L1a", "beta"))[0:H, 0:NT], ACT.Exp,
                                    bias=neg_bb[:], scale=-1.0), ring.free(("L1a", "beta")))
                for c in range(0, 8, 2):
                    to_sbuf(("L1x", f"k{c}"), k64[:, c:c + 2, :], shape=lambda s: heads(s, 2))
                for u in range(NS):
                    act.wait_ge(*nth("act", "L1a_min"))
                    o.count(act.activation(qk3[:, u], qk3[:, u], ACT.Exp), S("L1a_exp"))
                for u in range(NS):
                    to_pad4(("L1a", "kT", u), tk(u), T)
                attnT_copy("L1a")
                for u in range(NS):
                    act.wait_ge(*nth("act", "ms_ready"))
                    o.count(act.activation(lnv[:, u, :], mv[:, u, 1:2], ACT.Ln, bias=eps6, scale=1.0 / D))
                o.settle()
                each(lambda u: act.activation(rstd[:, u, :], lnv[:, u, :], ACT.Exp, scale=-0.5), S("rstd_ready"))
                norm_rstd()
                keep_xT(3)

                for c in range(0, 8, 2):
                    to_sbuf(("L1x", f"q{c}"), q64[:, c:c + 2, :], shape=lambda s: heads(s, 2))
                softmax_units("L1x", 4, R ** -0.5)
                for u in range(NS):
                    for c in range(0, 8, 4):
                        to_sbuf(("L1x", "aT", u, c), attn64T[:, u, c:c + 4, :], shape=lambda s: heads(s, 4))
                norm_rstd()
                keep_xT(4)

                gates_exp(1.0)
                for i in range(16):
                    act.wait_ge(*ring.full(("L1f", "up", i)))
                    if i >= NHB:
                        act.wait_ge(*ring.full(("L1f", "y", (i - NHB) // 2)))
                    o.count(act.activation(hT[:, i % NHB, :], ring.bank(("L1f", "up", i))[:], ACT.Gelu_apprx_tanh),
                         ring.free(("L1f", "up", i)))
                act.preload_act_table_set(EXP_LN)
                norm_rstd()
                keep_xT(5)

                to_sbuf(("L2a", "qk"), qT[:], shape=lambda s: heads(s, 2))
                for i in range(4):
                    act.wait_ge(*nth("act", "L2a_min"))
                    o.count(act.activation(gact[:, i, :], gact[:, i, :], ACT.Exp), S("L2a_exp"))
                attnT_copy("L2a")
                norm_rstd()
                for u in range(NS):
                    to_sbuf(("L2a", "x1T", u), kT[:, tk(u)], shape=lambda s: s[:, 0:T])
                act.preload_act_table_set("gelu_and_others")
                for c in range(4):
                    key = ("L2a", f"h{c // 2 * 2}")
                    act.wait_ge(*ring.full(key))
                    half = slice((c % 2) * NT, (c % 2 + 1) * NT)
                    ins = act.activation(gact[:, c // 2, half], ring.bank(key)[:, half], ACT.Gelu,
                                         bias=W["L2a_b1"][:, c:c + 1])
                    o.count(ins, ring.free(key) if c % 2 else None)
                act.preload_act_table_set(EXP_LN)
                norm_rstd()
                norm_rstd()
                keep_xT(6)

                act.wait_ge(*nth("act", "L2x_bias"))
                to_pad4(("L2x", "q"), slice(0, NT), NT, bias=bq4)
                softmax_units("L2x", 4, DH ** -0.5)
                attnT_copy("L2x", [1])
                norm_rstd()
                keep_xT(7)

                swiglu("L2f", -1.0)
                keep_xT(8)

                act.wait_ge(*nth("act", "L3a_zeros"))
                act.wait_ge(*ring.full(("L3a", "lat")))
                for r in range(2):
                    rows = slice(64 * r, 64 * r + 64)
                    o.count(act.copy(lat_pad[rows, r, :], ring.bank(("L3a", "lat"))[rows, 0:NT]),
                         ring.free(("L3a", "lat")) if r else None)
                for c in range(0, 8, 2):
                    to_sbuf(("L3a", f"q{c}"), q64[:, c:c + 2, :], shape=lambda s: heads(s, 2))
                softmax_units("L3a", 4, R ** -0.5)
                attnT_copy("L3a", [1])
                norm_rstd()
                keep_xT(9)

                act.wait_ge(*nth("act", "L3x_absf"))
                link(act.activation(gateT[0:8, 5, :], gateT[0:8, 5, :], ACT.Exp))
                link(act.activation(gateT[0:8, 5, :], gateT[0:8, 5, :], ACT.Ln, bias=one[0:8]), S("L3x_softplus"))
                act.wait_ge(*ring.full(("L3x", "mx")))
                link(act.activation(small2[:, :, 32:40], ring.bank(("L3x", "mx"))[:, 0:16].rearrange("p (u h) -> p u h", u=2),
                                    ACT.Exp, scale=-1.0))
                link(act.copy(a_tok[:], ring.bank(("L3x", "mx"))[:, 16:32].rearrange("p (u h) -> p u h", u=2)),
                     ring.free(("L3x", "mx")))
                for i in range(4):
                    act.wait_ge(*ring.full(("L3x", "D", i)))
                    if i >= NPB:
                        act.wait_ge(*ring.freed(("L3x", "s", i - NPB)))
                    for j in range(4):
                        cols = slice(j * T, j * T + T)
                        ins = act.activation(probs[:, i % NPB, cols], ring.bank(("L3x", "D", i))[:, cols], ACT.Exp,
                                             bias=a_tok[:, i // 2, 4 * (i % 2) + j:4 * (i % 2) + j + 1])
                        o.count(ins, ring.free(("L3x", "D", i)) if j == 3 else None)
                for u in range(NS):
                    act.wait_ge(*nth("act", "L3x_var"))
                    o.count(act.activation(small[:, u, 32:40], small[:, u, 16:24], ACT.Ln, bias=eps6, scale=1.0 / DC))
                o.settle()
                each(lambda u: act.activation(small[:, u, 24:32], small[:, u, 32:40], ACT.Exp, scale=-0.5),
                     S("L3x_rstd"))
                norm_rstd()
                for u in range(NS):
                    act.wait_ge(*ring.full(("xT", 10, u)))
                    o.count(act.copy(xT_all[:, bass.ds(pair * NT + u * T, T)], ring.bank(("xT", 10, u))[:, 0:T]),
                         ring.free(("xT", 10, u)))

            @block.sync
            def _(eng):
                def load_next(name):
                    sp.dma_start(inputs[name][:], dram[name][pair + 1]).then_inc(S("next_in"), 16)

                sp.wait_ge(*ring.freed(("L0a", "y", 0)))
                sp.wait_ge(*ring.freed(("L0a", "y", 1)))
                load_next("x_tok")
                for done, st in (("L0f", "L2f"), ("L2f", "L0f")):
                    sp.wait_ge(*ring.full((done, "y", 8)))
                    sp.dma_start(group_tile[st + "_experts"][:], dram[st + "_experts"]).then_inc(S(st + "_in"), 16)
                sp.wait_ge(*ring.full(("L3x", "gates", 1)))
                sp.wait_ge(S("L3x_bd"), NS)
                load_next("xT")
                sp.wait_ge(*ring.freed(("L3x", "s", 0)))
                load_next("ctx_tok")
                sp.wait_ge(*ring.full(("L3x", "s", 3)))
                load_next("ctxT")
                sp.wait_ge(S("next_in"), len(inputs) * 16)
                sp.wait_ge(S("L0f_in"), 16)

        with nc.Block(name="reset") as block:
            @block.sync
            def _(eng):
                nums = sorted(s.num for s in sems.values())
                assert nums == list(range(nums[0], nums[-1] + 1))
                sp.sem_clear(range(nums[0], nums[-1] + 1))

    amax = sb("amax", [P, 4])
    q_in = k64[:, 0:4, :].rearrange("p c t -> p (c t)")
    q_bf = sb("q_bf", [P, B * T], BF16)
    w_bf = sb("w_bf", [P, D], BF16)
    y_all = q64[:, 0:4, :].rearrange("p c t -> p (c t)").rearrange("p (b d) -> p b d", b=B)
    stats8 = sb("stats8", [P, B, 6])
    mv8 = sb("mv8", [P, B, 2])
    rstd8 = sb("rstd8", [P, B])
    fin = {n: ctx.enter_context(nc.semaphore(f"ffn_{n}")) for n in
           ("partial", "turned", "whole", "spread", "operands", "products", "var", "rstd", "normed")}
    fin_step = ctx.enter_context(nc.semaphore("ffn_dve_step"))
    fin_act = ctx.enter_context(nc.semaphore("ffn_act_step"))
    ROUND = float(1.5 * 2 ** 23)

    with nc.Block(name="last_ffn") as block:
        @block.tensor
        def _(eng):
            pe.wait_ge(fin["partial"], 2)
            pe.matmul(psum[1][:, 0:1], const("ones")[:, 0:P], amax[:, 1:2], start=True, stop=True)
            pe.transpose(psum[0][0:1, 0:P], amax[:, 0:1], IDENT).then_inc(fin["turned"], 1)
            pe.wait_ge(fin["whole"], 1)
            pe.matmul(psum[2][:, 0:1], ones_row, amax[0:1, 2:3], start=True, stop=True).then_inc(fin["spread"], 1)
            pe.wait_ge(fin["operands"], 1)
            for b in range(B):
                m = pe.matmul(psum[3 + b // 4][:, b % 4 * D:b % 4 * D + D], q_bf[:, b * T:(b + 1) * T], w_bf[:],
                              start=True, stop=True)
                if b % 4 == 3:
                    m.then_inc(fin["products"], 1)

        @block.vector
        def _(eng):
            o = Order(dve, "ffn")
            link = o.link
            st = fin_step
            dve.wait_ge(*weights("L3f"))
            link(dve.tensor_reduce(amax[:, 0:1], xT_all[:], X, ALU.max, apply_absolute_value=True), fin["partial"])
            link(dve.tensor_reduce(amax[:, 1:2], W["L3f_w"][:], X, ALU.add, apply_absolute_value=True), fin["partial"])
            link(dve.tensor_tensor(x_all[:], x_all[:], among(W["L3f_b"][:], B), ALU.add), st)
            dve.wait_ge(fin["turned"], 1)
            link(dve.tensor_reduce(amax[0:1, 2:3], psum[0][0:1, 0:P], X, ALU.max), fin["whole"])
            s = small[:, 0, :]
            link(dve.tensor_scalar(s[:, 2:3], psum[1][:, 0:1], 1.0 / (D * D), None, ALU.mult), st)
            link(dve.tensor_scalar(s[:, 3:4], s[:, 2:3], 0.5, None, ALU.mult), st)
            link(dve.tensor_scalar(s[:, 4:5], s[:, 2:3], -0.5, None, ALU.mult), st)
            link(dve.tensor_scalar(qs[:, 0, :], W["L3f_w"][:], s[:, 3:4], None, ALU.is_gt), st)
            link(dve.tensor_scalar(qs[:, 1, :], W["L3f_w"][:], s[:, 4:5], None, ALU.is_lt), st)
            link(dve.tensor_tensor(w_bf[:], qs[:, 0, :], qs[:, 1, :], ALU.subtract), st)
            dve.wait_ge(fin["spread"], 1)
            link(dve.tensor_scalar(s[:, 0:1], psum[2][:, 0:1], 1.0 / 127.0, None, ALU.mult), st)
            link(dve.reciprocal(s[:, 1:2], s[:, 0:1]), st)
            link(dve.tensor_tensor(s[:, 5:6], s[:, 2:3], s[:, 0:1], ALU.mult), st)
            link(dve.tensor_scalar(q_in, xT_all[:], s[:, 1:2], ROUND, ALU.mult, ALU.add), st)
            link(dve.tensor_scalar(q_in, q_in, ROUND, 127.0, ALU.subtract, ALU.min), st)
            link(dve.tensor_scalar(q_bf[:], q_in, -128.0, None, ALU.max), fin["operands"])
            half = B // 2
            for g in range(2):
                own = range(g * half, (g + 1) * half)
                dve.wait_ge(fin["products"], g + 1)
                xs = x_all[:, own[0]:own[-1] + 1, :].rearrange("p b d -> p (b d)")
                link(dve.scalar_tensor_tensor(xs, psum[3 + g][:], s[:, 5:6], xs, ALU.mult, ALU.add), st)
                for b in own:
                    o.count(dve.bn_stats(stats8[:, b, :], x_all[:, b, :]), st)
                o.settle(st)
                for b in own:
                    o.count(dve.bn_aggr(mv8[:, b, :], stats8[:, b, :]), fin["var"])
            o.settle(fin["var"])
            for b in range(B):
                if b % half == 0:
                    dve.wait_ge(fin["rstd"], b // half + 1)
                o.count(dve.tensor_scalar(y_all[:, b, :], x_all[:, b, :], mv8[:, b, 0:1], rstd8[:, b:b + 1],
                                          ALU.subtract, ALU.mult), fin["normed"])

        @block.scalar
        def _(eng):
            act.preload_act_table_set(EXP_LN)
            for g in range(2):
                own = slice(g * B // 2, (g + 1) * B // 2)
                act.wait_ge(fin["var"], (g + 1) * B // 2)
                act.activation(rstd8[:, own], mv8[:, own, 1], ACT.Ln, bias=const("eps")[:, 0:1]).then_inc(fin_act, 1)
                act.wait_ge(fin_act, g + 1)
                act.activation(rstd8[:, own], rstd8[:, own], ACT.Exp, scale=-0.5).then_inc(fin["rstd"], 1)

        @block.sync
        def _(eng):
            for g in w_in:
                sp.wait_ge(*weights(g))
            by_token = out.rearrange("b t d -> t b d")
            for g in range(2):
                own = slice(g * B // 2, (g + 1) * B // 2)
                sp.wait_ge(fin["normed"], (g + 1) * B // 2)
                sp.dma_start(by_token[:, own, :], y_all[:, own, :]).then_inc(stored, 16)
            sp.wait_ge(stored, 2 * 16)


def layouts(i):
    def rows(v):
        return np.broadcast_to(v.reshape(1, -1), (P, v.size))

    def chunks(w):
        return w.reshape(-1, P, w.shape[-1]).transpose(1, 0, 2).reshape(P, -1)

    def experts_in(*w):
        return np.concatenate(w, axis=0).transpose(1, 0, 2).reshape(P, -1)

    def experts_out(*w):
        w = np.concatenate(w, axis=0)
        return chunks(w.reshape(-1, D))

    proj = np.zeros((H, DH, H, 32), np.float32)
    proj[np.arange(H), :, np.arange(H), :] = i["L2_attn_proj"]
    g = np.stack([i["L3_xattn_igate_kernel"], i["L3_xattn_fgate_kernel"]], axis=1)
    t = np.swapaxes
    return {
        "con_sts": shape_constants(),
        "L0a_qkv": i["L0_attn_W_qkv"].T, "L0a_o": i["L0_attn_W_out"].T,
        "L0x_q": i["L0_xattn_Wq"], "L0x_kv": i["L0_xattn_Wkv"], "L0x_o": i["L0_xattn_Wout"],
        "L0x_bo": i["L0_xattn_bout"][None],
        "L0f_gate": i["L0_ffn_gate_w"].T, "L0f_gb": rows(i["L0_ffn_gate_bias"]),
        "L0f_w1": experts_in(i["L0_ffn_sw1"].T[None], t(i["L0_ffn_w1"], 1, 2)),
        "L0f_w3": experts_in(i["L0_ffn_sw3"].T[None], t(i["L0_ffn_w3"], 1, 2)),
        "L0f_w2": experts_out(i["L0_ffn_sw2"].T[None], t(i["L0_ffn_w2"], 1, 2)),
        "L1a_qkv": np.concatenate([i["L1_attn_Wq"].T, i["L1_attn_Wk"].T, i["L1_attn_Wv"].T], axis=1),
        "L1a_b": i["L1_attn_Wb"].T, "L1a_bb": i["L1_attn_bb"][:, None], "L1a_o": i["L1_attn_Wo"].T,
        "L1a_bo": i["L1_attn_bo"][None], "L1a_scale": rows(i["L1_attn_scale"]),
        "L1x_q": i["L1_xattn_w_q"], "L1x_kv": i["L1_xattn_w_kv"], "L1x_o": chunks(i["L1_xattn_w_out"]),
        "L1x_bo": i["L1_xattn_b_out"][None],
        "L1f_gate": i["L1_ffn_gate_w"], "L1f_w1": experts_in(i["L1_ffn_w1"]), "L1f_w2": experts_out(i["L1_ffn_w2"]),
        "L2a_qkv": i["L2_attn_w_qkv"].T, "L2a_proj": proj.reshape(P, H * 32), "L2a_o": i["L2_attn_w_out"].T,
        "L2a_bo": i["L2_attn_b_out"][None], "L2a_gamma": rows(i["L2_attn_gamma"]), "L2a_beta": rows(i["L2_attn_beta"]),
        "L2a_w1": i["L2_attn_w1"].T, "L2a_b1": i["L2_attn_b1"].reshape(4, P).T, "L2a_w2": chunks(i["L2_attn_w2"].T),
        "L2a_b2": i["L2_attn_b2"][None],
        "L2x_q": i["L2_xattn_Wq"], "L2x_k": i["L2_xattn_Wk"], "L2x_v": i["L2_xattn_Wv"], "L2x_o": i["L2_xattn_Wo"],
        "L2x_bq": i["L2_xattn_bq"][:, None], "L2x_bk": i["L2_xattn_bk"][:, None], "L2x_bv": i["L2_xattn_bv"][None],
        "L2x_bo": i["L2_xattn_bo"][None],
        "L2f_gate": i["L2_ffn_gate_w"].T, "L2f_gb": rows(i["L2_ffn_beta"]),
        "L2f_w1": experts_in(i["L2_ffn_shared_gate_w"], i["L2_ffn_gate_proj_w"]),
        "L2f_w3": experts_in(i["L2_ffn_shared_up_w"], i["L2_ffn_up_proj_w"]),
        "L2f_w2": experts_out(i["L2_ffn_shared_down_w"], i["L2_ffn_down_proj_w"]),
        "L3a_basis": np.concatenate([i["L3_attn_basis_w"].T] * 2, axis=1), "L3m_core": i["L3_attn_core"],
        "L3m_coreT": i["L3_attn_core"].T, "L3m_mats": i["L3_attn_head_residual"].transpose(1, 0, 2).reshape(R, H * R),
        "L3a_v": i["L3_attn_v_w"].T, "L3a_vb": i["L3_attn_v_b"][None], "L3a_o": i["L3_attn_o_w"].T,
        "L3a_bo": i["L3_attn_o_b"][None],
        "L3x_gates": chunks(g.reshape(3 * P, 16)), "L3x_ib": i["L3_xattn_igate_bias"][:, None],
        "L3x_fb": i["L3_xattn_fgate_bias"][:, None], "L3x_w": rows(i["L3_xattn_outnorm_weight"]),
        "L3f_w": i["L3_ffn_weight"].T, "L3f_b": rows(i["L3_ffn_bias"]),
    }


def kernel(**inputs):
    import concourse.bacc as bacc
    from concourse.bass_utils import run_bass_kernel_spmd

    i = {n: np.asarray(v) for n, v in inputs.items()}
    laid = layouts(i)
    arrays = {g: np.zeros((P, group_words(g)), np.float32) for g in GROUPS}
    for g, members in GROUPS.items():
        for n, (p, a, e) in members.items():
            assert laid[n].shape == (p, e - a) and laid[n].dtype == np.float32, (n, laid[n].shape)
            arrays[g][0:p, a:e] = laid[n]
    for n, v in (("x", i["x"]), ("ctx", i["ctx_1024"])):
        pairs = v.reshape(B // NS, NS, T, D)
        arrays[f"{n}_tok"] = np.ascontiguousarray(pairs.transpose(0, 2, 1, 3))
        arrays[f"{n}T"] = np.ascontiguousarray(pairs.transpose(0, 3, 1, 2).reshape(B // NS, D, NT))
    for n in ("x_tok", "xT", "ctx_tok", "ctxT"):
        arrays[n] = np.concatenate([arrays[n], arrays[n][:1]])

    nc = bacc.Bacc("TRN2", target_bir_lowering=False, num_devices=1)
    arrays = {f"in_{n}": a for n, a in arrays.items()}
    dram = {n[3:]: nc.dram_tensor(n, a.shape, F32, kind="ExternalInput").ap() for n, a in arrays.items()}
    out = nc.dram_tensor("y", (B, T, D), F32, kind="ExternalOutput").ap()
    build(nc, dram, out)
    r = run_bass_kernel_spmd(nc, [arrays], core_ids=[0])
    return r.results[0]["y"]
```
